# Optimizing a Trainium2 kernel written in Bass

```python
import numpy as np
import jax
import jax.numpy as jnp

def _softmax(x, axis=-1):
    return jax.nn.softmax(x, axis=axis)

def _gelu(x):
    return jax.nn.gelu(x, approximate=True)

def _silu(x):
    return jax.nn.silu(x)

def _sigmoid(x):
    return jax.nn.sigmoid(x)

def _layernorm(x, axis=-1, eps=1e-05):
    m = jnp.mean(x, axis=axis, keepdims=True)
    v = jnp.var(x, axis=axis, keepdims=True)
    return (x - m) / jnp.sqrt(v + eps)

def _scatter_add(tgt, idx, src, axis=0):
    return tgt.at[idx].add(src)

def _segment_sum(src, seg, n):
    return jax.ops.segment_sum(src, seg, n)
kernel_name = 'mk_sandwich_d2_jaxref_r4_273b7a'

def setup_inputs(seed: int=0):
    np.random.seed(seed)
    _w = jnp.asarray

    def _L0_attn_setup():
        import jax, jax.numpy as jnp
        import numpy as np
        D_MODEL = 256
        N_HEADS = 16
        HEAD_DIM = D_MODEL // N_HEADS
        WINDOW = 128
        LOCAL_BLOCK = 64
        LATENT_TOKENS = 64
        LATENT_D = 64
        LATENT_HEADS = 4
        LATENT_HD = LATENT_D // LATENT_HEADS
        NEG = -1000000000.0

        def _local_attention(q, k, v):
            B, H, S, hd = q.shape
            bs = min(S, max(WINDOW, LOCAL_BLOCK))
            nb = S // bs
            w = WINDOW
            L = bs + w - 1
            k_pad = jnp.pad(k, ((0, 0), (0, 0), (w - 1, 0), (0, 0)))
            v_pad = jnp.pad(v, ((0, 0), (0, 0), (w - 1, 0), (0, 0)))
            starts = jnp.arange(nb) * bs
            idx = starts[:, None] + jnp.arange(L)[None, :]
            kb = k_pad[:, :, idx]
            vb = v_pad[:, :, idx]
            qb = q.reshape(B, H, nb, bs, hd)
            q_pos = starts[:, None] + jnp.arange(bs)[None, :]
            k_gpos = starts[:, None] + jnp.arange(L)[None, :] - (w - 1)
            dist = q_pos[:, :, None] - k_gpos[:, None, :]
            allowed = (dist > 0) & (dist <= w) & (k_gpos[:, None, :] >= 0)
            scale = 1.0 / np.sqrt(hd)
            scores = jnp.einsum('bhnqd,bhnkd->bhnqk', qb, kb) * scale
            scores = jnp.where(allowed, scores, NEG)
            attn = jax.nn.softmax(scores, axis=-1)
            attn = jnp.where(allowed.any(-1)[None, None, :, :, None], attn, 0.0)
            out = jnp.einsum('bhnqk,bhnkd->bhnqd', attn, vb)
            return out.reshape(B, H, S, hd)
        key = jax.random.key(seed)
        ks = jax.random.split(key, 14)
        B, S = (2, 1024)
        s = 0.02
        f32 = jnp.float32
        return {'x': jax.random.normal(ks[0], (B, S, D_MODEL), f32), 'qkv_w': jax.random.normal(ks[1], (D_MODEL, 3 * D_MODEL), f32) * s, 'qkv_b': jnp.zeros((3 * D_MODEL,), f32), 'rq_w': jax.random.normal(ks[2], (D_MODEL, LATENT_D), f32) * s, 'rq_b': jnp.zeros((LATENT_D,), f32), 'rkv_w': jax.random.normal(ks[3], (D_MODEL, 2 * LATENT_D), f32) * s, 'rkv_b': jnp.zeros((2 * LATENT_D,), f32), 'rout_w': jax.random.normal(ks[4], (LATENT_D, D_MODEL), f32) * s, 'rout_b': jnp.zeros((D_MODEL,), f32), 'out_w': jax.random.normal(ks[5], (D_MODEL, D_MODEL), f32) * s, 'out_b': jnp.zeros((D_MODEL,), f32), 'gl_w': jax.random.normal(ks[6], (HEAD_DIM, 1), f32) * s, 'gr_w': jax.random.normal(ks[7], (HEAD_DIM, 1), f32) * s}
    _L0_attn_in = _L0_attn_setup()

    def _L0_ffn_setup():
        import jax, jax.numpy as jnp
        import numpy as np
        EMB = 256
        FF = 4 * EMB

        def _ternary(w):
            scale = jnp.maximum(jnp.mean(jnp.abs(w)), 1e-08)
            w_t = jnp.clip(jnp.round(w / scale), -1.0, 1.0)
            return w + jax.lax.stop_gradient(w_t - w)
        key = jax.random.key(seed)
        kx, k1, k2, kb1, kb2 = jax.random.split(key, 5)
        x = jax.random.normal(kx, (4, 512, EMB), dtype=jnp.float32)
        lim1 = 1.0 / np.sqrt(EMB)
        lim2 = 1.0 / np.sqrt(FF)
        W1 = jax.random.uniform(k1, (FF, EMB), jnp.float32, -lim1, lim1)
        b1 = jax.random.uniform(kb1, (FF,), jnp.float32, -lim1, lim1)
        W2 = jax.random.uniform(k2, (EMB, FF), jnp.float32, -lim2, lim2)
        b2 = jax.random.uniform(kb2, (EMB,), jnp.float32, -lim2, lim2)
        return {'x': x, 'W1': W1, 'b1': b1, 'W2': W2, 'b2': b2}
    _L0_ffn_in = _L0_ffn_setup()

    def _L1_attn_setup():
        import jax, jax.numpy as jnp
        import numpy as np
        B, T, D, H = (4, 256, 256, 16)
        DH = D // H
        EPS = 1e-05

        def _rwkv6(x, W_r, W_k, W_v, W_w, W_o, u, tm_r, tm_k, tm_v, tm_w, ln_w, ln_b):
            b, t, d = x.shape
            x_prev = jnp.concatenate([jnp.zeros_like(x[:, :1]), x[:, :-1]], axis=1)
            xr = tm_r * x + (1.0 - tm_r) * x_prev
            xk = tm_k * x + (1.0 - tm_k) * x_prev
            xv = tm_v * x + (1.0 - tm_v) * x_prev
            xw = tm_w * x + (1.0 - tm_w) * x_prev
            r = jax.nn.sigmoid(xr @ W_r.T)
            k = xk @ W_k.T
            v = xv @ W_v.T
            w = -jax.nn.softplus(-(xw @ W_w.T)) - 0.0001
            r = r.reshape(b, t, H, DH)
            k = k.reshape(b, t, H, DH)
            v = v.reshape(b, t, H, DH)
            w = w.reshape(b, t, H, DH)

            def step(s, rkvw):
                r_t, k_t, v_t, w_t = rkvw
                bonus = jnp.exp(u + k_t)[..., :, None] * v_t[..., None, :]
                o_t = jnp.einsum('bhi,bhij->bhj', r_t, s + bonus)
                s = jnp.exp(w_t)[..., None] * s + k_t[..., :, None] * v_t[..., None, :]
                return (s, o_t)
            s0 = jnp.zeros((b, H, DH, DH), x.dtype)
            rkvw = tuple((a.transpose(1, 0, 2, 3) for a in (r, k, v, w)))
            _, o = jax.lax.scan(step, s0, rkvw)
            o = o.transpose(1, 0, 2, 3)
            mu = jnp.mean(o, axis=-1, keepdims=True)
            var = jnp.var(o, axis=-1, keepdims=True)
            o = (o - mu) * jax.lax.rsqrt(var + EPS) * ln_w + ln_b
            o = o * r
            return o.reshape(b, t, d) @ W_o.T
        key = jax.random.key(seed)
        ks = jax.random.split(key, 14)
        sc = 1.0 / np.sqrt(D)
        x = jax.random.normal(ks[0], (B, T, D), jnp.float32)
        W_r = jax.random.normal(ks[1], (D, D), jnp.float32) * sc
        W_k = jax.random.normal(ks[2], (D, D), jnp.float32) * sc
        W_v = jax.random.normal(ks[3], (D, D), jnp.float32) * sc
        W_w = jax.random.normal(ks[4], (D, D), jnp.float32) * sc
        W_o = jax.random.normal(ks[5], (D, D), jnp.float32) * sc
        u = jax.random.normal(ks[6], (H, DH), jnp.float32) * 0.1
        tm_r = jax.random.uniform(ks[7], (D,), jnp.float32)
        tm_k = jax.random.uniform(ks[8], (D,), jnp.float32)
        tm_v = jax.random.uniform(ks[9], (D,), jnp.float32)
        tm_w = jax.random.uniform(ks[10], (D,), jnp.float32)
        ln_w = jnp.ones((DH,), jnp.float32) + 0.1 * jax.random.normal(ks[11], (DH,), jnp.float32)
        ln_b = 0.1 * jax.random.normal(ks[12], (DH,), jnp.float32)
        return {'x': x, 'W_r': W_r, 'W_k': W_k, 'W_v': W_v, 'W_w': W_w, 'W_o': W_o, 'u': u, 'tm_r': tm_r, 'tm_k': tm_k, 'tm_v': tm_v, 'tm_w': tm_w, 'ln_w': ln_w, 'ln_b': ln_b}
    _L1_attn_in = _L1_attn_setup()

    def _L1_ffn_setup():
        import jax, jax.numpy as jnp
        import numpy as np
        from jax import lax
        DIM = 256
        INTER = 128
        N_EXPERTS = 16
        TOPK = 4
        ROUTE_SCALE = 2.5
        VOCAB = 8000

        def _silu_and_mul(gu):
            gate, up = jnp.split(gu, 2, axis=-1)
            return jax.nn.silu(gate) * up
        key = jax.random.key(seed)
        ks = jax.random.split(key, 8)
        x = jax.random.normal(ks[0], (2, 128, DIM), dtype=jnp.float32)
        input_ids = jax.random.randint(ks[1], (2, 128), 0, VOCAB)
        s = 0.02
        gate_w = jax.random.normal(ks[2], (N_EXPERTS, DIM), dtype=jnp.float32) * s
        gate_b = jax.random.normal(ks[3], (N_EXPERTS,), dtype=jnp.float32) * s
        w13 = jax.random.normal(ks[4], (N_EXPERTS, 2 * INTER, DIM), dtype=jnp.float32) * s
        w2 = jax.random.normal(ks[5], (N_EXPERTS, DIM, INTER), dtype=jnp.float32) * s
        w13_s = jax.random.normal(ks[6], (2 * INTER, DIM), dtype=jnp.float32) * s
        w2_s = jax.random.normal(ks[7], (DIM, INTER), dtype=jnp.float32) * s
        return {'x': x, 'input_ids': input_ids, 'gate_w': gate_w, 'gate_b': gate_b, 'w13': w13, 'w2': w2, 'w13_s': w13_s, 'w2_s': w2_s}
    _L1_ffn_in = _L1_ffn_setup()
    _d = {'L0_attn_x': _L0_attn_in['x'], 'L0_attn_qkv_w': _L0_attn_in['qkv_w'], 'L0_attn_qkv_b': _L0_attn_in['qkv_b'], 'L0_attn_rq_w': _L0_attn_in['rq_w'], 'L0_attn_rq_b': _L0_attn_in['rq_b'], 'L0_attn_rkv_w': _L0_attn_in['rkv_w'], 'L0_attn_rkv_b': _L0_attn_in['rkv_b'], 'L0_attn_rout_w': _L0_attn_in['rout_w'], 'L0_attn_rout_b': _L0_attn_in['rout_b'], 'L0_attn_out_w': _L0_attn_in['out_w'], 'L0_attn_out_b': _L0_attn_in['out_b'], 'L0_attn_gl_w': _L0_attn_in['gl_w'], 'L0_attn_gr_w': _L0_attn_in['gr_w'], 'L0_ffn_W1': _L0_ffn_in['W1'], 'L0_ffn_b1': _L0_ffn_in['b1'], 'L0_ffn_W2': _L0_ffn_in['W2'], 'L0_ffn_b2': _L0_ffn_in['b2'], 'L1_attn_W_r': _L1_attn_in['W_r'], 'L1_attn_W_k': _L1_attn_in['W_k'], 'L1_attn_W_v': _L1_attn_in['W_v'], 'L1_attn_W_w': _L1_attn_in['W_w'], 'L1_attn_W_o': _L1_attn_in['W_o'], 'L1_attn_u': _L1_attn_in['u'], 'L1_attn_tm_r': _L1_attn_in['tm_r'], 'L1_attn_tm_k': _L1_attn_in['tm_k'], 'L1_attn_tm_v': _L1_attn_in['tm_v'], 'L1_attn_tm_w': _L1_attn_in['tm_w'], 'L1_attn_ln_w': _L1_attn_in['ln_w'], 'L1_attn_ln_b': _L1_attn_in['ln_b'], 'L1_ffn_input_ids': _L1_ffn_in['input_ids'], 'L1_ffn_gate_w': _L1_ffn_in['gate_w'], 'L1_ffn_gate_b': _L1_ffn_in['gate_b'], 'L1_ffn_w13': _L1_ffn_in['w13'], 'L1_ffn_w2': _L1_ffn_in['w2'], 'L1_ffn_w13_s': _L1_ffn_in['w13_s'], 'L1_ffn_w2_s': _L1_ffn_in['w2_s']}
    _x0 = _d['L0_attn_x']
    _d['L0_attn_x'] = jax.random.normal(jax.random.fold_in(jax.random.key(seed), 1), (8, 512, 256), dtype=_x0.dtype)
    del _x0
    return _d

def reference(L0_attn_x, L0_attn_qkv_w, L0_attn_qkv_b, L0_attn_rq_w, L0_attn_rq_b, L0_attn_rkv_w, L0_attn_rkv_b, L0_attn_rout_w, L0_attn_rout_b, L0_attn_out_w, L0_attn_out_b, L0_attn_gl_w, L0_attn_gr_w, L0_ffn_W1, L0_ffn_b1, L0_ffn_W2, L0_ffn_b2, L1_attn_W_r, L1_attn_W_k, L1_attn_W_v, L1_attn_W_w, L1_attn_W_o, L1_attn_u, L1_attn_tm_r, L1_attn_tm_k, L1_attn_tm_v, L1_attn_tm_w, L1_attn_ln_w, L1_attn_ln_b, L1_ffn_input_ids, L1_ffn_gate_w, L1_ffn_gate_b, L1_ffn_w13, L1_ffn_w2, L1_ffn_w13_s, L1_ffn_w2_s):

    def _L0_attn_ref(x, qkv_w, qkv_b, rq_w, rq_b, rkv_w, rkv_b, rout_w, rout_b, out_w, out_b, gl_w, gr_w):
        import jax, jax.numpy as jnp
        import numpy as np
        D_MODEL = 256
        N_HEADS = 16
        HEAD_DIM = D_MODEL // N_HEADS
        WINDOW = 128
        LOCAL_BLOCK = 64
        LATENT_TOKENS = 64
        LATENT_D = 64
        LATENT_HEADS = 4
        LATENT_HD = LATENT_D // LATENT_HEADS
        NEG = -1000000000.0

        def _local_attention(q, k, v):
            B, H, S, hd = q.shape
            bs = min(S, max(WINDOW, LOCAL_BLOCK))
            nb = S // bs
            w = WINDOW
            L = bs + w - 1
            k_pad = jnp.pad(k, ((0, 0), (0, 0), (w - 1, 0), (0, 0)))
            v_pad = jnp.pad(v, ((0, 0), (0, 0), (w - 1, 0), (0, 0)))
            starts = jnp.arange(nb) * bs
            idx = starts[:, None] + jnp.arange(L)[None, :]
            kb = k_pad[:, :, idx]
            vb = v_pad[:, :, idx]
            qb = q.reshape(B, H, nb, bs, hd)
            q_pos = starts[:, None] + jnp.arange(bs)[None, :]
            k_gpos = starts[:, None] + jnp.arange(L)[None, :] - (w - 1)
            dist = q_pos[:, :, None] - k_gpos[:, None, :]
            allowed = (dist > 0) & (dist <= w) & (k_gpos[:, None, :] >= 0)
            scale = 1.0 / np.sqrt(hd)
            scores = jnp.einsum('bhnqd,bhnkd->bhnqk', qb, kb) * scale
            scores = jnp.where(allowed, scores, NEG)
            attn = jax.nn.softmax(scores, axis=-1)
            attn = jnp.where(allowed.any(-1)[None, None, :, :, None], attn, 0.0)
            out = jnp.einsum('bhnqk,bhnkd->bhnqd', attn, vb)
            return out.reshape(B, H, S, hd)
        B, S, D = x.shape
        qkv = x @ qkv_w + qkv_b
        q, k, v = jnp.split(qkv, 3, axis=-1)

        def heads(t):
            return t.reshape(B, S, N_HEADS, HEAD_DIM).transpose(0, 2, 1, 3)
        local = _local_attention(heads(q), heads(k), heads(v))
        chunk = -(-S // min(LATENT_TOKENS, S))
        nlat = S // chunk
        pooled = x.reshape(B, nlat, chunk, D).mean(axis=2)
        chunk_ids = jnp.arange(S) // chunk
        rq = (x @ rq_w + rq_b).reshape(B, S, LATENT_HEADS, LATENT_HD).transpose(0, 2, 1, 3)
        rkv = pooled @ rkv_w + rkv_b
        rk, rv = jnp.split(rkv, 2, axis=-1)
        rk = rk.reshape(B, nlat, LATENT_HEADS, LATENT_HD).transpose(0, 2, 1, 3)
        rv = rv.reshape(B, nlat, LATENT_HEADS, LATENT_HD).transpose(0, 2, 1, 3)
        lscale = 1.0 / np.sqrt(LATENT_HD)
        lscores = jnp.einsum('bhsd,bhld->bhsl', rq, rk) * lscale
        lat_allowed = jnp.arange(nlat)[None, :] < chunk_ids[:, None]
        lscores = jnp.where(lat_allowed[None, None], lscores, NEG)
        lattn = jax.nn.softmax(lscores, axis=-1)
        lattn = jnp.where(lat_allowed.any(-1)[None, None, :, None], lattn, 0.0)
        lat_out = jnp.einsum('bhsl,bhld->bhsd', lattn, rv)
        lat_out = lat_out.transpose(0, 2, 1, 3).reshape(B, S, LATENT_D)
        remote = lat_out @ rout_w + rout_b
        remote_h = remote.reshape(B, S, N_HEADS, HEAD_DIM).transpose(0, 2, 1, 3)
        gate = jax.nn.sigmoid(local @ gl_w + remote_h @ gr_w)
        mixed = gate * local + (1.0 - gate) * remote_h
        mixed = mixed.transpose(0, 2, 1, 3).reshape(B, S, D)
        return mixed @ out_w + out_b

    def _L0_ffn_ref(x, W1, b1, W2, b2):
        import jax, jax.numpy as jnp
        import numpy as np
        EMB = 256
        FF = 4 * EMB

        def _ternary(w):
            scale = jnp.maximum(jnp.mean(jnp.abs(w)), 1e-08)
            w_t = jnp.clip(jnp.round(w / scale), -1.0, 1.0)
            return w + jax.lax.stop_gradient(w_t - w)
        h = jnp.einsum('bsd,fd->bsf', x, _ternary(W1)) + b1
        h = jax.nn.gelu(h, approximate=False)
        out = jnp.einsum('bsf,df->bsd', h, _ternary(W2)) + b2
        return out

    def _L1_attn_ref(x, W_r, W_k, W_v, W_w, W_o, u, tm_r, tm_k, tm_v, tm_w, ln_w, ln_b):
        import jax, jax.numpy as jnp
        import numpy as np
        B, T, D, H = (4, 256, 256, 16)
        DH = D // H
        EPS = 1e-05

        def _rwkv6(x, W_r, W_k, W_v, W_w, W_o, u, tm_r, tm_k, tm_v, tm_w, ln_w, ln_b):
            b, t, d = x.shape
            x_prev = jnp.concatenate([jnp.zeros_like(x[:, :1]), x[:, :-1]], axis=1)
            xr = tm_r * x + (1.0 - tm_r) * x_prev
            xk = tm_k * x + (1.0 - tm_k) * x_prev
            xv = tm_v * x + (1.0 - tm_v) * x_prev
            xw = tm_w * x + (1.0 - tm_w) * x_prev
            r = jax.nn.sigmoid(xr @ W_r.T)
            k = xk @ W_k.T
            v = xv @ W_v.T
            w = -jax.nn.softplus(-(xw @ W_w.T)) - 0.0001
            r = r.reshape(b, t, H, DH)
            k = k.reshape(b, t, H, DH)
            v = v.reshape(b, t, H, DH)
            w = w.reshape(b, t, H, DH)

            def step(s, rkvw):
                r_t, k_t, v_t, w_t = rkvw
                bonus = jnp.exp(u + k_t)[..., :, None] * v_t[..., None, :]
                o_t = jnp.einsum('bhi,bhij->bhj', r_t, s + bonus)
                s = jnp.exp(w_t)[..., None] * s + k_t[..., :, None] * v_t[..., None, :]
                return (s, o_t)
            s0 = jnp.zeros((b, H, DH, DH), x.dtype)
            rkvw = tuple((a.transpose(1, 0, 2, 3) for a in (r, k, v, w)))
            _, o = jax.lax.scan(step, s0, rkvw)
            o = o.transpose(1, 0, 2, 3)
            mu = jnp.mean(o, axis=-1, keepdims=True)
            var = jnp.var(o, axis=-1, keepdims=True)
            o = (o - mu) * jax.lax.rsqrt(var + EPS) * ln_w + ln_b
            o = o * r
            return o.reshape(b, t, d) @ W_o.T
        return _rwkv6(x, W_r, W_k, W_v, W_w, W_o, u, tm_r, tm_k, tm_v, tm_w, ln_w, ln_b)

    def _L1_ffn_ref(x, input_ids, gate_w, gate_b, w13, w2, w13_s, w2_s):
        import jax, jax.numpy as jnp
        import numpy as np
        from jax import lax
        DIM = 256
        INTER = 128
        N_EXPERTS = 16
        TOPK = 4
        ROUTE_SCALE = 2.5
        VOCAB = 8000

        def _silu_and_mul(gu):
            gate, up = jnp.split(gu, 2, axis=-1)
            return jax.nn.silu(gate) * up
        B, S, D = x.shape
        xt = x.reshape(-1, D)
        T = xt.shape[0]
        scores = jax.nn.sigmoid(xt.astype(jnp.float32) @ gate_w.T)
        biased = scores + gate_b
        _, idx = lax.top_k(biased, TOPK)
        w = jnp.take_along_axis(scores, idx, axis=-1)
        w = w / jnp.sum(w, axis=-1, keepdims=True)
        w = w * ROUTE_SCALE
        comb = jnp.zeros((T, N_EXPERTS), jnp.float32)
        comb = comb.at[jnp.arange(T)[:, None], idx].add(w)
        comb = comb.astype(x.dtype)

        def expert_body(y, args):
            w13_e, w2_e, c_e = args
            h = _silu_and_mul(xt @ w13_e.T)
            return (y + c_e[:, None] * (h @ w2_e.T), None)
        y, _ = lax.scan(expert_body, jnp.zeros_like(xt), (w13, w2, comb.T))
        y = y + _silu_and_mul(xt @ w13_s.T) @ w2_s.T
        return y.astype(x.dtype).reshape(B, S, D)
    x = L0_attn_x
    x = x + _layernorm(_L0_attn_ref(_layernorm(x, axis=-1), L0_attn_qkv_w, L0_attn_qkv_b, L0_attn_rq_w, L0_attn_rq_b, L0_attn_rkv_w, L0_attn_rkv_b, L0_attn_rout_w, L0_attn_rout_b, L0_attn_out_w, L0_attn_out_b, L0_attn_gl_w, L0_attn_gr_w), axis=-1)
    x = x + _layernorm(_L0_ffn_ref(_layernorm(x, axis=-1), L0_ffn_W1, L0_ffn_b1, L0_ffn_W2, L0_ffn_b2), axis=-1)
    x = x + _layernorm(_L1_attn_ref(_layernorm(x, axis=-1), L1_attn_W_r, L1_attn_W_k, L1_attn_W_v, L1_attn_W_w, L1_attn_W_o, L1_attn_u, L1_attn_tm_r, L1_attn_tm_k, L1_attn_tm_v, L1_attn_tm_w, L1_attn_ln_w, L1_attn_ln_b), axis=-1)
    x = x + _layernorm(_L1_ffn_ref(_layernorm(x, axis=-1), L1_ffn_input_ids, L1_ffn_gate_w, L1_ffn_gate_b, L1_ffn_w13, L1_ffn_w2, L1_ffn_w13_s, L1_ffn_w2_s), axis=-1)
    return x

_drawn_inputs = setup_inputs


def setup_inputs(seed=0):
    import zlib

    import numpy as np

    out = dict(_drawn_inputs(seed))
    spreads = {'L0_attn_qkv_b': (0.0, 0.1),
     'L0_attn_rq_b': (0.0, 2.0),
     'L0_attn_rkv_b': (0.0, 0.1),
     'L0_attn_rout_b': (0.0, 0.1),
     'L0_attn_out_b': (0.0, 0.1)}
    factors = {'L0_attn_rq_w': 8.0,
     'L0_attn_rkv_w': 2.769,
     'L0_attn_gl_w': 20.989,
     'L0_attn_gr_w': 30.785,
     'L0_ffn_b1': 5.293,
     'L0_ffn_b2': 200.0,
     'L1_attn_u': 3.482}
    for name, (base, spread) in spreads.items():
        noise = np.random.default_rng([zlib.crc32(name.encode()), seed]).standard_normal(out[name].shape)
        drawn = base * np.exp(spread * noise) if base else spread * noise
        out[name] = jnp.asarray(drawn.astype(out[name].dtype))
    for name, factor in factors.items():
        out[name] = (out[name] * factor).astype(out[name].dtype)
    return out
```

```python
from contextlib import ExitStack

import concourse.bass as bass
from concourse import mybir

F32 = mybir.dt.float32
F32R = mybir.dt.float32r
BF16 = mybir.dt.bfloat16
ALU = mybir.AluOpType
ACT = mybir.ActivationFunctionType
X = mybir.AxisListType.X

P = 128
B, S, D = 8, 512, 256
NT, NK = S // P, D // P
H, HD = 16, 16
LH, LD, NLAT = 4, 64, 64
CHUNK = S // NLAT
FF = 1024
NF = FF // P
NE, TOPK, INTER = 16, 4, 128
ROUTE_SCALE = 2.5
EPS = 1e-5
NEG = -1e30
BIG = 3e38
NPAIR = H // 2
PAIRS = 4
NLN = 6

PER = dict(
    x_in=16, x_out=16, var=NLN, rstd=NLN, normed=3 * NT, turned=NK * 3, evened=NK * 3,
    pooled=1, q_ps=2, k_ps=2, v_ps=2, rq_ps=1, rkv_ps=1, qk_hi=4, qk_lo=4, v_sb=1, rq_sb=1, rk_sb=1,
    lat_ps=1, lat_sub=2, lat_exp=2, lat_turned=NT, lat_probs=NT, lat_out=1, lat_normed=1, lat_nt=1, lat_nt_sb=1,
    remote_ps=1, remote=1, remote_gr=1,
    stack_q=NPAIR, stack_k=NPAIR, stq_sb=NPAIR, stk_sb=NPAIR, scores=NPAIR * NT, negmax=NPAIR * NT,
    probs=NPAIR * NT, p_turned=NPAIR * NT, p_even=NPAIR * NT // 2, p_odd=NPAIR * NT // 2, local_ps=NPAIR, local_raw=NPAIR,
    loc=1, diff=1, gate_z=1, gate_e=1, mixed=1, mixed_t=2, mixed_sb=2, out_ps=1,
    f_lo=1, h_ps=NF, gelu=NF, g_hi=NF, g_lo=NF, f_y=NF, fy_sb=2, fy_tok=1,
    mix=8, proj=8, v_hi=2, v_lo=1, v_f=2, k_f=2, ek=2, dec=2, decay=1, r_f=2, rb=1, bonus_ps=1, v_bc=2 * HD, kv=2 * HD,
    state=2 * HD, rs=2 * HD, summed=2 * HD, o_sb=1, o_tok=1, o_diff=1, o_sq=1, o_var=1, o_rstd=1, o_norm=1, o_back=1,
    o_aff=2, y_in=1, w_ps=1, x_final=1,
)


def program(nc, t, out):
    x3 = nc.dram_tensor("x_after_rwkv", (B, S, D), F32, kind="Internal").ap()
    mid_token_layers(nc, t, x3)
    expert_layer(nc, t, x3, out)


class Own:

    def __init__(self, eng, sem, per):
        self.eng, self.sem, self.per, self.n, self.base = eng, sem, per, 0, 0

    def start(self, b):
        self.base, self.n = b * self.per, 0

    def link(self, ins, tick=None):
        self.n += 1
        ins.then_inc(self.sem, 1)
        self.eng.wait_ge(self.sem, self.base + self.n)
        if tick is not None:
            self.eng.memset(tick, 0.0)

    def end(self):
        assert self.n == self.per, f"{self.n} links in a batch, not {self.per}"


VEC_OWN = 46
VEC_OWN_2 = 29


def mid_token_layers(nc, t, x3):
    with ExitStack() as ctx:
        def sb(name, shape, dt=F32):
            return ctx.enter_context(nc.sbuf_tensor(name, shape, dt))

        bank = [ctx.enter_context(nc.psum_tensor(f"bank{i}", [P, 512], F32)) for i in range(8)]
        sem = {n: ctx.enter_context(nc.semaphore(n)) for n in PER}
        vec_own = ctx.enter_context(nc.semaphore("vec_own"))
        loaded = ctx.enter_context(nc.semaphore("loaded"))
        const_ready = ctx.enter_context(nc.semaphore("const_ready"))
        tern_sum = ctx.enter_context(nc.semaphore("tern_sum"))
        tern_tot = ctx.enter_context(nc.semaphore("tern_tot"))
        setup_own = ctx.enter_context(nc.semaphore("setup_own"))
        s_zero = ctx.enter_context(nc.semaphore("s_zero"))

        ident = sb("ident", [P, P])
        ident_b = sb("ident_b", [P, P], BF16)
        blockones = sb("blockones", [P, P])
        sel_o = sb("sel_o", [P, HD, P])
        sel_v = sb("sel_v", [P, HD, P], F32R)
        sel_qk = sb("sel_qk", [P, PAIRS, 4, P], F32R)
        parmask = sb("parmask", [P, 2])
        lhmask = sb("lhmask", [LD, LH])
        lmask = sb("lmask", [P, NT, LH * NLAT], BF16)
        wmask = sb("wmask", [P, 2, 2 * P], BF16)
        row_loc = sb("row_loc", [P, NT, H])
        row_lat = sb("row_lat", [P, NT, LH])
        wqkv = sb("wqkv", [P, NK, 3 * D])
        qkb = sb("qkb", [P, 4])
        wrq = sb("wrq", [P, NK, LD])
        rqb = sb("rqb", [LD, 1])
        wrkv = sb("wrkv", [P, NK, 2 * LD])
        rkb = sb("rkb", [LD, 1])
        rvb = sb("rvb", [LD, LD])
        wrout = sb("wrout", [LD, D])
        wout = sb("wout", [P, NK, D])
        vb = sb("vb", [P, D])
        routb = sb("routb", [P, D])
        outb = sb("outb", [P, D])
        glr = sb("glr", [P, 2, HD])
        w1t = sb("w1t", [P, NK, FF], F32R)
        w2t = sb("w2t", [P, NF, D], F32R)
        b1 = sb("b1", [P, NF])
        b2 = sb("b2", [P, NK])
        wrk = sb("wrk", [P, 5, NK, D])
        tm = sb("tm", [P, 4, NK])
        u_c = sb("u_c", [P, NK])
        lnwb = sb("lnwb", [P, 2])
        mhalf = sb("mhalf", [P, 64])
        tick = sb("tick", [P, 1])[:]

        x_tok = sb("x_tok", [P, NT, D])
        xn = sb("xn", [P, NT, D])
        xT = sb("xT", [P, NK, S + 2])
        st = sb("st", [P, NT, 6])
        mv = sb("mv", [P, NT, 2])
        vare = sb("vare", [P, NT])
        rstd = sb("rstd", [P, NT])
        hiT = sb("hiT", [P, 4, S], F32R)
        loT = sb("loT", [P, 4, S], F32R)
        work = sb("work", [P, 12, S])
        stq = sb("stq", [P, 2, S], F32R)
        stk = sb("stk", [P, 2, 2, S], F32R)
        rsum = sb("rsum", [P, NT, H])
        rinv = sb("rinv", [P, NT, H])
        nmx = sb("nmx", [P, NPAIR * NT, 2])
        small = sb("small", [P, 6, 64])
        pt = sb("pt", [P, 2, 512])
        probs = sb("probs", [P, 4, 512])
        s_buf = sb("s_buf", [P, 2, S + 2])
        ones = sb("ones", [P, P])
        v_tok = sb("v_tok", [P, NT, D])
        poolx = sb("poolx", [P, 2, NK, NLAT])
        rk_bd = sb("rk_bd", [LD, LH, NLAT])
        rv_sb = sb("rv_sb", [LD, LD])

        def at(b, name, k):
            return b * PER[name] + k

        raw = work[:, :, :].rearrange("p a s -> p (a s)")
        n_load = [0]

        block = ctx.enter_context(nc.Block())

        def bc(ap, *shape):
            return ap.broadcast_to(shape)

        @block.sync
        def _(sp):
            def load(dst, src):
                n_load[0] += 1
                sp.dma_start(dst, src).then_inc(loaded, 16)
            load(ident[:], t["c_ident"])
            load(blockones[:], t["c_blockones"])
            load(sel_o[:], t["c_selo"])
            load(ones[:], t["c_ones"])
            load(parmask[:], t["c_parmask"])
            load(lhmask[:], t["c_lhmask"])
            load(row_loc[:], t["c_rowloc"])
            load(row_lat[:], t["c_rowlat"])
            load(mhalf[:], t["c_mhalf"])
            load(wqkv[:], t["wqkv"].rearrange("(k p) n -> p k n", p=P))
            load(qkb[:], t["qkb"])
            load(wrq[:], t["wrq"].rearrange("(k p) n -> p k n", p=P))
            load(rqb[:], t["rqb"])
            load(wrkv[:], t["wrkv"].rearrange("(k p) n -> p k n", p=P))
            load(rkb[:], t["rkb"])
            load(rvb[:], t["rvb"].partition_broadcast(LD))
            load(wrout[:], t["wrout"])
            load(wout[:], t["wout"].rearrange("(k p) n -> p k n", p=P))
            load(vb[:], t["vb"].partition_broadcast(P))
            load(routb[:], t["routb"].partition_broadcast(P))
            load(outb[:], t["outb"].partition_broadcast(P))
            load(glr[:, 0, :], t["gl"].partition_broadcast(P))
            load(glr[:, 1, :], t["gr"].partition_broadcast(P))
            load(b1[:], t["b1"])
            load(b2[:], t["b2"])
            load(wrk[:], t["wrk"].rearrange("w (k p) n -> p w k n", p=P))
            load(tm[:], t["tm"])
            load(u_c[:], t["u"])
            load(lnwb[:], t["lnwb"])
            load(raw[:, 0:2048], t["w1"].rearrange("(k p) n -> p k n", p=P))
            load(raw[:, 2048:4096], t["w2"].rearrange("(k p) n -> p k n", p=P))
            load(raw[:, 4096:6144], t["c_selv"])
            load(xT[:, 0, 0:512], t["c_wmask"])
            load(x_tok[:].rearrange("p a d -> p (a d)"), t["c_lmask"])
            load(probs[:].rearrange("p a d -> p (a d)"), t["c_selqk"])
            rows = lambda ap: ap.rearrange("o (t p) d -> p (o t) d", p=P)
            sp.wait_ge(const_ready, 1)
            sp.dma_start(x_tok[:], rows(t["x"][0:1])).then_inc(sem["x_in"], 16)
            with sp.Fori(0, B - 1) as b:
                sp.wait_ge(sem["x_final"], at(b, "x_final", 1))
                sp.dma_start(rows(x3[bass.ds(b, 1)]), x_tok[:]).then_inc(sem["x_out"], 16)
                sp.wait_ge(sem["x_out"], at(b, "x_out", 16))
                sp.dma_start(x_tok[:], rows(t["x"][bass.ds(b + 1, 1)])).then_inc(sem["x_in"], 16)
            sp.wait_ge(sem["x_final"], B)
            sp.dma_start(rows(x3[B - 1:B]), x_tok[:]).then_inc(sem["x_out"], 16)
            sp.wait_ge(sem["x_out"], B * 16)

        @block.vector
        def _(ve):
            V = nc.vector
            own = Own(ve, setup_own, 0)
            ve.wait_ge(loaded, 16 * n_load[0])
            V.tensor_copy(ident_b[:], ident[:])
            V.tensor_copy(sel_v[:].rearrange("p a m -> p (a m)"), raw[:, 4096:6144])
            V.tensor_copy(wmask[:].rearrange("p a m -> p (a m)"), xT[:, 0, 0:512])
            V.tensor_copy(lmask[:].rearrange("p a m -> p (a m)"), x_tok[:].rearrange("p a d -> p (a d)"))
            V.tensor_copy(sel_qk[:].rearrange("p a c m -> p (a c m)"), probs[:].rearrange("p a d -> p (a d)"))
            V.tensor_scalar(qkb[:, 0:2], qkb[:, 0:2], 0.25, None, ALU.mult)
            V.tensor_scalar(wqkv[:, :, 0:D], wqkv[:, :, 0:D], 0.25, None, ALU.mult)
            for i in range(2):
                V.tensor_reduce(small[:, i, 0:1], raw[:, 2048 * i:2048 * i + 2048], X, ALU.add,
                                apply_absolute_value=True).then_inc(tern_sum, 1)
            ve.wait_ge(tern_tot, 1)
            for i in range(2):
                own.link(V.tensor_scalar(small[:, i, 1:2], bank[0][:, i:i + 1], 1.0 / (FF * D), 1e-8, ALU.mult, ALU.max))
                own.link(V.tensor_scalar(small[:, i, 2:3], small[:, i, 1:2], 0.5, None, ALU.mult))
                own.link(V.tensor_scalar(small[:, i, 3:4], small[:, i, 1:2], -0.5, None, ALU.mult))
                w = raw[:, 2048 * i:2048 * i + 2048]
                neg = hiT[:].rearrange("p a s -> p (a s)")
                dst = (w1t, w2t)[i][:].rearrange("p a s -> p (a s)")
                own.link(V.tensor_scalar(neg, w, small[:, i, 3:4], None, ALU.is_lt))
                own.link(V.scalar_tensor_tensor(dst, w, small[:, i, 2:3], neg.bitcast(F32), ALU.is_gt, ALU.subtract))
            V.memset(xT[:, :, 0:1], 0.0).then_inc(const_ready, 1)

            own = Own(ve, vec_own, VEC_OWN)
            with ve.Fori(0, B) as b:
                own.start(b)
                ln = [0]

                def stats(src):
                    for i in range(NT):
                        ins = V.bn_stats(st[:, i, :], src(i))
                    own.link(ins, tick)
                    for i in range(NT):
                        ins = V.bn_aggr(mv[:, i, :], st[:, i, :])
                    own.link(ins)
                    V.tensor_scalar(vare[:], mv[:, :, 1], EPS, None, ALU.add).then_inc(sem["var"], 1)
                    ln[0] += 1
                    ve.wait_ge(sem["rstd"], at(b, "rstd", ln[0]))

                def pre_norm():
                    stats(lambda i: x_tok[:, i, :])
                    for i in range(NT):
                        V.tensor_scalar(xn[:, i, :], x_tok[:, i, :], mv[:, i, 0:1], rstd[:, i:i + 1],
                                        ALU.subtract, ALU.mult).then_inc(sem["normed"], 1)

                def residual(src, last=False):
                    stats(src)
                    for i in range(NT):
                        ins = V.tensor_scalar(xn[:, i, :], src(i), mv[:, i, 0:1], rstd[:, i:i + 1],
                                              ALU.subtract, ALU.mult)
                    own.link(ins)
                    ins = V.tensor_tensor(x_tok[:], x_tok[:], xn[:], ALU.add)
                    if last:
                        ins.then_inc(sem["x_final"], 1)
                    else:
                        own.link(ins)

                ve.wait_ge(sem["x_in"], at(b, "x_in", 16))
                pre_norm()
                ve.wait_ge(sem["evened"], at(b, "evened", 2))
                own.link(V.tensor_reduce(poolx[:, 0], xT[:, :, 1:S + 1].rearrange("p k (l c) -> p k l c", c=CHUNK), X, ALU.add))
                V.tensor_scalar(poolx[:, 1], poolx[:, 0], 1.0 / CHUNK, None, ALU.mult).then_inc(sem["pooled"], 1)
                for i in range(4):
                    ve.wait_ge(sem["qk_hi"], at(b, "qk_hi", i + 1))
                    V.scalar_tensor_tensor(loT[:, i, :], bank[2 + i][:], qkb[:, i:i + 1], hiT[:, i, :].bitcast(F32),
                                           ALU.add, ALU.subtract).then_inc(sem["qk_lo"], 1)
                ve.wait_ge(sem["v_ps"], at(b, "v_ps", 2))
                for i in range(2):
                    ins = V.tensor_tensor(v_tok[:, 2 * i:2 * i + 2, :], bank[6 + i][:].rearrange("p (a d) -> p a d", a=2),
                                          bc(vb[:].unsqueeze(1), P, 2, D), ALU.add)
                ins.then_inc(sem["v_sb"], 1)
                ve.wait_ge(sem["rkv_ps"], at(b, "rkv_ps", 1))
                for h in range(LH):
                    V.tensor_scalar(rk_bd[:, h, :], bank[1][0:LD, 0:NLAT], rkb[:, 0:1], lhmask[:, h:h + 1], ALU.add, ALU.mult)
                V.tensor_tensor(rv_sb[:], bank[1][0:NLAT, NLAT:NLAT + LD], rvb[:], ALU.add).then_inc(sem["rk_sb"], 1)

                lsub = work[:, 0:2, :]
                lexp = work[:, 2:4, :]
                ve.wait_ge(sem["lat_ps"], at(b, "lat_ps", 1))
                for i in range(2):
                    ps = bank[2 + i][:].rearrange("p (a l) -> p a l", l=NLAT)
                    own.link(V.tensor_reduce(small[:, 0, 8 * i:8 * i + 8], ps, X, ALU.max))
                    V.tensor_tensor(lsub[:, i, :].rearrange("p (a l) -> p a l", l=NLAT), ps,
                                    bc(small[:, 0, 8 * i:8 * i + 8].unsqueeze(2), P, 8, NLAT), ALU.subtract
                                    ).then_inc(sem["lat_sub"], 1)
                ve.wait_ge(sem["lat_exp"], at(b, "lat_exp", 2))
                own.link(V.tensor_reduce(small[:, 1, 0:16], lexp.rearrange("p a (h l) -> p (a h) l", l=NLAT), X, ALU.add))
                own.link(V.reciprocal(small[:, 2, 0:16], small[:, 1, 0:16]))
                own.link(V.tensor_tensor(small[:, 3, 0:16], small[:, 2, 0:16], row_lat[:].rearrange("p a h -> p (a h)"), ALU.mult))
                lat_n = work[:, 4, 0:256]
                ve.wait_ge(sem["lat_out"], at(b, "lat_out", 1))
                V.tensor_tensor(lat_n.rearrange("p (a d) -> p a d", d=16), bank[0][:, 0:256].rearrange("p (a d) -> p a d", d=16),
                                bc(small[:, 3, 0:16].unsqueeze(2), P, 16, 16), ALU.mult).then_inc(sem["lat_normed"], 1)
                rem = work[:, 6:8, :]
                ve.wait_ge(sem["remote_ps"], at(b, "remote_ps", 1))
                for i in range(2):
                    ins = V.tensor_tensor(rem[:, i, :].rearrange("p (a d) -> p a d", a=2), bank[2 + i][:].rearrange("p (a d) -> p a d", a=2),
                                          bc(routb[:].unsqueeze(1), P, 2, D), ALU.add)
                ins.then_inc(sem["remote"], 1)

                def stack_k(p):
                    ve.wait_ge(sem["stack_k"], at(b, "stack_k", p + 1))
                    for par in range(2):
                        ins = V.tensor_scalar(stk[:, p % 2, par, :], bank[0][:], parmask[:, par:par + 1], None, ALU.mult)
                    ins.then_inc(sem["stk_sb"], 1)

                def negmax(p, i):
                    n = NT * p + i
                    w = P if i == 0 else 2 * P
                    ve.wait_ge(sem["scores"], at(b, "scores", n + 1))
                    V.tensor_reduce(nmx[:, n, :], bank[2 + i][:, 0:2 * w].rearrange("p (h k) -> p h k", h=2), X, ALU.max,
                                    negate=True).then_inc(sem["negmax"], 1)

                def turn_even(p, i):
                    n = NT * p + i
                    w = 256 if i == 0 else 512
                    ve.wait_ge(sem["p_turned"], at(b, "p_turned", n + 1))
                    V.tensor_copy(pt[:, 0, 0:w], bank[6][:, 0:w]).then_inc(sem["p_even"], 1)

                loc_raw = work[:, 8:10, :]

                def local_raw(p):
                    ve.wait_ge(sem["local_ps"], at(b, "local_ps", p + 1))
                    V.tensor_copy(loc_raw.rearrange("p a (c d) -> p (a c) d", d=D)[:, :, 32 * p:32 * p + 32],
                                  bank[7][:, 128 * (p % 2):128 * (p % 2) + 128].rearrange("p (a d) -> p a d", d=32)
                                  ).then_inc(sem["local_raw"], 1)

                stack_k(0)
                for i in range(NT):
                    negmax(0, i)
                stack_k(1)
                for p in range(NPAIR):
                    for i in range(NT):
                        if i % 2 == 0:
                            turn_even(p, i)
                        if p + 1 < NPAIR:
                            negmax(p + 1, i)
                    if p + 2 < NPAIR:
                        stack_k(p + 2)
                    local_raw(p)
                ve.wait_ge(sem["probs"], at(b, "probs", NPAIR * NT))
                own.link(V.reciprocal(rinv[:], rsum[:]))
                own.link(V.tensor_tensor(rinv[:], rinv[:], row_loc[:], ALU.mult))
                loc = work[:, 0:2, :]
                v4 = lambda a: a.rearrange("p a (h d) -> p (a h) d", d=HD)
                own.link(V.tensor_tensor(v4(loc), v4(loc_raw), bc(rinv[:].rearrange("p a h -> p (a h)").unsqueeze(2), P, 64, HD), ALU.mult))
                c1 = work[:, 2:4, :]
                V.tensor_tensor(v4(c1), v4(loc), bc(glr[:, 0, :].unsqueeze(1), P, 64, HD), ALU.mult).then_inc(sem["loc"], 1)
                ve.wait_ge(sem["loc"], at(b, "loc", 1))
                ve.wait_ge(sem["remote_gr"], at(b, "remote_gr", 1))
                own.link(V.tensor_tensor(c1, c1, work[:, 10:12, :], ALU.add))
                V.tensor_reduce(small[:, 4, :], v4(c1), X, ALU.add).then_inc(sem["gate_z"], 1)
                ve.wait_ge(sem["gate_e"], at(b, "gate_e", 1))
                own.link(V.tensor_scalar(small[:, 5, :], small[:, 5, :], 1.0, None, ALU.add))
                own.link(V.reciprocal(small[:, 5, :], small[:, 5, :]))
                ve.wait_ge(sem["diff"], at(b, "diff", 1))
                own.link(V.tensor_tensor(v4(c1), v4(work[:, 4:6, :]), bc(small[:, 5, :].unsqueeze(2), P, 64, HD), ALU.mult))
                V.tensor_tensor(c1, c1, rem, ALU.add).then_inc(sem["mixed"], 1)
                ve.wait_ge(sem["out_ps"], at(b, "out_ps", 1))
                y_tok = work[:, 0:2, :].rearrange("p a (c d) -> p (a c) d", d=D)
                for i in range(2):
                    ins = V.tensor_tensor(y_tok[:, 2 * i:2 * i + 2, :], bank[2 + i][:].rearrange("p (a d) -> p a d", a=2),
                                          bc(outb[:].unsqueeze(1), P, 2, D), ALU.add)
                own.link(ins)
                residual(lambda i: y_tok[:, i, :])

                pre_norm()
                ve.wait_ge(sem["evened"], at(b, "evened", 4))
                for k in range(NK):
                    ins = V.tensor_tensor(loT[:, k, :], bank[k][:], hiT[:, k, :].bitcast(F32), ALU.subtract)
                ins.then_inc(sem["f_lo"], 1)
                for f in range(NF):
                    ve.wait_ge(sem["gelu"], at(b, "gelu", f + 1))
                    if f >= 2:
                        ve.wait_ge(sem["f_y"], at(b, "f_y", f - 1))
                    own.link(V.tensor_copy(stq[:, f % 2, :], work[:, f % 2, :]))
                    V.tensor_tensor(stk[:, 0, f % 2, :], work[:, f % 2, :], stq[:, f % 2, :].bitcast(F32), ALU.subtract
                                    ).then_inc(sem["g_lo"], 1)
                tok = lambda i: bank[2 + i // 2][:, (i % 2) * D:(i % 2) * D + D]
                ve.wait_ge(sem["fy_tok"], at(b, "fy_tok", 1))
                residual(tok)

                pre_norm()
                ve.wait_ge(sem["evened"], at(b, "evened", 6))
                dx = work[:, 0:2, :]
                own.link(V.tensor_tensor(dx, xT[:, :, 1:S + 1], xT[:, :, 0:S], ALU.subtract))
                for w in range(4):
                    for k in range(NK):
                        V.scalar_tensor_tensor(work[:, 2 + 2 * w + k, :], dx[:, k, :], tm[:, w, k:k + 1], xT[:, k, 0:S],
                                               ALU.mult, ALU.add).then_inc(sem["mix"], 1)
                v_hi, v_lo = hiT[:, 0:2, :], loT[:, 0:2, :]
                for g in range(2):
                    ve.wait_ge(sem["v_f"], at(b, "v_f", g + 1))
                    ins = V.tensor_tensor(v_lo[:, g, :], work[:, g, :], v_hi[:, g, :].bitcast(F32), ALU.subtract)
                ins.then_inc(sem["v_lo"], 1)
                vf, kf, ek, dec, rf = (work[:, i:i + 2, :] for i in (0, 2, 4, 6, 8))
                ve.wait_ge(sem["dec"], at(b, "dec", 2))
                own.link(V.tensor_scalar(dec, dec, 0.9999000049998333, None, ALU.mult))
                ve.wait_ge(sem["r_f"], at(b, "r_f", 2))
                V.tensor_tensor(work[:, 10:12, :], rf, ek, ALU.mult).then_inc(sem["rb"], 1)
                kvb, sbuf = pt, probs

                def kv(n):
                    ve.wait_ge(sem["v_bc"], at(b, "v_bc", n + 1))
                    if n >= 2:
                        ve.wait_ge(sem["state"], at(b, "state", n - 1))
                    V.tensor_tensor(kvb[:, n % 2, :], kf[:, n // HD, :], bank[2 + n % 3][:], ALU.mult).then_inc(sem["kv"], 1)

                kv(0)
                for n in range(2 * HD):
                    if n + 1 < 2 * HD:
                        kv(n + 1)
                    ve.wait_ge(sem["kv"], at(b, "kv", n + 1))
                    if n >= 2:
                        ve.wait_ge(sem["rs"], at(b, "rs", n - 1))
                    V.tensor_tensor_scan(s_buf[:, n % 2, 1:S + 1], dec[:, n // HD, :], kvb[:, n % 2, :], 0.0, ALU.mult, ALU.add
                                         ).then_inc(sem["state"], 1)
                ve.wait_ge(sem["bonus_ps"], at(b, "bonus_ps", 1))
                o_f = work[:, 2:4, :]
                for g in range(2):
                    own.link(V.tensor_tensor(o_f[:, g, :], vf[:, g, :], bank[g][:], ALU.mult))
                ve.wait_ge(sem["summed"], at(b, "summed", 2 * HD))
                for g in range(2):
                    ins = V.tensor_tensor(o_f[:, g, :], o_f[:, g, :], bank[6 + g][:], ALU.add)
                ins.then_inc(sem["o_sb"], 1)
                ve.wait_ge(sem["o_tok"], at(b, "o_tok", 1))
                od, osq = work[:, 4:6, :], work[:, 6:8, :]
                for i in range(2):
                    ins = V.tensor_reduce(small[:, 0, 32 * i:32 * i + 32], bank[i][:].rearrange("p (a d) -> p a d", d=HD), X, ALU.add)
                own.link(ins)
                own.link(V.tensor_scalar(small[:, 1, :], small[:, 0, :], 1.0 / HD, None, ALU.mult))
                for i in range(2):
                    ins = V.tensor_tensor(od[:, i, :].rearrange("p (a d) -> p a d", d=HD), bank[i][:].rearrange("p (a d) -> p a d", d=HD),
                                          bc(small[:, 1, 32 * i:32 * i + 32].unsqueeze(2), P, 32, HD), ALU.subtract)
                ins.then_inc(sem["o_diff"], 1)
                ve.wait_ge(sem["o_sq"], at(b, "o_sq", 1))
                own.link(V.tensor_reduce(small[:, 2, :], v4(osq), X, ALU.add))
                V.tensor_scalar(small[:, 3, :], small[:, 2, :], 1.0 / HD, EPS, ALU.mult, ALU.add).then_inc(sem["o_var"], 1)
                ve.wait_ge(sem["o_rstd"], at(b, "o_rstd", 1))
                V.tensor_tensor(v4(osq), v4(od), bc(small[:, 4, :].unsqueeze(2), P, 64, HD), ALU.mult).then_inc(sem["o_norm"], 1)
                ve.wait_ge(sem["o_aff"], at(b, "o_aff", 2))
                V.tensor_tensor(work[:, 4:6, :], work[:, 2:4, :], rf, ALU.mult).then_inc(sem["y_in"], 1)
                ve.wait_ge(sem["w_ps"], at(b, "w_ps", 1))
                residual(lambda i: bank[4 + i // 2][:, (i % 2) * D:(i % 2) * D + D], last=True)
                own.end()

        @block.gpsimd
        def _(gp):
            G = nc.gpsimd
            G.memset(s_buf[:, :, 0:1], 0.0).then_inc(s_zero, 1)
            gp.wait_ge(const_ready, 1)
            with gp.Fori(0, B) as b:
                def pow_(k):
                    gp.wait_ge(sem["var"], at(b, "var", k + 1))
                    G.tensor_tensor(rstd[:], vare[:], mhalf[:, 0:NT], ALU.pow).then_inc(sem["rstd"], 1)

                pow_(0)
                gp.wait_ge(sem["remote"], at(b, "remote", 1))
                v4 = lambda a: a.rearrange("p a (h d) -> p (a h) d", d=HD)
                G.tensor_tensor(v4(work[:, 10:12, :]), v4(work[:, 6:8, :]), bc(glr[:, 1, :].unsqueeze(1), P, 64, HD), ALU.mult
                                ).then_inc(sem["remote_gr"], 1)
                gp.wait_ge(sem["loc"], at(b, "loc", 1))
                G.tensor_tensor(work[:, 4:6, :], work[:, 0:2, :], work[:, 6:8, :], ALU.subtract).then_inc(sem["diff"], 1)
                for k in range(1, NLN):
                    if k == NLN - 1:
                        gp.wait_ge(s_zero, 1)
                        rf = work[:, 8:10, :]
                        for n in range(2 * HD):
                            gp.wait_ge(sem["state"], at(b, "state", n + 1))
                            if n == 0:
                                gp.wait_ge(sem["r_f"], at(b, "r_f", 2))
                            if n >= 2:
                                gp.wait_ge(sem["summed"], at(b, "summed", n - 1))
                            G.tensor_tensor(probs[:, n % 2, :], s_buf[:, n % 2, 0:S], rf[:, n // HD, :], ALU.mult
                                            ).then_inc(sem["rs"], 1)
                        gp.wait_ge(sem["o_var"], at(b, "o_var", 1))
                        G.tensor_tensor(small[:, 4, :], small[:, 3, :], mhalf[:], ALU.pow).then_inc(sem["o_rstd"], 1)
                    pow_(k)

        @block.scalar
        def _(sc):
            A = nc.scalar.activation
            sc.wait_ge(const_ready, 1)
            with sc.Fori(0, B) as b:
                for k in range(NK):
                    sc.wait_ge(sem["turned"], at(b, "turned", k + 1))
                    A(xT[:, k, 1:S + 1], bank[k][:], ACT.Copy).then_inc(sem["evened"], 1)
                for i in range(4):
                    sc.wait_ge(sem["q_ps" if i < 2 else "k_ps"], at(b, "q_ps", i % 2 + 1))
                    A(hiT[:, i, :], bank[2 + i][:], ACT.Identity, bias=qkb[:, i:i + 1]).then_inc(sem["qk_hi"], 1)
                sc.wait_ge(sem["rq_ps"], at(b, "rq_ps", 1))
                rqT = work[0:LD, 5, :]
                A(rqT, bank[0][0:LD, :], ACT.Identity, bias=rqb[:, 0:1]).then_inc(sem["rq_sb"], 1)
                for i in range(2):
                    sc.wait_ge(sem["lat_sub"], at(b, "lat_sub", i + 1))
                    A(work[:, 2 + i, :], work[:, i, :], ACT.Exp, scale=0.25).then_inc(sem["lat_exp"], 1)
                for i in range(NT):
                    sc.wait_ge(sem["lat_turned"], at(b, "lat_turned", i + 1))
                    A(work[0:NLAT, 8 + i, :], bank[4 + i][0:NLAT, :], ACT.Copy).then_inc(sem["lat_probs"], 1)
                sc.wait_ge(sem["lat_nt"], at(b, "lat_nt", 1))
                A(work[0:LD, 5, :], bank[1][0:LD, :], ACT.Copy).then_inc(sem["lat_nt_sb"], 1)

                def stack_q(p):
                    sc.wait_ge(sem["stack_q"], at(b, "stack_q", p + 1))
                    A(stq[:, p % 2, :], bank[0][:], ACT.Copy).then_inc(sem["stq_sb"], 1)

                def exps(p, i):
                    n = NT * p + i
                    w = P if i == 0 else 2 * P
                    sc.wait_ge(sem["negmax"], at(b, "negmax", n + 1))
                    for h in range(2):
                        ins = A(probs[:, i, h * w:h * w + w], bank[2 + i][:, h * w:h * w + w], ACT.Exp, bias=nmx[:, n, h:h + 1],
                                accum_out=rsum[:, i, 2 * p + h:2 * p + h + 1])
                    ins.then_inc(sem["probs"], 1)

                def turn_odd(p, i):
                    n = NT * p + i
                    sc.wait_ge(sem["p_turned"], at(b, "p_turned", n + 1))
                    A(pt[:, 1, :], bank[1][:], ACT.Copy).then_inc(sem["p_odd"], 1)

                stack_q(0)
                for i in range(NT):
                    exps(0, i)
                stack_q(1)
                for p in range(NPAIR):
                    for i in range(NT):
                        if i % 2 == 1:
                            turn_odd(p, i)
                        if i == 3 and p + 2 < NPAIR:
                            stack_q(p + 2)
                        if p + 1 < NPAIR:
                            exps(p + 1, i)
                sc.wait_ge(sem["gate_z"], at(b, "gate_z", 1))
                A(small[:, 5, :], small[:, 4, :], ACT.Exp, scale=-1.0).then_inc(sem["gate_e"], 1)
                for k in range(NK):
                    sc.wait_ge(sem["mixed_t"], at(b, "mixed_t", k + 1))
                    A(work[:, 8 + k, :], bank[k][:], ACT.Copy).then_inc(sem["mixed_sb"], 1)
                for k in range(NK):
                    sc.wait_ge(sem["turned"], at(b, "turned", 2 + k + 1))
                    A(hiT[:, k, :], bank[k][:], ACT.Copy).then_inc(sem["evened"], 1)
                for f in range(NF):
                    sc.wait_ge(sem["h_ps"], at(b, "h_ps", f + 1))
                    if f >= 2:
                        sc.wait_ge(sem["g_lo"], at(b, "g_lo", f - 1))
                    A(work[:, f % 2, :], bank[2 + f % 4][:], ACT.Gelu, bias=b1[:, f:f + 1]).then_inc(sem["gelu"], 1)
                sc.wait_ge(sem["f_y"], at(b, "f_y", NF))
                for k in range(NK):
                    A(work[:, 2 + k, :], bank[6 + k][:], ACT.Identity, bias=b2[:, k:k + 1]).then_inc(sem["fy_sb"], 1)
                for k in range(NK):
                    sc.wait_ge(sem["turned"], at(b, "turned", 4 + k + 1))
                    A(xT[:, k, 1:S + 1], bank[k][:], ACT.Copy).then_inc(sem["evened"], 1)
                vf, kf, ek, dec, rf = (work[:, i:i + 2, :] for i in (0, 2, 4, 6, 8))
                sc.wait_ge(sem["mix"], at(b, "mix", 8))
                for g in range(2):
                    sc.wait_ge(sem["proj"], at(b, "proj", g + 1))
                    A(hiT[:, g, :], bank[2 + g][:], ACT.Copy).then_inc(sem["v_hi"], 1)
                    A(vf[:, g, :], bank[2 + g][:], ACT.Copy).then_inc(sem["v_f"], 1)
                sc.wait_ge(sem["proj"], at(b, "proj", 8))
                for g in range(2):
                    A(kf[:, g, :], bank[4 + g][:], ACT.Copy).then_inc(sem["k_f"], 1)
                    A(ek[:, g, :], bank[4 + g][:], ACT.Exp, bias=u_c[:, g:g + 1]).then_inc(sem["ek"], 1)
                for g in range(2):
                    A(dec[:, g, :], bank[6 + g][:], ACT.Sigmoid).then_inc(sem["dec"], 1)
                for g in range(2):
                    A(rf[:, g, :], bank[g][:], ACT.Sigmoid).then_inc(sem["r_f"], 1)
                sc.wait_ge(sem["o_diff"], at(b, "o_diff", 1))
                A(work[:, 6:8, :], work[:, 4:6, :], ACT.Square).then_inc(sem["o_sq"], 1)
                sc.wait_ge(sem["o_back"], at(b, "o_back", 1))
                for g in range(2):
                    A(work[:, 2 + g, :], bank[2 + g][:], ACT.Identity, bias=lnwb[:, 1:2], scale=lnwb[:, 0:1]).then_inc(sem["o_aff"], 1)

        @block.tensor
        def _(pe):
            T = nc.tensor
            pe.wait_ge(loaded, 16 * n_load[0])
            pe.wait_ge(tern_sum, 2)
            for i in range(2):
                ins = T.matmul(bank[0][:, i:i + 1], ones[:], small[:, i, 0:1], start=True, stop=True)
            ins.then_inc(tern_tot, 1)
            pe.wait_ge(const_ready, 1)

            with pe.Fori(0, B) as b:
                def turn_x(n):
                    for i in range(NT):
                        pe.wait_ge(sem["normed"], at(b, "normed", NT * n + i + 1))
                        for k in range(NK):
                            ins = T.transpose(bank[k][:, i * P:(i + 1) * P], xn[:, i, k * P:(k + 1) * P], ident[:])
                            if i == NT - 1:
                                ins.then_inc(sem["turned"], 1)

                turn_x(0)
                pe.wait_ge(sem["evened"], at(b, "evened", 2))
                for i in range(4):
                    for k in range(NK):
                        ins = T.matmul(bank[2 + i][:], wqkv[:, k, i * P:(i + 1) * P], xT[:, k, 1:S + 1], start=k == 0, stop=k == NK - 1)
                    ins.then_inc(sem["q_ps" if i < 2 else "k_ps"], 1)
                for i in range(NT):
                    for k in range(NK):
                        ins = T.matmul(bank[6 + i // 2][:, (i % 2) * D:(i % 2) * D + D], xT[:, k, 1 + i * P:1 + (i + 1) * P],
                                       wqkv[:, k, 2 * D:3 * D], start=k == 0, stop=k == NK - 1)
                    if i % 2:
                        ins.then_inc(sem["v_ps"], 1)
                for k in range(NK):
                    ins = T.matmul(bank[0][0:LD, :], wrq[:, k, :], xT[:, k, 1:S + 1], start=k == 0, stop=k == NK - 1)
                ins.then_inc(sem["rq_ps"], 1)
                pe.wait_ge(sem["pooled"], at(b, "pooled", 1))
                for k in range(NK):
                    T.matmul(bank[1][0:LD, 0:NLAT], wrkv[:, k, 0:LD], poolx[:, 1, k, :], start=k == 0, stop=k == NK - 1)
                for k in range(NK):
                    ins = T.matmul(bank[1][0:NLAT, NLAT:NLAT + LD], poolx[:, 1, k, :], wrkv[:, k, LD:2 * LD], start=k == 0, stop=k == NK - 1)
                ins.then_inc(sem["rkv_ps"], 1)
                pe.wait_ge(sem["qk_lo"], at(b, "qk_lo", 4))
                pe.wait_ge(sem["rk_sb"], at(b, "rk_sb", 1))
                pe.wait_ge(sem["rq_sb"], at(b, "rq_sb", 1))
                for i in range(NT):
                    o = bank[2 + i // 2][:, (i % 2) * 256:(i % 2) * 256 + 256]
                    T.matmul(o, ident_b[:], lmask[:, i, :], start=True, stop=False)
                    ins = T.matmul(o, work[0:LD, 5, i * P:(i + 1) * P], rk_bd[:].rearrange("p h l -> p (h l)"), start=False, stop=True)
                ins.then_inc(sem["lat_ps"], 1)
                pe.wait_ge(sem["lat_exp"], at(b, "lat_exp", 2))
                pe.wait_ge(sem["v_sb"], at(b, "v_sb", 1))
                T.transpose(bank[4][:, 0:P], work[:, 2, 0:P], ident[:])
                for i in range(NT):
                    for h in range(LH):
                        ins = T.transpose(bank[4 + i][0:NLAT, h * P:(h + 1) * P],
                                          work[:, 2 + i // 2, (i % 2) * 256 + h * NLAT:(i % 2) * 256 + (h + 1) * NLAT], ident[:])
                    ins.then_inc(sem["lat_turned"], 1)
                for i in range(NT):
                    pe.wait_ge(sem["lat_probs"], at(b, "lat_probs", i + 1))
                    for h in range(LH):
                        ins = T.matmul(bank[0][:, i * LD + h * 16:i * LD + h * 16 + 16], work[0:NLAT, 8 + i, h * P:(h + 1) * P],
                                       rv_sb[:, h * 16:h * 16 + 16], start=True, stop=True)
                ins.then_inc(sem["lat_out"], 1)
                pe.wait_ge(sem["lat_normed"], at(b, "lat_normed", 1))
                T.transpose(bank[1][:, 0:P], work[:, 4, 0:P], ident[:])
                for i in range(NT):
                    ins = T.transpose(bank[1][0:LD, i * P:(i + 1) * P], work[:, 4, i * LD:(i + 1) * LD], ident[:])
                ins.then_inc(sem["lat_nt"], 1)
                pe.wait_ge(sem["lat_nt_sb"], at(b, "lat_nt_sb", 1))
                for i in range(NT):
                    ins = T.matmul(bank[2 + i // 2][:, (i % 2) * D:(i % 2) * D + D], work[0:LD, 5, i * P:(i + 1) * P], wrout[:],
                                   start=True, stop=True)
                ins.then_inc(sem["remote_ps"], 1)

                def stack_q(p):
                    g, j = p // PAIRS, p % PAIRS
                    if p:
                        pe.wait_ge(sem["stk_sb"], at(b, "stk_sb", p))
                    T.matmul(bank[0][:], sel_qk[:, j, 0, :], hiT[:, g, :], start=True, stop=False)
                    T.matmul(bank[0][:], sel_qk[:, j, 1, :], loT[:, g, :], start=False, stop=True).then_inc(sem["stack_q"], 1)

                def stack_k(p):
                    g, j = p // PAIRS, p % PAIRS
                    pe.wait_ge(sem["stq_sb"], at(b, "stq_sb", p + 1))
                    T.matmul(bank[0][:], sel_qk[:, j, 2, :], hiT[:, 2 + g, :], start=True, stop=False)
                    T.matmul(bank[0][:], sel_qk[:, j, 3, :], loT[:, 2 + g, :], start=False, stop=True).then_inc(sem["stack_k"], 1)

                def scores(p, i):
                    if i == 0:
                        pe.wait_ge(sem["stq_sb"], at(b, "stq_sb", p + 1))
                        pe.wait_ge(sem["stk_sb"], at(b, "stk_sb", p + 1))
                    o = bank[2 + i]
                    q = stq[:, p % 2, i * P:(i + 1) * P]
                    w, k0 = (P, 0) if i == 0 else (2 * P, (i - 1) * P)
                    mask = wmask[:, :, P:2 * P] if i == 0 else wmask[:]
                    T.matmul(o[:, 0:2 * w], ident_b[:], mask, start=True, stop=True)
                    for par in range(2):
                        ins = T.matmul(o[:, par * w:par * w + w], q, stk[:, p % 2, par, k0:k0 + w], start=False, stop=True,
                                       skip_group_check=True)
                    ins.then_inc(sem["scores"], 1)

                def turn_p(p, i):
                    n = NT * p + i
                    pe.wait_ge(sem["probs"], at(b, "probs", n + 1))
                    o = (bank[6], bank[1])[i % 2]
                    if n >= 2:
                        pe.wait_ge(sem["p_odd" if i % 2 else "p_even"], at(b, "p_odd", n // 2))
                    w = P if i == 0 else 2 * P
                    for c in range(2 * w // P):
                        ins = T.transpose(o[:, c * P:(c + 1) * P], probs[:, i, c * P:(c + 1) * P], ident[:])
                    ins.then_inc(sem["p_turned"], 1)

                def pv(p, i):
                    n = NT * p + i
                    pe.wait_ge(sem["p_odd" if i % 2 else "p_even"], at(b, "p_odd", n // 2 + 1))
                    if i == 0 and p >= 2:
                        pe.wait_ge(sem["local_raw"], at(b, "local_raw", p - 1))
                    for h in range(2):
                        o = bank[7][:, 128 * (p % 2) + 32 * i + 16 * h:128 * (p % 2) + 32 * i + 16 * h + 16]
                        hh = 2 * p + h
                        blocks = [0] if i == 0 else [i - 1, i]
                        for c, kb in enumerate(blocks):
                            ins = T.matmul(o, pt[:, i % 2, (h * len(blocks) + c) * P:(h * len(blocks) + c + 1) * P],
                                           v_tok[:, kb, hh * HD:(hh + 1) * HD], start=c == 0, stop=c == len(blocks) - 1)
                    if i == NT - 1:
                        ins.then_inc(sem["local_ps"], 1)

                pe.wait_ge(sem["remote"], at(b, "remote", 1))
                stack_q(0)
                stack_k(0)
                for i in range(NT):
                    scores(0, i)
                stack_q(1)
                stack_k(1)
                for p in range(NPAIR):
                    for i in range(NT):
                        turn_p(p, i)
                        if p + 1 < NPAIR:
                            scores(p + 1, i)
                        if i:
                            pv(p, i - 1)
                        if i == 2 and p + 2 < NPAIR:
                            stack_q(p + 2)
                        if i == 3 and p + 2 < NPAIR:
                            stack_k(p + 2)
                    pv(p, NT - 1)
                pe.wait_ge(sem["mixed"], at(b, "mixed", 1))
                for k in range(NK):
                    for i in range(NT):
                        c = (i % 2) * D + k * P
                        ins = T.transpose(bank[k][:, i * P:(i + 1) * P], work[:, 2 + i // 2, c:c + P], ident[:])
                    ins.then_inc(sem["mixed_t"], 1)
                pe.wait_ge(sem["mixed_sb"], at(b, "mixed_sb", 2))
                for i in range(NT):
                    for k in range(NK):
                        ins = T.matmul(bank[2 + i // 2][:, (i % 2) * D:(i % 2) * D + D], work[:, 8 + k, i * P:(i + 1) * P],
                                       wout[:, k, :], start=k == 0, stop=k == NK - 1)
                ins.then_inc(sem["out_ps"], 1)

                turn_x(1)
                pe.wait_ge(sem["evened"], at(b, "evened", 4))
                pe.wait_ge(sem["f_lo"], at(b, "f_lo", 1))

                def up(f):
                    if f >= 4:
                        pe.wait_ge(sem["gelu"], at(b, "gelu", f - 3))
                    for k in range(NK):
                        for c, part in enumerate((hiT, loT)):
                            ins = T.matmul(bank[2 + f % 4][:], w1t[:, k, f * P:(f + 1) * P], part[:, k, :],
                                           start=k == 0 and c == 0, stop=k == NK - 1 and c == 1)
                    ins.then_inc(sem["h_ps"], 1)

                def down(f):
                    pe.wait_ge(sem["g_lo"], at(b, "g_lo", f + 1))
                    for k in range(NK):
                        for c, part in enumerate((stq[:, f % 2, :], stk[:, 0, f % 2, :])):
                            ins = T.matmul(bank[6 + k][:], w2t[:, f, k * P:(k + 1) * P], part, start=f == 0 and c == 0,
                                           stop=f == NF - 1 and c == 1)
                    ins.then_inc(sem["f_y"], 1)

                for f in range(NF + 2):
                    if f < NF:
                        up(f)
                    if f >= 2:
                        down(f - 2)
                pe.wait_ge(sem["fy_sb"], at(b, "fy_sb", 2))
                for i in range(NT):
                    for k in range(NK):
                        ins = T.transpose(bank[2 + i // 2][:, (i % 2) * D + k * P:(i % 2) * D + (k + 1) * P],
                                          work[:, 2 + k, i * P:(i + 1) * P], ident[:])
                ins.then_inc(sem["fy_tok"], 1)

                turn_x(2)
                pe.wait_ge(sem["mix"], at(b, "mix", 2))
                for w in range(4):
                    pe.wait_ge(sem["mix"], at(b, "mix", 2 * w + 2))
                    if w == 3:
                        pe.wait_ge(sem["evened"], at(b, "evened", 6))
                    for g in range(2):
                        o = bank[(2 + 2 * w + g) % 8]
                        for k in range(NK):
                            ins = T.matmul(o[:], wrk[:, w, k, g * P:(g + 1) * P], work[:, 2 + 2 * w + k, :], start=k == 0, stop=k == NK - 1)
                        ins.then_inc(sem["proj"], 1)

                def spread_v(n):
                    g, j = divmod(n, HD)
                    if n >= 3:
                        pe.wait_ge(sem["kv"], at(b, "kv", n - 2))
                    o = bank[2 + n % 3]
                    T.matmul(o[:], sel_v[:, j, :], hiT[:, g, :], start=True, stop=False)
                    T.matmul(o[:], sel_v[:, j, :], loT[:, g, :], start=False, stop=True).then_inc(sem["v_bc"], 1)

                def reduce_o(n):
                    g, j = divmod(n, HD)
                    pe.wait_ge(sem["rs"], at(b, "rs", n + 1))
                    T.matmul(bank[6 + g][:], sel_o[:, j, :], probs[:, n % 2, :], start=j == 0, stop=j == HD - 1
                             ).then_inc(sem["summed"], 1)

                pe.wait_ge(sem["v_lo"], at(b, "v_lo", 1))
                pe.wait_ge(sem["v_f"], at(b, "v_f", 2))
                pe.wait_ge(sem["ek"], at(b, "ek", 2))
                for n in range(3):
                    spread_v(n)
                pe.wait_ge(sem["rb"], at(b, "rb", 1))
                for g in range(2):
                    ins = T.matmul(bank[g][:], blockones[:], work[:, 10 + g, :], start=True, stop=True)
                ins.then_inc(sem["bonus_ps"], 1)
                for n in range(2 * HD):
                    reduce_o(n)
                    if n + 3 < 2 * HD:
                        spread_v(n + 3)
                pe.wait_ge(sem["o_sb"], at(b, "o_sb", 1))
                for i in range(NT):
                    for g in range(2):
                        ins = T.transpose(bank[i // 2][:, (i % 2) * D + g * P:(i % 2) * D + (g + 1) * P], work[:, 2 + g, i * P:(i + 1) * P], ident[:])
                ins.then_inc(sem["o_tok"], 1)
                pe.wait_ge(sem["o_norm"], at(b, "o_norm", 1))
                for g in range(2):
                    for i in range(NT):
                        c = (i % 2) * D + g * P
                        ins = T.transpose(bank[2 + g][:, i * P:(i + 1) * P], work[:, 6 + i // 2, c:c + P], ident[:])
                ins.then_inc(sem["o_back"], 1)
                pe.wait_ge(sem["y_in"], at(b, "y_in", 1))
                for i in range(NT):
                    for k in range(NK):
                        ins = T.matmul(bank[4 + i // 2][:, (i % 2) * D:(i % 2) * D + D], work[:, 4 + k, i * P:(i + 1) * P],
                                       wrk[:, 4, k, :], start=k == 0, stop=k == NK - 1)
                ins.then_inc(sem["w_ps"], 1)


PER2 = dict(
    x_in=16, x_out=16, var=2, rstd=2, normed=NT, turned=NK, x_f=NK, x_hi=NK, x_lo=NK, route_ps=1, score=1, comb=1, comb_ps=1,
    comb_hi=1, comb_lo=1, gate_ps=NE + 1, up_ps=NE + 1, c_ps=NE, silu=NE + 1, h_f=NE + 1, h_hi=NE + 1, h_lo=NE + 1,
    y_acc=NE + 1, y_sb=NK, y_tok=1, x_final=1,
)


def expert_layer(nc, t, x3, out):
    with ExitStack() as ctx:
        def sb(name, shape, dt=F32):
            return ctx.enter_context(nc.sbuf_tensor(name, shape, dt))

        bank = [ctx.enter_context(nc.psum_tensor(f"mbank{i}", [P, 512], F32)) for i in range(8)]
        sem = {n: ctx.enter_context(nc.semaphore("m_" + n)) for n in PER2}
        vec_own = ctx.enter_context(nc.semaphore("m_vec_own"))
        loaded = ctx.enter_context(nc.semaphore("m_loaded"))
        w_loaded = [ctx.enter_context(nc.semaphore(f"m_w_loaded{i}")) for i in range(2)]
        w_split = ctx.enter_context(nc.semaphore("m_w_split"))
        w_hi_made = ctx.enter_context(nc.semaphore("m_w_hi_made"))
        const_ready = ctx.enter_context(nc.semaphore("m_const_ready"))

        NX = NE + 1
        W13, W2 = NK * 2 * INTER, D
        ident = sb("m_ident", [P, P])
        sel_e = sb("sel_e", [64, NE, P], F32R)
        gate_w = sb("gate_w", [P, NK, NE])
        gate_b = sb("gate_b", [P, NE])
        mhalf = sb("m_mhalf", [P, NT])
        tick = sb("m_tick", [P, 1])[:]
        w_hi = sb("w_hi", [P, NX, W13 + W2], F32R)
        w_lo = sb("w_lo", [P, NX, W13 + W2], F32R)
        w_raw = sb("w_raw", [P, 2, W13 + W2])
        sel_raw = sb("sel_raw", [64, NE * P])

        x_tok = sb("m_x_tok", [P, NT, D])
        xn = sb("m_xn", [P, NT, D])
        xf = sb("m_xf", [P, NK, S])
        xh = sb("m_xh", [P, NK, S], F32R)
        xl = sb("m_xl", [P, NK, S], F32R)
        st = sb("m_st", [P, NT, 6])
        mv = sb("m_mv", [P, NT, 2])
        vare = sb("m_vare", [P, NT])
        rstd = sb("m_rstd", [P, NT])
        score = sb("score", [P, NT, NE])
        biased = sb("biased", [P, NT, NE + TOPK])
        rest = sb("rest", [P, NT, NE + TOPK])
        top = sb("top", [P, NT, 8])
        comb = sb("comb", [P, NT, NE])
        csum = sb("csum", [P, 2, NT])
        combT = sb("combT", [64, S], F32R)
        sg = sb("sg", [P, 2, S])
        hf = sb("hf", [P, 2, S])
        hh = sb("hh", [P, 2, S], F32R)
        hl = sb("hl", [P, 2, S], F32R)
        yT = sb("yT", [P, NK, S])

        def at(b, name, k):
            return b * PER2[name] + k

        def bc(ap, *shape):
            return ap.broadcast_to(shape)

        N_LOAD = 5
        block = ctx.enter_context(nc.Block())

        @block.sync
        def _(sp):
            sp.dma_start(ident[:], t["c_ident"]).then_inc(loaded, 16)
            sp.dma_start(gate_w[:], t["gate_w"].rearrange("(k p) n -> p k n", p=P)).then_inc(loaded, 16)
            sp.dma_start(gate_b[:], t["gate_b"].partition_broadcast(P)).then_inc(loaded, 16)
            sp.dma_start(mhalf[:], t["c_mhalf"][:, 0:NT]).then_inc(loaded, 16)
            sp.dma_start(sel_raw[:], t["c_sele"]).then_inc(loaded, 16)

            def weights(e):
                if e >= 2:
                    sp.wait_ge(w_split, e - 1)
                sp.dma_start(w_raw[:, e % 2, 0:W13], t["w13"][e].rearrange("(k p) n -> p k n", p=P)).then_inc(w_loaded[e % 2], 16)
                sp.dma_start(w_raw[:, e % 2, W13:], t["w2e"][e]).then_inc(w_loaded[e % 2], 16)

            for e in range(NX):
                weights(e)
            rows = lambda ap: ap.rearrange("o (t p) d -> p (o t) d", p=P)
            sp.dma_start(x_tok[:], rows(x3[0:1])).then_inc(sem["x_in"], 16)
            with sp.Fori(0, B - 1) as b:
                sp.wait_ge(sem["x_final"], at(b, "x_final", 1))
                sp.dma_start(rows(out[bass.ds(b, 1)]), x_tok[:]).then_inc(sem["x_out"], 16)
                sp.wait_ge(sem["x_out"], at(b, "x_out", 16))
                sp.dma_start(x_tok[:], rows(x3[bass.ds(b + 1, 1)])).then_inc(sem["x_in"], 16)
            sp.wait_ge(sem["x_final"], B)
            sp.dma_start(rows(out[B - 1:B]), x_tok[:]).then_inc(sem["x_out"], 16)
            sp.wait_ge(sem["x_out"], B * 16)

        @block.vector
        def _(ve):
            V = nc.vector
            V.memset(biased[:, :, NE:], BIG)
            V.memset(combT[:].bitcast(F32), 0.0)
            ve.wait_ge(loaded, 16 * N_LOAD)
            V.tensor_copy(sel_e[:].rearrange("p e m -> p (e m)"), sel_raw[:]).then_inc(const_ready, 1)
            for e in range(NX):
                ve.wait_ge(w_hi_made, e + 1)
                V.tensor_tensor(w_lo[:, e, :], w_raw[:, e % 2, :], w_hi[:, e, :].bitcast(F32), ALU.subtract).then_inc(w_split, 1)
            own = Own(ve, vec_own, VEC_OWN_2)
            with ve.Fori(0, B) as b:
                own.start(b)

                def stats(src, k):
                    for i in range(NT):
                        ins = V.bn_stats(st[:, i, :], src(i))
                    own.link(ins, tick)
                    for i in range(NT):
                        ins = V.bn_aggr(mv[:, i, :], st[:, i, :])
                    own.link(ins)
                    V.tensor_scalar(vare[:], mv[:, :, 1], EPS, None, ALU.add).then_inc(sem["var"], 1)
                    ve.wait_ge(sem["rstd"], at(b, "rstd", k))

                ve.wait_ge(sem["x_in"], at(b, "x_in", 16))
                stats(lambda i: x_tok[:, i, :], 1)
                for i in range(NT):
                    V.tensor_scalar(xn[:, i, :], x_tok[:, i, :], mv[:, i, 0:1], rstd[:, i:i + 1], ALU.subtract, ALU.mult
                                    ).then_inc(sem["normed"], 1)
                for k in range(NK):
                    ve.wait_ge(sem["x_f"], at(b, "x_f", k + 1))
                    V.tensor_tensor(xl[:, k, :], xf[:, k, :], xh[:, k, :].bitcast(F32), ALU.subtract).then_inc(sem["x_lo"], 1)
                ve.wait_ge(sem["score"], at(b, "score", 1))
                own.link(V.tensor_tensor(biased[:, :, 0:NE], score[:], bc(gate_b[:].unsqueeze(1), P, NT, NE), ALU.add), tick)
                for i in range(NT):
                    ins = V.max(top[:, i, :], biased[:, i, :])
                own.link(ins, tick)
                for i in range(NT):
                    ins = V.match_replace(rest[:, i, :], top[:, i, :], biased[:, i, :], -BIG)
                own.link(ins)
                own.link(V.tensor_tensor(comb[:], rest[:, :, 0:NE], biased[:, :, 0:NE], ALU.is_lt))
                own.link(V.tensor_tensor(comb[:], comb[:], score[:], ALU.mult))
                own.link(V.tensor_reduce(csum[:, 0, :], comb[:], X, ALU.add))
                own.link(V.reciprocal(csum[:, 1, :], csum[:, 0, :]))
                own.link(V.tensor_tensor(comb[:], comb[:], bc(csum[:, 1, :].unsqueeze(2), P, NT, NE), ALU.mult))
                V.tensor_scalar(comb[:], comb[:], ROUTE_SCALE, None, ALU.mult).then_inc(sem["comb"], 1)
                ve.wait_ge(sem["comb_hi"], at(b, "comb_hi", 1))
                V.tensor_tensor(combT[32:32 + NE, :], bank[3][0:NE, :], combT[0:NE, :].bitcast(F32), ALU.subtract).then_inc(sem["comb_lo"], 1)

                def hidden(e):
                    ve.wait_ge(sem["silu"], at(b, "silu", e + 1))
                    ve.wait_ge(sem["up_ps"], at(b, "up_ps", e + 1))
                    if e >= 2:
                        ve.wait_ge(sem["h_hi"], at(b, "h_hi", e - 1))
                    if e < NE:
                        own.link(V.tensor_tensor(sg[:, e % 2, :], sg[:, e % 2, :], bank[2 + e % 2][:], ALU.mult))
                        ve.wait_ge(sem["c_ps"], at(b, "c_ps", e + 1))
                        V.tensor_tensor(hf[:, e % 2, :], sg[:, e % 2, :], bank[4 + e % 2][:], ALU.mult).then_inc(sem["h_f"], 1)
                    else:
                        V.tensor_tensor(hf[:, e % 2, :], sg[:, e % 2, :], bank[2 + e % 2][:], ALU.mult).then_inc(sem["h_f"], 1)

                def low(e):
                    ve.wait_ge(sem["h_hi"], at(b, "h_hi", e + 1))
                    V.tensor_tensor(hl[:, e % 2, :], hf[:, e % 2, :], hh[:, e % 2, :].bitcast(F32), ALU.subtract).then_inc(sem["h_lo"], 1)

                for e in range(NX + 1):
                    if e < NX:
                        hidden(e)
                    if e:
                        low(e - 1)
                ve.wait_ge(sem["y_tok"], at(b, "y_tok", 1))
                tok = lambda i: bank[i // 2][:, (i % 2) * D:(i % 2) * D + D]
                stats(tok, 2)
                for i in range(NT):
                    ins = V.tensor_scalar(xn[:, i, :], tok(i), mv[:, i, 0:1], rstd[:, i:i + 1], ALU.subtract, ALU.mult)
                own.link(ins)
                V.tensor_tensor(x_tok[:], x_tok[:], xn[:], ALU.add).then_inc(sem["x_final"], 1)
                own.end()

        @block.gpsimd
        def _(gp):
            gp.wait_ge(loaded, 16 * N_LOAD)
            with gp.Fori(0, B) as b:
                for k in range(2):
                    gp.wait_ge(sem["var"], at(b, "var", k + 1))
                    nc.gpsimd.tensor_tensor(rstd[:], vare[:], mhalf[:], ALU.pow).then_inc(sem["rstd"], 1)

        @block.scalar
        def _(sc):
            A = nc.scalar.activation
            for e in range(NX):
                sc.wait_ge(w_loaded[e % 2], 32 * (e // 2 + 1))
                A(w_hi[:, e, :], w_raw[:, e % 2, :], ACT.Copy).then_inc(w_hi_made, 1)
            with sc.Fori(0, B) as b:
                for k in range(NK):
                    sc.wait_ge(sem["turned"], at(b, "turned", k + 1))
                    A(xh[:, k, :], bank[k][:], ACT.Copy).then_inc(sem["x_hi"], 1)
                    A(xf[:, k, :], bank[k][:], ACT.Copy).then_inc(sem["x_f"], 1)
                sc.wait_ge(sem["route_ps"], at(b, "route_ps", 1))
                A(score[:].rearrange("p a e -> p (a e)"), bank[2][:, 0:NT * NE], ACT.Sigmoid).then_inc(sem["score"], 1)
                sc.wait_ge(sem["comb_ps"], at(b, "comb_ps", 1))
                A(combT[0:NE, :], bank[3][0:NE, :], ACT.Copy).then_inc(sem["comb_hi"], 1)

                def silu(e):
                    sc.wait_ge(sem["gate_ps"], at(b, "gate_ps", e + 1))
                    if e >= 2:
                        sc.wait_ge(sem["h_f"], at(b, "h_f", e - 1))
                    A(sg[:, e % 2, :], bank[e % 2][:], ACT.Silu).then_inc(sem["silu"], 1)

                def high(e):
                    sc.wait_ge(sem["h_f"], at(b, "h_f", e + 1))
                    if e >= 2:
                        sc.wait_ge(sem["y_acc"], at(b, "y_acc", e - 1))
                    A(hh[:, e % 2, :], hf[:, e % 2, :], ACT.Copy).then_inc(sem["h_hi"], 1)

                for e in range(NX + 1):
                    if e < NX:
                        silu(e)
                    if e:
                        high(e - 1)
                sc.wait_ge(sem["y_acc"], at(b, "y_acc", NX))
                for k in range(NK):
                    A(yT[:, k, :], bank[6 + k][:], ACT.Copy).then_inc(sem["y_sb"], 1)

        @block.tensor
        def _(pe):
            T = nc.tensor
            pe.wait_ge(const_ready, 1)
            pe.wait_ge(w_split, NX)
            with pe.Fori(0, B) as b:
                for i in range(NT):
                    pe.wait_ge(sem["normed"], at(b, "normed", i + 1))
                    for k in range(NK):
                        ins = T.transpose(bank[k][:, i * P:(i + 1) * P], xn[:, i, k * P:(k + 1) * P], ident[:])
                        if i == NT - 1:
                            ins.then_inc(sem["turned"], 1)
                pe.wait_ge(sem["x_f"], at(b, "x_f", NK))
                for i in range(NT):
                    for k in range(NK):
                        ins = T.matmul(bank[2][:, i * NE:(i + 1) * NE], xf[:, k, i * P:(i + 1) * P], gate_w[:, k, :],
                                       start=k == 0, stop=k == NK - 1)
                ins.then_inc(sem["route_ps"], 1)
                pe.wait_ge(sem["comb"], at(b, "comb", 1))
                for i in range(NT):
                    ins = T.transpose(bank[3][0:NE, i * P:(i + 1) * P], comb[:, i, :], ident[:])
                ins.then_inc(sem["comb_ps"], 1)
                pe.wait_ge(sem["comb_lo"], at(b, "comb_lo", 1))
                pe.wait_ge(sem["x_lo"], at(b, "x_lo", NK))

                def product(o, cols, e, hi, lo, first, last):
                    terms = ((w_hi, hi), (w_hi, lo), (w_lo, hi))
                    for c, (w, m) in enumerate(terms):
                        ins = T.matmul(o, w[:, e, cols:cols + P], m, start=first and c == 0, stop=last and c == 2)
                    return ins

                def gate_up(e):
                    if e >= 2:
                        pe.wait_ge(sem["silu"], at(b, "silu", e - 1))
                    for k in range(NK):
                        ins = product(bank[e % 2][:], k * 2 * INTER, e, xh[:, k, :], xl[:, k, :], k == 0, k == NK - 1)
                    ins.then_inc(sem["gate_ps"], 1)
                    if e >= 2:
                        pe.wait_ge(sem["h_f"], at(b, "h_f", e - 1))
                    for k in range(NK):
                        ins = product(bank[2 + e % 2][:], k * 2 * INTER + INTER, e, xh[:, k, :], xl[:, k, :], k == 0, k == NK - 1)
                    ins.then_inc(sem["up_ps"], 1)
                    if e < NE:
                        T.matmul(bank[4 + e % 2][:], sel_e[:, e, :], combT[:], start=True, stop=True).then_inc(sem["c_ps"], 1)

                def down(e):
                    pe.wait_ge(sem["h_lo"], at(b, "h_lo", e + 1))
                    for k in range(NK):
                        ins = product(bank[6 + k][:], W13 + k * P, e, hh[:, e % 2, :], hl[:, e % 2, :], e == 0, e == NX - 1)
                    ins.then_inc(sem["y_acc"], 1)

                for e in range(NX + 1):
                    if e < NX:
                        gate_up(e)
                    if e:
                        down(e - 1)
                pe.wait_ge(sem["y_sb"], at(b, "y_sb", NK))
                for i in range(NT):
                    for k in range(NK):
                        ins = T.transpose(bank[i // 2][:, (i % 2) * D + k * P:(i % 2) * D + (k + 1) * P],
                                          yT[:, k, i * P:(i + 1) * P], ident[:])
                ins.then_inc(sem["y_tok"], 1)


def constants():
    import numpy as np

    f = np.float32
    p = np.arange(P)
    c = {"c_ident": np.eye(P, dtype=f), "c_ones": np.ones((P, P), f)}
    block = (p[:, None] // HD == p[None, :] // HD).astype(f)
    c["c_blockones"] = block
    c["c_selo"] = np.stack([block * (p[None, :] % HD == j) for j in range(HD)], 1).astype(f)
    c["c_selv"] = np.stack([block * (p[:, None] % HD == j) for j in range(HD)], 1).reshape(P, HD * P).astype(f)
    sel = np.zeros((P, PAIRS, 4, P), f)
    quarters = ((0, 1), (2, 3), (0, 2), (1, 3))
    for j in range(PAIRS):
        for c4, qs in enumerate(quarters):
            for q in qs:
                r = np.arange(32)
                sel[32 * j + r, j, c4, 32 * q + r] = 1
    c["c_selqk"] = sel.reshape(P, -1)
    c["c_parmask"] = np.stack([(p % 32 // HD == par) for par in range(2)], 1).astype(f)
    c["c_lhmask"] = (np.arange(LD)[:, None] // 16 == np.arange(LH)[None, :]).astype(f)
    i, k = p[:, None], p[None, :]
    prev = (k >= i) & ~((i == 0) & (k == 0))
    own = k < i
    m = np.where(np.concatenate([prev, own], 1), 0, NEG).astype(f)
    c["c_wmask"] = np.stack([m, m], 1).reshape(P, 512)
    tok = np.arange(NT)[None, :, None] * P + p[:, None, None]
    lm = np.where(np.arange(NLAT)[None, None, :] < tok // CHUNK, 0, NEG).astype(f)
    c["c_lmask"] = np.repeat(lm[:, :, None, :], LH, 2).reshape(P, -1)
    c["c_rowloc"] = np.repeat(tok > 0, H, 2).astype(f)
    c["c_rowlat"] = np.repeat(tok >= CHUNK, LH, 2).astype(f)
    c["c_mhalf"] = np.full((P, 64), -0.5, f)
    se = np.zeros((64, NE, P), f)
    for e in range(NE):
        se[e, e] = se[32 + e, e] = 1
    c["c_sele"] = se.reshape(64, -1)
    return c


def kernel(**inputs):
    import numpy as np
    import concourse.bacc as _bacc
    from concourse.bass_utils import run_bass_kernel_spmd as _run

    a = {k: np.asarray(v) for k, v in inputs.items()}
    col = lambda v: v.reshape(-1, P).T
    t = constants()
    t["x"] = a["L0_attn_x"]
    t["wqkv"] = a["L0_attn_qkv_w"]
    t["qkb"] = col(a["L0_attn_qkv_b"][:2 * D])
    t["vb"] = a["L0_attn_qkv_b"][2 * D:]
    t["wrq"] = a["L0_attn_rq_w"]
    t["rqb"] = a["L0_attn_rq_b"].reshape(LD, 1)
    t["wrkv"] = a["L0_attn_rkv_w"]
    t["rkb"] = a["L0_attn_rkv_b"][:LD].reshape(LD, 1)
    t["rvb"] = a["L0_attn_rkv_b"][LD:]
    t["wrout"], t["routb"] = a["L0_attn_rout_w"], a["L0_attn_rout_b"]
    t["wout"], t["outb"] = a["L0_attn_out_w"], a["L0_attn_out_b"]
    t["gl"], t["gr"] = a["L0_attn_gl_w"][:, 0], a["L0_attn_gr_w"][:, 0]
    t["w1"], t["w2"] = a["L0_ffn_W1"].T, a["L0_ffn_W2"].T
    t["b1"], t["b2"] = col(a["L0_ffn_b1"]), col(a["L0_ffn_b2"])
    t["wrk"] = np.stack([a["L1_attn_W_" + n].T for n in "vkwro"])
    t["tm"] = np.stack([col(a["L1_attn_tm_" + n]) for n in "vkwr"], 1)
    t["u"] = col(a["L1_attn_u"].reshape(-1))
    t["lnwb"] = np.stack([np.tile(a["L1_attn_ln_w"], 8), np.tile(a["L1_attn_ln_b"], 8)], 1)
    t["gate_w"], t["gate_b"] = a["L1_ffn_gate_w"].T, a["L1_ffn_gate_b"]
    t["w13"] = np.concatenate([a["L1_ffn_w13"], a["L1_ffn_w13_s"][None]]).transpose(0, 2, 1)
    t["w2e"] = np.concatenate([a["L1_ffn_w2"], a["L1_ffn_w2_s"][None]]).transpose(0, 2, 1)

    nc = _bacc.Bacc("TRN2", target_bir_lowering=False, num_devices=1)
    arrays, aps = {}, {}
    for name, v in t.items():
        v = np.ascontiguousarray(v)
        arrays[f"in_{name}"] = v
        aps[name] = nc.dram_tensor(f"in_{name}", v.shape, mybir.dt.from_np(v.dtype), kind="ExternalInput").ap()
    out = nc.dram_tensor("out_0", (B, S, D), F32, kind="ExternalOutput").ap()
    program(nc, aps, out)
    r = _run(nc, [arrays], core_ids=[0])
    return r.results[0]["out_0"]
```

```python
from contextlib import ExitStack

import concourse.bass as bass
from concourse import mybir

F32 = mybir.dt.float32
F32R = mybir.dt.float32r
BF16 = mybir.dt.bfloat16
ALU = mybir.AluOpType
ACT = mybir.ActivationFunctionType
X = mybir.AxisListType.X

P = 128
B, S, D = 8, 512, 256
NT, NK = S // P, D // P
H, HD = 16, 16
LH, LD, NLAT = 4, 64, 64
CHUNK = S // NLAT
FF = 1024
NF = FF // P
NE, TOPK, INTER = 16, 4, 128
ROUTE_SCALE = 2.5
EPS = 1e-5
NEG = -1e30
BIG = 3e38
NPAIR = H // 2
PAIRS = 4
NLN = 6

PER = dict(
    x_in=16, x_out=16, var=NLN, rstd=NLN, normed=3 * NT, turned=NK * 3, evened=NK * 3,
    pooled=1, q_ps=2, k_ps=2, v_ps=2, rq_ps=1, rkv_ps=1, qk_hi=4, qk_lo=4, v_sb=1, rq_sb=1, rk_sb=1,
    lat_ps=1, lat_sub=2, lat_exp=2, lat_turned=NT, lat_probs=NT, lat_out=1, lat_normed=1, lat_nt=1, lat_nt_sb=1,
    remote_ps=1, remote=1, remote_gr=1,
    stack_q=NPAIR, stack_k=NPAIR, stq_sb=NPAIR, stk_sb=NPAIR, scores=NPAIR * NT, negmax=NPAIR * NT,
    probs=NPAIR * NT, p_turned=NPAIR * NT, p_even=NPAIR * NT // 2, p_odd=NPAIR * NT // 2, local_ps=NPAIR, local_raw=NPAIR,
    loc=1, diff=1, gate_z=1, gate_e=1, mixed=1, mixed_t=2, mixed_sb=2, out_ps=1,
    f_lo=1, h_ps=NF, gelu=NF, g_hi=NF, g_lo=NF, f_y=NF, fy_sb=2, fy_tok=1,
    mix=8, proj=8, v_hi=2, v_lo=1, v_f=2, k_f=2, ek=2, dec=2, decay=1, r_f=2, rb=1, bonus_ps=1, v_bc=2 * HD, kv=2 * HD,
    state=2 * HD, rs=2 * HD, summed=2 * HD, o_sb=1, o_tok=1, o_diff=1, o_sq=1, o_var=1, o_rstd=1, o_norm=1, o_back=1,
    o_aff=2, y_in=1, w_ps=1, x_final=1,
)


def program(nc, t, out):
    x3 = nc.dram_tensor("x_after_rwkv", (B, S, D), F32, kind="Internal").ap()
    mid_token_layers(nc, t, x3)
    expert_layer(nc, t, x3, out)


class Own:

    def __init__(self, eng, sem, per):
        self.eng, self.sem, self.per, self.n, self.base = eng, sem, per, 0, 0

    def start(self, b):
        self.base, self.n = b * self.per, 0

    def link(self, ins, tick=None):
        self.n += 1
        ins.then_inc(self.sem, 1)
        self.eng.wait_ge(self.sem, self.base + self.n)
        if tick is not None:
            self.eng.memset(tick, 0.0)

    def end(self):
        assert self.n == self.per, f"{self.n} links in a batch, not {self.per}"


VEC_OWN = 46
VEC_OWN_2 = 29


def mid_token_layers(nc, t, x3):
    with ExitStack() as ctx:
        def sb(name, shape, dt=F32):
            return ctx.enter_context(nc.sbuf_tensor(name, shape, dt))

        bank = [ctx.enter_context(nc.psum_tensor(f"bank{i}", [P, 512], F32)) for i in range(8)]
        sem = {n: ctx.enter_context(nc.semaphore(n)) for n in PER}
        vec_own = ctx.enter_context(nc.semaphore("vec_own"))
        loaded = ctx.enter_context(nc.semaphore("loaded"))
        const_ready = ctx.enter_context(nc.semaphore("const_ready"))
        tern_sum = ctx.enter_context(nc.semaphore("tern_sum"))
        tern_tot = ctx.enter_context(nc.semaphore("tern_tot"))
        setup_own = ctx.enter_context(nc.semaphore("setup_own"))
        s_zero = ctx.enter_context(nc.semaphore("s_zero"))

        ident = sb("ident", [P, P])
        ident_b = sb("ident_b", [P, P], BF16)
        blockones = sb("blockones", [P, P])
        sel_o = sb("sel_o", [P, HD, P])
        sel_v = sb("sel_v", [P, HD, P], F32R)
        sel_qk = sb("sel_qk", [P, PAIRS, 4, P], F32R)
        parmask = sb("parmask", [P, 2])
        lhmask = sb("lhmask", [LD, LH])
        lmask = sb("lmask", [P, NT, LH * NLAT], BF16)
        wmask = sb("wmask", [P, 2, 2 * P], BF16)
        row_loc = sb("row_loc", [P, NT, H])
        row_lat = sb("row_lat", [P, NT, LH])
        wqkv = sb("wqkv", [P, NK, 3 * D])
        qkb = sb("qkb", [P, 4])
        wrq = sb("wrq", [P, NK, LD])
        rqb = sb("rqb", [LD, 1])
        wrkv = sb("wrkv", [P, NK, 2 * LD])
        rkb = sb("rkb", [LD, 1])
        rvb = sb("rvb", [LD, LD])
        wrout = sb("wrout", [LD, D])
        wout = sb("wout", [P, NK, D])
        vb = sb("vb", [P, D])
        routb = sb("routb", [P, D])
        outb = sb("outb", [P, D])
        glr = sb("glr", [P, 2, HD])
        w1t = sb("w1t", [P, NK, FF], F32R)
        w2t = sb("w2t", [P, NF, D], F32R)
        b1 = sb("b1", [P, NF])
        b2 = sb("b2", [P, NK])
        wrk = sb("wrk", [P, 5, NK, D])
        tm = sb("tm", [P, 4, NK])
        u_c = sb("u_c", [P, NK])
        lnwb = sb("lnwb", [P, 2])
        mhalf = sb("mhalf", [P, 64])
        tick = sb("tick", [P, 1])[:]

        x_tok = sb("x_tok", [P, NT, D])
        xn = sb("xn", [P, NT, D])
        xT = sb("xT", [P, NK, S + 2])
        st = sb("st", [P, NT, 6])
        mv = sb("mv", [P, NT, 2])
        vare = sb("vare", [P, NT])
        rstd = sb("rstd", [P, NT])
        hiT = sb("hiT", [P, 4, S], F32R)
        loT = sb("loT", [P, 4, S], F32R)
        work = sb("work", [P, 12, S])
        stq = sb("stq", [P, 2, S], F32R)
        stk = sb("stk", [P, 2, 2, S], F32R)
        rsum = sb("rsum", [P, NT, H])
        rinv = sb("rinv", [P, NT, H])
        nmx = sb("nmx", [P, NPAIR * NT, 2])
        small = sb("small", [P, 6, 64])
        pt = sb("pt", [P, 2, 512])
        probs = sb("probs", [P, 4, 512])
        s_buf = sb("s_buf", [P, 2, S + 2])
        ones = sb("ones", [P, P])
        v_tok = sb("v_tok", [P, NT, D])
        poolx = sb("poolx", [P, 2, NK, NLAT])
        rk_bd = sb("rk_bd", [LD, LH, NLAT])
        rv_sb = sb("rv_sb", [LD, LD])

        def at(b, name, k):
            return b * PER[name] + k

        raw = work[:, :, :].rearrange("p a s -> p (a s)")
        n_load = [0]

        block = ctx.enter_context(nc.Block())

        def bc(ap, *shape):
            return ap.broadcast_to(shape)

        @block.sync
        def _(sp):
            def load(dst, src):
                n_load[0] += 1
                sp.dma_start(dst, src).then_inc(loaded, 16)
            load(ident[:], t["c_ident"])
            load(blockones[:], t["c_blockones"])
            load(sel_o[:], t["c_selo"])
            load(ones[:], t["c_ones"])
            load(parmask[:], t["c_parmask"])
            load(lhmask[:], t["c_lhmask"])
            load(row_loc[:], t["c_rowloc"])
            load(row_lat[:], t["c_rowlat"])
            load(mhalf[:], t["c_mhalf"])
            load(wqkv[:], t["wqkv"].rearrange("(k p) n -> p k n", p=P))
            load(qkb[:], t["qkb"])
            load(wrq[:], t["wrq"].rearrange("(k p) n -> p k n", p=P))
            load(rqb[:], t["rqb"])
            load(wrkv[:], t["wrkv"].rearrange("(k p) n -> p k n", p=P))
            load(rkb[:], t["rkb"])
            load(rvb[:], t["rvb"].partition_broadcast(LD))
            load(wrout[:], t["wrout"])
            load(wout[:], t["wout"].rearrange("(k p) n -> p k n", p=P))
            load(vb[:], t["vb"].partition_broadcast(P))
            load(routb[:], t["routb"].partition_broadcast(P))
            load(outb[:], t["outb"].partition_broadcast(P))
            load(glr[:, 0, :], t["gl"].partition_broadcast(P))
            load(glr[:, 1, :], t["gr"].partition_broadcast(P))
            load(b1[:], t["b1"])
            load(b2[:], t["b2"])
            load(wrk[:], t["wrk"].rearrange("w (k p) n -> p w k n", p=P))
            load(tm[:], t["tm"])
            load(u_c[:], t["u"])
            load(lnwb[:], t["lnwb"])
            load(raw[:, 0:2048], t["w1"].rearrange("(k p) n -> p k n", p=P))
            load(raw[:, 2048:4096], t["w2"].rearrange("(k p) n -> p k n", p=P))
            load(raw[:, 4096:6144], t["c_selv"])
            load(xT[:, 0, 0:512], t["c_wmask"])
            load(x_tok[:].rearrange("p a d -> p (a d)"), t["c_lmask"])
            load(probs[:].rearrange("p a d -> p (a d)"), t["c_selqk"])
            rows = lambda ap: ap.rearrange("o (t p) d -> p (o t) d", p=P)
            sp.wait_ge(const_ready, 1)
            sp.dma_start(x_tok[:], rows(t["x"][0:1])).then_inc(sem["x_in"], 16)
            with sp.Fori(0, B - 1) as b:
                sp.wait_ge(sem["x_final"], at(b, "x_final", 1))
                sp.dma_start(rows(x3[bass.ds(b, 1)]), x_tok[:]).then_inc(sem["x_out"], 16)
                sp.wait_ge(sem["x_out"], at(b, "x_out", 16))
                sp.dma_start(x_tok[:], rows(t["x"][bass.ds(b + 1, 1)])).then_inc(sem["x_in"], 16)
            sp.wait_ge(sem["x_final"], B)
            sp.dma_start(rows(x3[B - 1:B]), x_tok[:]).then_inc(sem["x_out"], 16)
            sp.wait_ge(sem["x_out"], B * 16)

        @block.vector
        def _(ve):
            V = nc.vector
            own = Own(ve, setup_own, 0)
            ve.wait_ge(loaded, 16 * n_load[0])
            V.tensor_copy(ident_b[:], ident[:])
            V.tensor_copy(sel_v[:].rearrange("p a m -> p (a m)"), raw[:, 4096:6144])
            V.tensor_copy(wmask[:].rearrange("p a m -> p (a m)"), xT[:, 0, 0:512])
            V.tensor_copy(lmask[:].rearrange("p a m -> p (a m)"), x_tok[:].rearrange("p a d -> p (a d)"))
            V.tensor_copy(sel_qk[:].rearrange("p a c m -> p (a c m)"), probs[:].rearrange("p a d -> p (a d)"))
            V.tensor_scalar(qkb[:, 0:2], qkb[:, 0:2], 0.25, None, ALU.mult)
            V.tensor_scalar(wqkv[:, :, 0:D], wqkv[:, :, 0:D], 0.25, None, ALU.mult)
            for i in range(2):
                V.tensor_reduce(small[:, i, 0:1], raw[:, 2048 * i:2048 * i + 2048], X, ALU.add,
                                apply_absolute_value=True).then_inc(tern_sum, 1)
            ve.wait_ge(tern_tot, 1)
            for i in range(2):
                own.link(V.tensor_scalar(small[:, i, 1:2], bank[0][:, i:i + 1], 1.0 / (FF * D), 1e-8, ALU.mult, ALU.max))
                own.link(V.tensor_scalar(small[:, i, 2:3], small[:, i, 1:2], 0.5, None, ALU.mult))
                own.link(V.tensor_scalar(small[:, i, 3:4], small[:, i, 1:2], -0.5, None, ALU.mult))
                w = raw[:, 2048 * i:2048 * i + 2048]
                neg = hiT[:].rearrange("p a s -> p (a s)")
                dst = (w1t, w2t)[i][:].rearrange("p a s -> p (a s)")
                own.link(V.tensor_scalar(neg, w, small[:, i, 3:4], None, ALU.is_lt))
                own.link(V.scalar_tensor_tensor(dst, w, small[:, i, 2:3], neg.bitcast(F32), ALU.is_gt, ALU.subtract))
            V.memset(xT[:, :, 0:1], 0.0).then_inc(const_ready, 1)

            own = Own(ve, vec_own, VEC_OWN)
            with ve.Fori(0, B) as b:
                own.start(b)
                ln = [0]

                def stats(src):
                    for i in range(NT):
                        ins = V.bn_stats(st[:, i, :], src(i))
                    own.link(ins, tick)
                    for i in range(NT):
                        ins = V.bn_aggr(mv[:, i, :], st[:, i, :])
                    own.link(ins)
                    V.tensor_scalar(vare[:], mv[:, :, 1], EPS, None, ALU.add).then_inc(sem["var"], 1)
                    ln[0] += 1
                    ve.wait_ge(sem["rstd"], at(b, "rstd", ln[0]))

                def pre_norm():
                    stats(lambda i: x_tok[:, i, :])
                    for i in range(NT):
                        V.tensor_scalar(xn[:, i, :], x_tok[:, i, :], mv[:, i, 0:1], rstd[:, i:i + 1],
                                        ALU.subtract, ALU.mult).then_inc(sem["normed"], 1)

                def residual(src, last=False):
                    stats(src)
                    for i in range(NT):
                        ins = V.tensor_scalar(xn[:, i, :], src(i), mv[:, i, 0:1], rstd[:, i:i + 1],
                                              ALU.subtract, ALU.mult)
                    own.link(ins)
                    ins = V.tensor_tensor(x_tok[:], x_tok[:], xn[:], ALU.add)
                    if last:
                        ins.then_inc(sem["x_final"], 1)
                    else:
                        own.link(ins)

                ve.wait_ge(sem["x_in"], at(b, "x_in", 16))
                pre_norm()
                ve.wait_ge(sem["evened"], at(b, "evened", 2))
                own.link(V.tensor_reduce(poolx[:, 0], xT[:, :, 1:S + 1].rearrange("p k (l c) -> p k l c", c=CHUNK), X, ALU.add))
                V.tensor_scalar(poolx[:, 1], poolx[:, 0], 1.0 / CHUNK, None, ALU.mult).then_inc(sem["pooled"], 1)
                for i in range(4):
                    ve.wait_ge(sem["qk_hi"], at(b, "qk_hi", i + 1))
                    V.scalar_tensor_tensor(loT[:, i, :], bank[2 + i][:], qkb[:, i:i + 1], hiT[:, i, :].bitcast(F32),
                                           ALU.add, ALU.subtract).then_inc(sem["qk_lo"], 1)
                ve.wait_ge(sem["v_ps"], at(b, "v_ps", 2))
                for i in range(2):
                    ins = V.tensor_tensor(v_tok[:, 2 * i:2 * i + 2, :], bank[6 + i][:].rearrange("p (a d) -> p a d", a=2),
                                          bc(vb[:].unsqueeze(1), P, 2, D), ALU.add)
                ins.then_inc(sem["v_sb"], 1)
                ve.wait_ge(sem["rkv_ps"], at(b, "rkv_ps", 1))
                for h in range(LH):
                    V.tensor_scalar(rk_bd[:, h, :], bank[1][0:LD, 0:NLAT], rkb[:, 0:1], lhmask[:, h:h + 1], ALU.add, ALU.mult)
                V.tensor_tensor(rv_sb[:], bank[1][0:NLAT, NLAT:NLAT + LD], rvb[:], ALU.add).then_inc(sem["rk_sb"], 1)

                lsub = work[:, 0:2, :]
                lexp = work[:, 2:4, :]
                ve.wait_ge(sem["lat_ps"], at(b, "lat_ps", 1))
                for i in range(2):
                    ps = bank[2 + i][:].rearrange("p (a l) -> p a l", l=NLAT)
                    own.link(V.tensor_reduce(small[:, 0, 8 * i:8 * i + 8], ps, X, ALU.max))
                    V.tensor_tensor(lsub[:, i, :].rearrange("p (a l) -> p a l", l=NLAT), ps,
                                    bc(small[:, 0, 8 * i:8 * i + 8].unsqueeze(2), P, 8, NLAT), ALU.subtract
                                    ).then_inc(sem["lat_sub"], 1)
                ve.wait_ge(sem["lat_exp"], at(b, "lat_exp", 2))
                own.link(V.tensor_reduce(small[:, 1, 0:16], lexp.rearrange("p a (h l) -> p (a h) l", l=NLAT), X, ALU.add))
                own.link(V.reciprocal(small[:, 2, 0:16], small[:, 1, 0:16]))
                own.link(V.tensor_tensor(small[:, 3, 0:16], small[:, 2, 0:16], row_lat[:].rearrange("p a h -> p (a h)"), ALU.mult))
                lat_n = work[:, 4, 0:256]
                ve.wait_ge(sem["lat_out"], at(b, "lat_out", 1))
                V.tensor_tensor(lat_n.rearrange("p (a d) -> p a d", d=16), bank[0][:, 0:256].rearrange("p (a d) -> p a d", d=16),
                                bc(small[:, 3, 0:16].unsqueeze(2), P, 16, 16), ALU.mult).then_inc(sem["lat_normed"], 1)
                rem = work[:, 6:8, :]
                ve.wait_ge(sem["remote_ps"], at(b, "remote_ps", 1))
                for i in range(2):
                    ins = V.tensor_tensor(rem[:, i, :].rearrange("p (a d) -> p a d", a=2), bank[2 + i][:].rearrange("p (a d) -> p a d", a=2),
                                          bc(routb[:].unsqueeze(1), P, 2, D), ALU.add)
                ins.then_inc(sem["remote"], 1)

                def stack_k(p):
                    ve.wait_ge(sem["stack_k"], at(b, "stack_k", p + 1))
                    for par in range(2):
                        ins = V.tensor_scalar(stk[:, p % 2, par, :], bank[0][:], parmask[:, par:par + 1], None, ALU.mult)
                    ins.then_inc(sem["stk_sb"], 1)

                def negmax(p, i):
                    n = NT * p + i
                    w = P if i == 0 else 2 * P
                    ve.wait_ge(sem["scores"], at(b, "scores", n + 1))
                    V.tensor_reduce(nmx[:, n, :], bank[2 + i][:, 0:2 * w].rearrange("p (h k) -> p h k", h=2), X, ALU.max,
                                    negate=True).then_inc(sem["negmax"], 1)

                def turn_even(p, i):
                    n = NT * p + i
                    w = 256 if i == 0 else 512
                    ve.wait_ge(sem["p_turned"], at(b, "p_turned", n + 1))
                    V.tensor_copy(pt[:, 0, 0:w], bank[6][:, 0:w]).then_inc(sem["p_even"], 1)

                loc_raw = work[:, 8:10, :]

                def local_raw(p):
                    ve.wait_ge(sem["local_ps"], at(b, "local_ps", p + 1))
                    V.tensor_copy(loc_raw.rearrange("p a (c d) -> p (a c) d", d=D)[:, :, 32 * p:32 * p + 32],
                                  bank[7][:, 128 * (p % 2):128 * (p % 2) + 128].rearrange("p (a d) -> p a d", d=32)
                                  ).then_inc(sem["local_raw"], 1)

                stack_k(0)
                for i in range(NT):
                    negmax(0, i)
                stack_k(1)
                for p in range(NPAIR):
                    for i in range(NT):
                        if i % 2 == 0:
                            turn_even(p, i)
                        if p + 1 < NPAIR:
                            negmax(p + 1, i)
                    if p + 2 < NPAIR:
                        stack_k(p + 2)
                    local_raw(p)
                ve.wait_ge(sem["probs"], at(b, "probs", NPAIR * NT))
                own.link(V.reciprocal(rinv[:], rsum[:]))
                own.link(V.tensor_tensor(rinv[:], rinv[:], row_loc[:], ALU.mult))
                loc = work[:, 0:2, :]
                v4 = lambda a: a.rearrange("p a (h d) -> p (a h) d", d=HD)
                own.link(V.tensor_tensor(v4(loc), v4(loc_raw), bc(rinv[:].rearrange("p a h -> p (a h)").unsqueeze(2), P, 64, HD), ALU.mult))
                c1 = work[:, 2:4, :]
                V.tensor_tensor(v4(c1), v4(loc), bc(glr[:, 0, :].unsqueeze(1), P, 64, HD), ALU.mult).then_inc(sem["loc"], 1)
                ve.wait_ge(sem["loc"], at(b, "loc", 1))
                ve.wait_ge(sem["remote_gr"], at(b, "remote_gr", 1))
                own.link(V.tensor_tensor(c1, c1, work[:, 10:12, :], ALU.add))
                V.tensor_reduce(small[:, 4, :], v4(c1), X, ALU.add).then_inc(sem["gate_z"], 1)
                ve.wait_ge(sem["gate_e"], at(b, "gate_e", 1))
                own.link(V.tensor_scalar(small[:, 5, :], small[:, 5, :], 1.0, None, ALU.add))
                own.link(V.reciprocal(small[:, 5, :], small[:, 5, :]))
                ve.wait_ge(sem["diff"], at(b, "diff", 1))
                own.link(V.tensor_tensor(v4(c1), v4(work[:, 4:6, :]), bc(small[:, 5, :].unsqueeze(2), P, 64, HD), ALU.mult))
                V.tensor_tensor(c1, c1, rem, ALU.add).then_inc(sem["mixed"], 1)
                ve.wait_ge(sem["out_ps"], at(b, "out_ps", 1))
                y_tok = work[:, 0:2, :].rearrange("p a (c d) -> p (a c) d", d=D)
                for i in range(2):
                    ins = V.tensor_tensor(y_tok[:, 2 * i:2 * i + 2, :], bank[2 + i][:].rearrange("p (a d) -> p a d", a=2),
                                          bc(outb[:].unsqueeze(1), P, 2, D), ALU.add)
                own.link(ins)
                residual(lambda i: y_tok[:, i, :])

                pre_norm()
                ve.wait_ge(sem["evened"], at(b, "evened", 4))
                for k in range(NK):
                    ins = V.tensor_tensor(loT[:, k, :], bank[k][:], hiT[:, k, :].bitcast(F32), ALU.subtract)
                ins.then_inc(sem["f_lo"], 1)
                for f in range(NF):
                    ve.wait_ge(sem["gelu"], at(b, "gelu", f + 1))
                    if f >= 2:
                        ve.wait_ge(sem["f_y"], at(b, "f_y", f - 1))
                    own.link(V.tensor_copy(stq[:, f % 2, :], work[:, f % 2, :]))
                    V.tensor_tensor(stk[:, 0, f % 2, :], work[:, f % 2, :], stq[:, f % 2, :].bitcast(F32), ALU.subtract
                                    ).then_inc(sem["g_lo"], 1)
                tok = lambda i: bank[2 + i // 2][:, (i % 2) * D:(i % 2) * D + D]
                ve.wait_ge(sem["fy_tok"], at(b, "fy_tok", 1))
                residual(tok)

                pre_norm()
                ve.wait_ge(sem["evened"], at(b, "evened", 6))
                dx = work[:, 0:2, :]
                own.link(V.tensor_tensor(dx, xT[:, :, 1:S + 1], xT[:, :, 0:S], ALU.subtract))
                for w in range(4):
                    for k in range(NK):
                        V.scalar_tensor_tensor(work[:, 2 + 2 * w + k, :], dx[:, k, :], tm[:, w, k:k + 1], xT[:, k, 0:S],
                                               ALU.mult, ALU.add).then_inc(sem["mix"], 1)
                v_hi, v_lo = hiT[:, 0:2, :], loT[:, 0:2, :]
                for g in range(2):
                    ve.wait_ge(sem["v_f"], at(b, "v_f", g + 1))
                    ins = V.tensor_tensor(v_lo[:, g, :], work[:, g, :], v_hi[:, g, :].bitcast(F32), ALU.subtract)
                ins.then_inc(sem["v_lo"], 1)
                vf, kf, ek, dec, rf = (work[:, i:i + 2, :] for i in (0, 2, 4, 6, 8))
                ve.wait_ge(sem["dec"], at(b, "dec", 2))
                own.link(V.tensor_scalar(dec, dec, 0.9999000049998333, None, ALU.mult))
                ve.wait_ge(sem["r_f"], at(b, "r_f", 2))
                V.tensor_tensor(work[:, 10:12, :], rf, ek, ALU.mult).then_inc(sem["rb"], 1)
                kvb, sbuf = pt, probs

                def kv(n):
                    ve.wait_ge(sem["v_bc"], at(b, "v_bc", n + 1))
                    if n >= 2:
                        ve.wait_ge(sem["state"], at(b, "state", n - 1))
                    V.tensor_tensor(kvb[:, n % 2, :], kf[:, n // HD, :], bank[2 + n % 3][:], ALU.mult).then_inc(sem["kv"], 1)

                kv(0)
                for n in range(2 * HD):
                    if n + 1 < 2 * HD:
                        kv(n + 1)
                    ve.wait_ge(sem["kv"], at(b, "kv", n + 1))
                    if n >= 2:
                        ve.wait_ge(sem["rs"], at(b, "rs", n - 1))
                    V.tensor_tensor_scan(s_buf[:, n % 2, 1:S + 1], dec[:, n // HD, :], kvb[:, n % 2, :], 0.0, ALU.mult, ALU.add
                                         ).then_inc(sem["state"], 1)
                ve.wait_ge(sem["bonus_ps"], at(b, "bonus_ps", 1))
                o_f = work[:, 2:4, :]
                for g in range(2):
                    own.link(V.tensor_tensor(o_f[:, g, :], vf[:, g, :], bank[g][:], ALU.mult))
                ve.wait_ge(sem["summed"], at(b, "summed", 2 * HD))
                for g in range(2):
                    ins = V.tensor_tensor(o_f[:, g, :], o_f[:, g, :], bank[6 + g][:], ALU.add)
                ins.then_inc(sem["o_sb"], 1)
                ve.wait_ge(sem["o_tok"], at(b, "o_tok", 1))
                od, osq = work[:, 4:6, :], work[:, 6:8, :]
                for i in range(2):
                    ins = V.tensor_reduce(small[:, 0, 32 * i:32 * i + 32], bank[i][:].rearrange("p (a d) -> p a d", d=HD), X, ALU.add)
                own.link(ins)
                own.link(V.tensor_scalar(small[:, 1, :], small[:, 0, :], 1.0 / HD, None, ALU.mult))
                for i in range(2):
                    ins = V.tensor_tensor(od[:, i, :].rearrange("p (a d) -> p a d", d=HD), bank[i][:].rearrange("p (a d) -> p a d", d=HD),
                                          bc(small[:, 1, 32 * i:32 * i + 32].unsqueeze(2), P, 32, HD), ALU.subtract)
                ins.then_inc(sem["o_diff"], 1)
                ve.wait_ge(sem["o_sq"], at(b, "o_sq", 1))
                own.link(V.tensor_reduce(small[:, 2, :], v4(osq), X, ALU.add))
                V.tensor_scalar(small[:, 3, :], small[:, 2, :], 1.0 / HD, EPS, ALU.mult, ALU.add).then_inc(sem["o_var"], 1)
                ve.wait_ge(sem["o_rstd"], at(b, "o_rstd", 1))
                V.tensor_tensor(v4(osq), v4(od), bc(small[:, 4, :].unsqueeze(2), P, 64, HD), ALU.mult).then_inc(sem["o_norm"], 1)
                ve.wait_ge(sem["o_aff"], at(b, "o_aff", 2))
                V.tensor_tensor(work[:, 4:6, :], work[:, 2:4, :], rf, ALU.mult).then_inc(sem["y_in"], 1)
                ve.wait_ge(sem["w_ps"], at(b, "w_ps", 1))
                residual(lambda i: bank[4 + i // 2][:, (i % 2) * D:(i % 2) * D + D], last=True)
                own.end()

        @block.gpsimd
        def _(gp):
            G = nc.gpsimd
            G.memset(s_buf[:, :, 0:1], 0.0).then_inc(s_zero, 1)
            gp.wait_ge(const_ready, 1)
            with gp.Fori(0, B) as b:
                def pow_(k):
                    gp.wait_ge(sem["var"], at(b, "var", k + 1))
                    G.tensor_tensor(rstd[:], vare[:], mhalf[:, 0:NT], ALU.pow).then_inc(sem["rstd"], 1)

                pow_(0)
                gp.wait_ge(sem["remote"], at(b, "remote", 1))
                v4 = lambda a: a.rearrange("p a (h d) -> p (a h) d", d=HD)
                G.tensor_tensor(v4(work[:, 10:12, :]), v4(work[:, 6:8, :]), bc(glr[:, 1, :].unsqueeze(1), P, 64, HD), ALU.mult
                                ).then_inc(sem["remote_gr"], 1)
                gp.wait_ge(sem["loc"], at(b, "loc", 1))
                G.tensor_tensor(work[:, 4:6, :], work[:, 0:2, :], work[:, 6:8, :], ALU.subtract).then_inc(sem["diff"], 1)
                for k in range(1, NLN):
                    if k == NLN - 1:
                        gp.wait_ge(s_zero, 1)
                        rf = work[:, 8:10, :]
                        for n in range(2 * HD):
                            gp.wait_ge(sem["state"], at(b, "state", n + 1))
                            if n == 0:
                                gp.wait_ge(sem["r_f"], at(b, "r_f", 2))
                            if n >= 2:
                                gp.wait_ge(sem["summed"], at(b, "summed", n - 1))
                            G.tensor_tensor(probs[:, n % 2, :], s_buf[:, n % 2, 0:S], rf[:, n // HD, :], ALU.mult
                                            ).then_inc(sem["rs"], 1)
                        gp.wait_ge(sem["o_var"], at(b, "o_var", 1))
                        G.tensor_tensor(small[:, 4, :], small[:, 3, :], mhalf[:], ALU.pow).then_inc(sem["o_rstd"], 1)
                    pow_(k)

        @block.scalar
        def _(sc):
            A = nc.scalar.activation
            sc.wait_ge(const_ready, 1)
            with sc.Fori(0, B) as b:
                for k in range(NK):
                    sc.wait_ge(sem["turned"], at(b, "turned", k + 1))
                    A(xT[:, k, 1:S + 1], bank[k][:], ACT.Copy).then_inc(sem["evened"], 1)
                for i in range(4):
                    sc.wait_ge(sem["q_ps" if i < 2 else "k_ps"], at(b, "q_ps", i % 2 + 1))
                    A(hiT[:, i, :], bank[2 + i][:], ACT.Identity, bias=qkb[:, i:i + 1]).then_inc(sem["qk_hi"], 1)
                sc.wait_ge(sem["rq_ps"], at(b, "rq_ps", 1))
                rqT = work[0:LD, 5, :]
                A(rqT, bank[0][0:LD, :], ACT.Identity, bias=rqb[:, 0:1]).then_inc(sem["rq_sb"], 1)
                for i in range(2):
                    sc.wait_ge(sem["lat_sub"], at(b, "lat_sub", i + 1))
                    A(work[:, 2 + i, :], work[:, i, :], ACT.Exp, scale=0.25).then_inc(sem["lat_exp"], 1)
                for i in range(NT):
                    sc.wait_ge(sem["lat_turned"], at(b, "lat_turned", i + 1))
                    A(work[0:NLAT, 8 + i, :], bank[4 + i][0:NLAT, :], ACT.Copy).then_inc(sem["lat_probs"], 1)
                sc.wait_ge(sem["lat_nt"], at(b, "lat_nt", 1))
                A(work[0:LD, 5, :], bank[1][0:LD, :], ACT.Copy).then_inc(sem["lat_nt_sb"], 1)

                def stack_q(p):
                    sc.wait_ge(sem["stack_q"], at(b, "stack_q", p + 1))
                    A(stq[:, p % 2, :], bank[0][:], ACT.Copy).then_inc(sem["stq_sb"], 1)

                def exps(p, i):
                    n = NT * p + i
                    w = P if i == 0 else 2 * P
                    sc.wait_ge(sem["negmax"], at(b, "negmax", n + 1))
                    for h in range(2):
                        ins = A(probs[:, i, h * w:h * w + w], bank[2 + i][:, h * w:h * w + w], ACT.Exp, bias=nmx[:, n, h:h + 1],
                                accum_out=rsum[:, i, 2 * p + h:2 * p + h + 1])
                    ins.then_inc(sem["probs"], 1)

                def turn_odd(p, i):
                    n = NT * p + i
                    sc.wait_ge(sem["p_turned"], at(b, "p_turned", n + 1))
                    A(pt[:, 1, :], bank[1][:], ACT.Copy).then_inc(sem["p_odd"], 1)

                stack_q(0)
                for i in range(NT):
                    exps(0, i)
                stack_q(1)
                for p in range(NPAIR):
                    for i in range(NT):
                        if i % 2 == 1:
                            turn_odd(p, i)
                        if i == 3 and p + 2 < NPAIR:
                            stack_q(p + 2)
                        if p + 1 < NPAIR:
                            exps(p + 1, i)
                sc.wait_ge(sem["gate_z"], at(b, "gate_z", 1))
                A(small[:, 5, :], small[:, 4, :], ACT.Exp, scale=-1.0).then_inc(sem["gate_e"], 1)
                for k in range(NK):
                    sc.wait_ge(sem["mixed_t"], at(b, "mixed_t", k + 1))
                    A(work[:, 8 + k, :], bank[k][:], ACT.Copy).then_inc(sem["mixed_sb"], 1)
                for k in range(NK):
                    sc.wait_ge(sem["turned"], at(b, "turned", 2 + k + 1))
                    A(hiT[:, k, :], bank[k][:], ACT.Copy).then_inc(sem["evened"], 1)
                for f in range(NF):
                    sc.wait_ge(sem["h_ps"], at(b, "h_ps", f + 1))
                    if f >= 2:
                        sc.wait_ge(sem["g_lo"], at(b, "g_lo", f - 1))
                    A(work[:, f % 2, :], bank[2 + f % 4][:], ACT.Gelu, bias=b1[:, f:f + 1]).then_inc(sem["gelu"], 1)
                sc.wait_ge(sem["f_y"], at(b, "f_y", NF))
                for k in range(NK):
                    A(work[:, 2 + k, :], bank[6 + k][:], ACT.Identity, bias=b2[:, k:k + 1]).then_inc(sem["fy_sb"], 1)
                for k in range(NK):
                    sc.wait_ge(sem["turned"], at(b, "turned", 4 + k + 1))
                    A(xT[:, k, 1:S + 1], bank[k][:], ACT.Copy).then_inc(sem["evened"], 1)
                vf, kf, ek, dec, rf = (work[:, i:i + 2, :] for i in (0, 2, 4, 6, 8))
                sc.wait_ge(sem["mix"], at(b, "mix", 8))
                for g in range(2):
                    sc.wait_ge(sem["proj"], at(b, "proj", g + 1))
                    A(hiT[:, g, :], bank[2 + g][:], ACT.Copy).then_inc(sem["v_hi"], 1)
                    A(vf[:, g, :], bank[2 + g][:], ACT.Copy).then_inc(sem["v_f"], 1)
                sc.wait_ge(sem["proj"], at(b, "proj", 8))
                for g in range(2):
                    A(kf[:, g, :], bank[4 + g][:], ACT.Copy).then_inc(sem["k_f"], 1)
                    A(ek[:, g, :], bank[4 + g][:], ACT.Exp, bias=u_c[:, g:g + 1]).then_inc(sem["ek"], 1)
                for g in range(2):
                    A(dec[:, g, :], bank[6 + g][:], ACT.Sigmoid).then_inc(sem["dec"], 1)
                for g in range(2):
                    A(rf[:, g, :], bank[g][:], ACT.Sigmoid).then_inc(sem["r_f"], 1)
                sc.wait_ge(sem["o_diff"], at(b, "o_diff", 1))
                A(work[:, 6:8, :], work[:, 4:6, :], ACT.Square).then_inc(sem["o_sq"], 1)
                sc.wait_ge(sem["o_back"], at(b, "o_back", 1))
                for g in range(2):
                    A(work[:, 2 + g, :], bank[2 + g][:], ACT.Identity, bias=lnwb[:, 1:2], scale=lnwb[:, 0:1]).then_inc(sem["o_aff"], 1)

        @block.tensor
        def _(pe):
            T = nc.tensor
            pe.wait_ge(loaded, 16 * n_load[0])
            pe.wait_ge(tern_sum, 2)
            for i in range(2):
                ins = T.matmul(bank[0][:, i:i + 1], ones[:], small[:, i, 0:1], start=True, stop=True)
            ins.then_inc(tern_tot, 1)
            pe.wait_ge(const_ready, 1)

            with pe.Fori(0, B) as b:
                def turn_x(n):
                    for i in range(NT):
                        pe.wait_ge(sem["normed"], at(b, "normed", NT * n + i + 1))
                        for k in range(NK):
                            ins = T.transpose(bank[k][:, i * P:(i + 1) * P], xn[:, i, k * P:(k + 1) * P], ident[:])
                            if i == NT - 1:
                                ins.then_inc(sem["turned"], 1)

                turn_x(0)
                pe.wait_ge(sem["evened"], at(b, "evened", 2))
                for i in range(4):
                    for k in range(NK):
                        ins = T.matmul(bank[2 + i][:], wqkv[:, k, i * P:(i + 1) * P], xT[:, k, 1:S + 1], start=k == 0, stop=k == NK - 1)
                    ins.then_inc(sem["q_ps" if i < 2 else "k_ps"], 1)
                for i in range(NT):
                    for k in range(NK):
                        ins = T.matmul(bank[6 + i // 2][:, (i % 2) * D:(i % 2) * D + D], xT[:, k, 1 + i * P:1 + (i + 1) * P],
                                       wqkv[:, k, 2 * D:3 * D], start=k == 0, stop=k == NK - 1)
                    if i % 2:
                        ins.then_inc(sem["v_ps"], 1)
                for k in range(NK):
                    ins = T.matmul(bank[0][0:LD, :], wrq[:, k, :], xT[:, k, 1:S + 1], start=k == 0, stop=k == NK - 1)
                ins.then_inc(sem["rq_ps"], 1)
                pe.wait_ge(sem["pooled"], at(b, "pooled", 1))
                for k in range(NK):
                    T.matmul(bank[1][0:LD, 0:NLAT], wrkv[:, k, 0:LD], poolx[:, 1, k, :], start=k == 0, stop=k == NK - 1)
                for k in range(NK):
                    ins = T.matmul(bank[1][0:NLAT, NLAT:NLAT + LD], poolx[:, 1, k, :], wrkv[:, k, LD:2 * LD], start=k == 0, stop=k == NK - 1)
                ins.then_inc(sem["rkv_ps"], 1)
                pe.wait_ge(sem["qk_lo"], at(b, "qk_lo", 4))
                pe.wait_ge(sem["rk_sb"], at(b, "rk_sb", 1))
                pe.wait_ge(sem["rq_sb"], at(b, "rq_sb", 1))
                for i in range(NT):
                    o = bank[2 + i // 2][:, (i % 2) * 256:(i % 2) * 256 + 256]
                    T.matmul(o, ident_b[:], lmask[:, i, :], start=True, stop=False)
                    ins = T.matmul(o, work[0:LD, 5, i * P:(i + 1) * P], rk_bd[:].rearrange("p h l -> p (h l)"), start=False, stop=True)
                ins.then_inc(sem["lat_ps"], 1)
                pe.wait_ge(sem["lat_exp"], at(b, "lat_exp", 2))
                pe.wait_ge(sem["v_sb"], at(b, "v_sb", 1))
                T.transpose(bank[4][:, 0:P], work[:, 2, 0:P], ident[:])
                for i in range(NT):
                    for h in range(LH):
                        ins = T.transpose(bank[4 + i][0:NLAT, h * P:(h + 1) * P],
                                          work[:, 2 + i // 2, (i % 2) * 256 + h * NLAT:(i % 2) * 256 + (h + 1) * NLAT], ident[:])
                    ins.then_inc(sem["lat_turned"], 1)
                for i in range(NT):
                    pe.wait_ge(sem["lat_probs"], at(b, "lat_probs", i + 1))
                    for h in range(LH):
                        ins = T.matmul(bank[0][:, i * LD + h * 16:i * LD + h * 16 + 16], work[0:NLAT, 8 + i, h * P:(h + 1) * P],
                                       rv_sb[:, h * 16:h * 16 + 16], start=True, stop=True)
                ins.then_inc(sem["lat_out"], 1)
                pe.wait_ge(sem["lat_normed"], at(b, "lat_normed", 1))
                T.transpose(bank[1][:, 0:P], work[:, 4, 0:P], ident[:])
                for i in range(NT):
                    ins = T.transpose(bank[1][0:LD, i * P:(i + 1) * P], work[:, 4, i * LD:(i + 1) * LD], ident[:])
                ins.then_inc(sem["lat_nt"], 1)
                pe.wait_ge(sem["lat_nt_sb"], at(b, "lat_nt_sb", 1))
                for i in range(NT):
                    ins = T.matmul(bank[2 + i // 2][:, (i % 2) * D:(i % 2) * D + D], work[0:LD, 5, i * P:(i + 1) * P], wrout[:],
                                   start=True, stop=True)
                ins.then_inc(sem["remote_ps"], 1)

                def stack_q(p):
                    g, j = p // PAIRS, p % PAIRS
                    if p:
                        pe.wait_ge(sem["stk_sb"], at(b, "stk_sb", p))
                    T.matmul(bank[0][:], sel_qk[:, j, 0, :], hiT[:, g, :], start=True, stop=False)
                    T.matmul(bank[0][:], sel_qk[:, j, 1, :], loT[:, g, :], start=False, stop=True).then_inc(sem["stack_q"], 1)

                def stack_k(p):
                    g, j = p // PAIRS, p % PAIRS
                    pe.wait_ge(sem["stq_sb"], at(b, "stq_sb", p + 1))
                    T.matmul(bank[0][:], sel_qk[:, j, 2, :], hiT[:, 2 + g, :], start=True, stop=False)
                    T.matmul(bank[0][:], sel_qk[:, j, 3, :], loT[:, 2 + g, :], start=False, stop=True).then_inc(sem["stack_k"], 1)

                def scores(p, i):
                    if i == 0:
                        pe.wait_ge(sem["stq_sb"], at(b, "stq_sb", p + 1))
                        pe.wait_ge(sem["stk_sb"], at(b, "stk_sb", p + 1))
                    o = bank[2 + i]
                    q = stq[:, p % 2, i * P:(i + 1) * P]
                    w, k0 = (P, 0) if i == 0 else (2 * P, (i - 1) * P)
                    mask = wmask[:, :, P:2 * P] if i == 0 else wmask[:]
                    T.matmul(o[:, 0:2 * w], ident_b[:], mask, start=True, stop=True)
                    for par in range(2):
                        ins = T.matmul(o[:, par * w:par * w + w], q, stk[:, p % 2, par, k0:k0 + w], start=False, stop=True,
                                       skip_group_check=True)
                    ins.then_inc(sem["scores"], 1)

                def turn_p(p, i):
                    n = NT * p + i
                    pe.wait_ge(sem["probs"], at(b, "probs", n + 1))
                    o = (bank[6], bank[1])[i % 2]
                    if n >= 2:
                        pe.wait_ge(sem["p_odd" if i % 2 else "p_even"], at(b, "p_odd", n // 2))
                    w = P if i == 0 else 2 * P
                    for c in range(2 * w // P):
                        ins = T.transpose(o[:, c * P:(c + 1) * P], probs[:, i, c * P:(c + 1) * P], ident[:])
                    ins.then_inc(sem["p_turned"], 1)

                def pv(p, i):
                    n = NT * p + i
                    pe.wait_ge(sem["p_odd" if i % 2 else "p_even"], at(b, "p_odd", n // 2 + 1))
                    if i == 0 and p >= 2:
                        pe.wait_ge(sem["local_raw"], at(b, "local_raw", p - 1))
                    for h in range(2):
                        o = bank[7][:, 128 * (p % 2) + 32 * i + 16 * h:128 * (p % 2) + 32 * i + 16 * h + 16]
                        hh = 2 * p + h
                        blocks = [0] if i == 0 else [i - 1, i]
                        for c, kb in enumerate(blocks):
                            ins = T.matmul(o, pt[:, i % 2, (h * len(blocks) + c) * P:(h * len(blocks) + c + 1) * P],
                                           v_tok[:, kb, hh * HD:(hh + 1) * HD], start=c == 0, stop=c == len(blocks) - 1)
                    if i == NT - 1:
                        ins.then_inc(sem["local_ps"], 1)

                pe.wait_ge(sem["remote"], at(b, "remote", 1))
                stack_q(0)
                stack_k(0)
                for i in range(NT):
                    scores(0, i)
                stack_q(1)
                stack_k(1)
                for p in range(NPAIR):
                    for i in range(NT):
                        turn_p(p, i)
                        if p + 1 < NPAIR:
                            scores(p + 1, i)
                        if i:
                            pv(p, i - 1)
                        if i == 2 and p + 2 < NPAIR:
                            stack_q(p + 2)
                        if i == 3 and p + 2 < NPAIR:
                            stack_k(p + 2)
                    pv(p, NT - 1)
                pe.wait_ge(sem["mixed"], at(b, "mixed", 1))
                for k in range(NK):
                    for i in range(NT):
                        c = (i % 2) * D + k * P
                        ins = T.transpose(bank[k][:, i * P:(i + 1) * P], work[:, 2 + i // 2, c:c + P], ident[:])
                    ins.then_inc(sem["mixed_t"], 1)
                pe.wait_ge(sem["mixed_sb"], at(b, "mixed_sb", 2))
                for i in range(NT):
                    for k in range(NK):
                        ins = T.matmul(bank[2 + i // 2][:, (i % 2) * D:(i % 2) * D + D], work[:, 8 + k, i * P:(i + 1) * P],
                                       wout[:, k, :], start=k == 0, stop=k == NK - 1)
                ins.then_inc(sem["out_ps"], 1)

                turn_x(1)
                pe.wait_ge(sem["evened"], at(b, "evened", 4))
                pe.wait_ge(sem["f_lo"], at(b, "f_lo", 1))

                def up(f):
                    if f >= 4:
                        pe.wait_ge(sem["gelu"], at(b, "gelu", f - 3))
                    for k in range(NK):
                        for c, part in enumerate((hiT, loT)):
                            ins = T.matmul(bank[2 + f % 4][:], w1t[:, k, f * P:(f + 1) * P], part[:, k, :],
                                           start=k == 0 and c == 0, stop=k == NK - 1 and c == 1)
                    ins.then_inc(sem["h_ps"], 1)

                def down(f):
                    pe.wait_ge(sem["g_lo"], at(b, "g_lo", f + 1))
                    for k in range(NK):
                        for c, part in enumerate((stq[:, f % 2, :], stk[:, 0, f % 2, :])):
                            ins = T.matmul(bank[6 + k][:], w2t[:, f, k * P:(k + 1) * P], part, start=f == 0 and c == 0,
                                           stop=f == NF - 1 and c == 1)
                    ins.then_inc(sem["f_y"], 1)

                for f in range(NF + 2):
                    if f < NF:
                        up(f)
                    if f >= 2:
                        down(f - 2)
                pe.wait_ge(sem["fy_sb"], at(b, "fy_sb", 2))
                for i in range(NT):
                    for k in range(NK):
                        ins = T.transpose(bank[2 + i // 2][:, (i % 2) * D + k * P:(i % 2) * D + (k + 1) * P],
                                          work[:, 2 + k, i * P:(i + 1) * P], ident[:])
                ins.then_inc(sem["fy_tok"], 1)

                turn_x(2)
                pe.wait_ge(sem["mix"], at(b, "mix", 2))
                for w in range(4):
                    pe.wait_ge(sem["mix"], at(b, "mix", 2 * w + 2))
                    if w == 3:
                        pe.wait_ge(sem["evened"], at(b, "evened", 6))
                    for g in range(2):
                        o = bank[(2 + 2 * w + g) % 8]
                        for k in range(NK):
                            ins = T.matmul(o[:], wrk[:, w, k, g * P:(g + 1) * P], work[:, 2 + 2 * w + k, :], start=k == 0, stop=k == NK - 1)
                        ins.then_inc(sem["proj"], 1)

                def spread_v(n):
                    g, j = divmod(n, HD)
                    if n >= 3:
                        pe.wait_ge(sem["kv"], at(b, "kv", n - 2))
                    o = bank[2 + n % 3]
                    T.matmul(o[:], sel_v[:, j, :], hiT[:, g, :], start=True, stop=False)
                    T.matmul(o[:], sel_v[:, j, :], loT[:, g, :], start=False, stop=True).then_inc(sem["v_bc"], 1)

                def reduce_o(n):
                    g, j = divmod(n, HD)
                    pe.wait_ge(sem["rs"], at(b, "rs", n + 1))
                    T.matmul(bank[6 + g][:], sel_o[:, j, :], probs[:, n % 2, :], start=j == 0, stop=j == HD - 1
                             ).then_inc(sem["summed"], 1)

                pe.wait_ge(sem["v_lo"], at(b, "v_lo", 1))
                pe.wait_ge(sem["v_f"], at(b, "v_f", 2))
                pe.wait_ge(sem["ek"], at(b, "ek", 2))
                for n in range(3):
                    spread_v(n)
                pe.wait_ge(sem["rb"], at(b, "rb", 1))
                for g in range(2):
                    ins = T.matmul(bank[g][:], blockones[:], work[:, 10 + g, :], start=True, stop=True)
                ins.then_inc(sem["bonus_ps"], 1)
                for n in range(2 * HD):
                    reduce_o(n)
                    if n + 3 < 2 * HD:
                        spread_v(n + 3)
                pe.wait_ge(sem["o_sb"], at(b, "o_sb", 1))
                for i in range(NT):
                    for g in range(2):
                        ins = T.transpose(bank[i // 2][:, (i % 2) * D + g * P:(i % 2) * D + (g + 1) * P], work[:, 2 + g, i * P:(i + 1) * P], ident[:])
                ins.then_inc(sem["o_tok"], 1)
                pe.wait_ge(sem["o_norm"], at(b, "o_norm", 1))
                for g in range(2):
                    for i in range(NT):
                        c = (i % 2) * D + g * P
                        ins = T.transpose(bank[2 + g][:, i * P:(i + 1) * P], work[:, 6 + i // 2, c:c + P], ident[:])
                ins.then_inc(sem["o_back"], 1)
                pe.wait_ge(sem["y_in"], at(b, "y_in", 1))
                for i in range(NT):
                    for k in range(NK):
                        ins = T.matmul(bank[4 + i // 2][:, (i % 2) * D:(i % 2) * D + D], work[:, 4 + k, i * P:(i + 1) * P],
                                       wrk[:, 4, k, :], start=k == 0, stop=k == NK - 1)
                ins.then_inc(sem["w_ps"], 1)


PER2 = dict(
    x_in=16, x_out=16, var0=1, var1=1, rstd0=1, rstd1=1, normed=NT, turned=NK, x_f=NK, x_lo=NK, route_ps=1, route_z=1, route_e=1, comb=1, comb_ps=1,
    comb_hi=1, comb_lo=1, gate_ps=NE + 1, up_ps=NE + 1, c_ps=NE, silu=NE + 1, h_f=NE + 1, h_hi=NE + 1, h_lo=NE + 1,
    y_acc=NE + 1, y_sb=NK, y_turned=2, y_tok=2, x_final=1, own_hidden=NE, own_norm=2, own_route=11, own_end=3,
)
S_YT = (2, 3)
S_END = (4, 5)
S_STAT, S_NORM, S_TURN, S_ROUTE, S_TOP, S_COMB = 7, 8, (9, 10), 11, 15, 16


def expert_layer(nc, t, x3, out):
    with ExitStack() as ctx:
        def sb(name, shape, dt=F32):
            return ctx.enter_context(nc.sbuf_tensor(name, shape, dt))

        bank = [ctx.enter_context(nc.psum_tensor(f"mbank{i}", [P, 512], F32)) for i in range(8)]
        gate_bank, up_bank, c_bank, y_bank, side = bank[0:2], bank[2:4], bank[4], bank[5:7], bank[7]
        sem = {n: ctx.enter_context(nc.semaphore("m_" + n)) for n in PER2}
        loaded = ctx.enter_context(nc.semaphore("m_loaded"))
        w_loaded = [ctx.enter_context(nc.semaphore(f"m_w_loaded{i}")) for i in range(2)]
        w_split = ctx.enter_context(nc.semaphore("m_w_split"))
        w_hi_made = ctx.enter_context(nc.semaphore("m_w_hi_made"))
        const_ready = ctx.enter_context(nc.semaphore("m_const_ready"))

        NX = NE + 1
        W13, W2 = NK * 2 * INTER, D
        ident = sb("m_ident", [P, P])
        sel_e = sb("sel_e", [64, NE, P], F32R)
        gate_w = sb("gate_w", [P, NK, NE])
        gate_b = sb("gate_b", [P, NE])
        mhalf = sb("m_mhalf", [P, NT])
        euler = sb("euler", [P, NT * NE])
        w_hi = sb("w_hi", [P, NX, W13 + W2], F32R)
        w_lo = sb("w_lo", [P, NX, W13 + W2], F32R)
        w_raw = sb("w_raw", [P, 2, W13 + W2])
        sel_raw = sb("sel_raw", [64, NE * P])
        tick = sb("m_tick", [P, 1])[:]

        x_tok = [sb(f"m_x_tok{i}", [P, NT, D]) for i in range(2)]
        xh = [sb(f"m_xh{i}", [P, NK, S], F32R) for i in range(2)]
        xl = [sb(f"m_xl{i}", [P, NK, S], F32R) for i in range(2)]
        combT = [sb(f"combT{i}", [64, S], F32R) for i in range(2)]
        xn = sb("m_xn", [P, NT, D])
        xf = sb("m_xf", [P, NK, S])
        y_tok = sb("m_y_tok_sb", [P, NT, D])
        yn = sb("m_yn", [P, NT, D])
        st = sb("m_st", [P, 2, NT, 6])
        mv = sb("m_mv", [P, 2, NT, 2])
        vare = sb("m_vare", [P, 2, NT])
        rstd = sb("m_rstd", [P, 2, NT])
        rz = sb("rz", [P, NT * NE])
        re_ = sb("re_", [P, NT * NE])
        score = sb("score", [P, NT, NE])
        biased = sb("biased", [P, NT, NE + TOPK])
        rest = sb("rest", [P, NT, NE + TOPK])
        top = sb("top", [P, NT, 8])
        comb = sb("comb", [P, NT, NE])
        csum = sb("csum", [P, 2, NT])
        sg = sb("sg", [P, 3, S])
        hf = sb("hf", [P, 3, S])
        hh = sb("hh", [P, 3, S], F32R)
        hl = sb("hl", [P, 3, S], F32R)
        yT = sb("yT", [P, NK, S])

        def at(b, name, k):
            return b * PER2[name] + k

        def bc(ap, *shape):
            return ap.broadcast_to(shape)

        def batches(eng, body):
            body(0, 0, True, False)
            with eng.Fori(0, B // 2 - 1) as i:
                body(i * 2 + 1, 1, False, False)
                body(i * 2 + 2, 0, False, False)
            body(B - 1, 1, False, True)

        N_LOAD = 6
        rows = lambda ap: ap.rearrange("o (t p) d -> p (o t) d", p=P)
        block = ctx.enter_context(nc.Block())

        @block.sync
        def _(sp):
            sp.dma_start(ident[:], t["c_ident"]).then_inc(loaded, 16)
            sp.dma_start(gate_w[:], t["gate_w"].rearrange("(k p) n -> p k n", p=P)).then_inc(loaded, 16)
            sp.dma_start(gate_b[:], t["gate_b"].partition_broadcast(P)).then_inc(loaded, 16)
            sp.dma_start(mhalf[:], t["c_mhalf"][:, 0:NT]).then_inc(loaded, 16)
            sp.dma_start(euler[:], t["c_euler"]).then_inc(loaded, 16)
            sp.dma_start(sel_raw[:], t["c_sele"]).then_inc(loaded, 16)
            for i in range(2):
                sp.dma_start(x_tok[i][:], rows(x3[i:i + 1])).then_inc(sem["x_in"], 16)
            for e in range(NX):
                if e >= 2:
                    sp.wait_ge(w_split, e - 1)
                sp.dma_start(w_raw[:, e % 2, 0:W13], t["w13"][e].rearrange("(k p) n -> p k n", p=P)).then_inc(w_loaded[e % 2], 16)
                sp.dma_start(w_raw[:, e % 2, W13:], t["w2e"][e]).then_inc(w_loaded[e % 2], 16)

            def store(b, par):
                sp.wait_ge(sem["x_final"], at(b, "x_final", 1))
                sp.dma_start(rows(out[bass.ds(b, 1)]), x_tok[par][:]).then_inc(sem["x_out"], 16)

            def exchange(b, par):
                store(b, par)
                sp.wait_ge(sem["x_out"], at(b, "x_out", 16))
                sp.dma_start(x_tok[par][:], rows(x3[bass.ds(b + 2, 1)])).then_inc(sem["x_in"], 16)

            with sp.Fori(0, B // 2 - 1) as i:
                exchange(i * 2, 0)
                exchange(i * 2 + 1, 1)
            store(B - 2, 0)
            store(B - 1, 1)
            sp.wait_ge(sem["x_out"], B * 16)

        @block.vector
        def _(ve):
            V = nc.vector
            for i in range(2):
                V.memset(combT[i][:].bitcast(F32), 0.0)
            V.memset(biased[:, :, NE:], BIG)
            ve.wait_ge(loaded, 16 * N_LOAD)
            V.tensor_copy(sel_e[:].rearrange("p e m -> p (e m)"), sel_raw[:]).then_inc(const_ready, 1)

            own_hidden, own_norm, own_route, own_end = (Own(ve, sem[n], PER2[n]) for n in ("own_hidden", "own_norm", "own_route", "own_end"))

            def stats(own, b, side_, src):
                for i in range(NT):
                    ins = V.bn_stats(st[:, side_, i, :], src[:, i, :])
                own.link(ins, tick)
                for i in range(NT):
                    ins = V.bn_aggr(mv[:, side_, i, :], st[:, side_, i, :])
                own.link(ins)
                V.tensor_scalar(vare[:, side_], mv[:, side_, :, 1], EPS, None, ALU.add).then_inc(sem["var0" if side_ == 0 else "var1"], 1)

            def norm(b, par):
                ve.wait_ge(sem["rstd0"], at(b, "rstd0", 1))
                for i in range(NT):
                    V.tensor_scalar(xn[:, i, :], x_tok[par][:, i, :], mv[:, 0, i, 0:1], rstd[:, 0, i:i + 1], ALU.subtract, ALU.mult
                                    ).then_inc(sem["normed"], 1)

            def x_low(b, par, k):
                ve.wait_ge(sem["x_f"], at(b, "x_f", k + 1))
                V.tensor_tensor(xl[par][:, k, :], xf[:, k, :], xh[par][:, k, :].bitcast(F32), ALU.subtract).then_inc(sem["x_lo"], 1)

            def route(b):
                own = own_route
                own.start(b)
                ve.wait_ge(sem["route_e"], at(b, "route_e", 1))
                own.link(V.tensor_scalar(re_[:], re_[:], 1.0, None, ALU.add))
                own.link(V.reciprocal(score[:].rearrange("p a e -> p (a e)"), re_[:]))
                own.link(V.tensor_tensor(biased[:, :, 0:NE], score[:], bc(gate_b[:].unsqueeze(1), P, NT, NE), ALU.add), tick)
                for i in range(NT):
                    ins = V.max(top[:, i, :], biased[:, i, :])
                own.link(ins, tick)
                for i in range(NT):
                    ins = V.match_replace(rest[:, i, :], top[:, i, :], biased[:, i, :], -BIG)
                own.link(ins)
                own.link(V.tensor_tensor(comb[:], rest[:, :, 0:NE], biased[:, :, 0:NE], ALU.is_lt))
                own.link(V.tensor_tensor(comb[:], comb[:], score[:], ALU.mult))
                own.link(V.tensor_reduce(csum[:, 0, :], comb[:], X, ALU.add))
                own.link(V.reciprocal(csum[:, 1, :], csum[:, 0, :]))
                own.link(V.tensor_tensor(comb[:], comb[:], bc(csum[:, 1, :].unsqueeze(2), P, NT, NE), ALU.mult))
                own.link(V.tensor_scalar(comb[:], comb[:], ROUTE_SCALE, None, ALU.mult))
                V.memset(tick, 0.0).then_inc(sem["comb"], 1)
                own.end()

            def comb_low(b, par):
                ve.wait_ge(sem["comb_hi"], at(b, "comb_hi", 1))
                V.tensor_tensor(combT[par][32:32 + NE, :], side[0:NE, :], combT[par][0:NE, :].bitcast(F32), ALU.subtract
                                ).then_inc(sem["comb_lo"], 1)

            def start_stats(b, par):
                ve.wait_ge(sem["x_in"], at(b, "x_in", 16))
                own_norm.start(b)
                stats(own_norm, b, 0, x_tok[par])
                own_norm.end()

            def end_stats(b):
                ve.wait_ge(sem["y_tok"], at(b, "y_tok", 2))
                own_end.start(b)
                stats(own_end, b, 1, y_tok)

            def end_norm(b, par):
                ve.wait_ge(sem["rstd1"], at(b, "rstd1", 1))
                for i in range(NT):
                    ins = V.tensor_scalar(yn[:, i, :], y_tok[:, i, :], mv[:, 1, i, 0:1], rstd[:, 1, i:i + 1], ALU.subtract, ALU.mult)
                own_end.link(ins)
                V.tensor_tensor(x_tok[par][:], x_tok[par][:], yn[:], ALU.add).then_inc(sem["x_final"], 1)
                own_end.end()

            def hidden(b, e):
                ve.wait_ge(sem["silu"], at(b, "silu", e + 1))
                ve.wait_ge(sem["up_ps"], at(b, "up_ps", e + 1))
                sl = e % 3
                if e < NE:
                    own_hidden.link(V.tensor_tensor(sg[:, sl, :], sg[:, sl, :], up_bank[e % 2][:], ALU.mult))
                    ve.wait_ge(sem["c_ps"], at(b, "c_ps", e + 1))
                    V.tensor_tensor(hf[:, sl, :], sg[:, sl, :], c_bank[:], ALU.mult).then_inc(sem["h_f"], 1)
                else:
                    V.tensor_tensor(hf[:, sl, :], sg[:, sl, :], up_bank[e % 2][:], ALU.mult).then_inc(sem["h_f"], 1)

            def low(b, e):
                ve.wait_ge(sem["h_hi"], at(b, "h_hi", e + 1))
                V.tensor_tensor(hl[:, e % 3, :], hf[:, e % 3, :], hh[:, e % 3, :].bitcast(F32), ALU.subtract).then_inc(sem["h_lo"], 1)

            for e in range(NX):
                ve.wait_ge(w_hi_made, e + 1)
                V.tensor_tensor(w_lo[:, e, :], w_raw[:, e % 2, :], w_hi[:, e, :].bitcast(F32), ALU.subtract).then_inc(w_split, 1)
            start_stats(0, 0)
            norm(0, 0)
            for k in range(NK):
                x_low(0, 0, k)
            route(0)

            def body(b, par, first, last):
                own_hidden.start(b)
                for e in range(NX):
                    if e == 0:
                        comb_low(b, par)
                    if e:
                        low(b, e - 1)
                    elif not first:
                        low(b - 1, NX - 1)
                    hidden(b, e)
                    if not first:
                        if e == S_END[0]:
                            end_stats(b - 1)
                        if e == S_END[1]:
                            end_norm(b - 1, 1 - par)
                    if not last:
                        if e == S_STAT:
                            start_stats(b + 1, 1 - par)
                        if e == S_NORM:
                            norm(b + 1, 1 - par)
                        if e == S_TURN[0] + 1:
                            x_low(b + 1, 1 - par, 0)
                        if e == S_TURN[1] + 1:
                            x_low(b + 1, 1 - par, 1)
                        if e == S_TOP:
                            route(b + 1)
                own_hidden.end()

            batches(ve, body)
            low(B - 1, NX - 1)
            end_stats(B - 1)
            end_norm(B - 1, 1)

        @block.gpsimd
        def _(gp):
            G = nc.gpsimd
            gp.wait_ge(loaded, 16 * N_LOAD)

            def root(b, side_):
                n = f"{side_}"
                gp.wait_ge(sem["var" + n], at(b, "var" + n, 1))
                G.tensor_tensor(rstd[:, side_], vare[:, side_], mhalf[:], ALU.pow).then_inc(sem["rstd" + n], 1)

            def route_exp(b):
                gp.wait_ge(sem["route_z"], at(b, "route_z", 1))
                G.tensor_tensor(re_[:], euler[:], rz[:], ALU.pow).then_inc(sem["route_e"], 1)

            def body(b, par, first, last):
                if not first:
                    root(b - 1, 1)
                if not last:
                    root(b + 1, 0)
                    route_exp(b + 1)

            root(0, 0)
            route_exp(0)
            batches(gp, body)
            root(B - 1, 1)

        @block.scalar
        def _(sc):
            A = nc.scalar.activation
            for e in range(NX):
                sc.wait_ge(w_loaded[e % 2], 32 * (e // 2 + 1))
                A(w_hi[:, e, :], w_raw[:, e % 2, :], ACT.Copy).then_inc(w_hi_made, 1)

            def x_parts(b, par, k):
                sc.wait_ge(sem["turned"], at(b, "turned", k + 1))
                A(xh[par][:, k, :], side[:], ACT.Copy)
                A(xf[:, k, :], side[:], ACT.Copy).then_inc(sem["x_f"], 1)

            def route_logits(b):
                sc.wait_ge(sem["route_ps"], at(b, "route_ps", 1))
                A(rz[:], side[:, 0:NT * NE], ACT.Copy, scale=-1.0).then_inc(sem["route_z"], 1)

            def comb_high(b, par):
                sc.wait_ge(sem["comb_ps"], at(b, "comb_ps", 1))
                A(combT[par][0:NE, :], side[0:NE, :], ACT.Copy).then_inc(sem["comb_hi"], 1)

            def silu(b, e):
                sc.wait_ge(sem["gate_ps"], at(b, "gate_ps", e + 1))
                A(sg[:, e % 3, :], gate_bank[e % 2][:], ACT.Silu).then_inc(sem["silu"], 1)

            def high(b, e):
                sc.wait_ge(sem["h_f"], at(b, "h_f", e + 1))
                A(hh[:, e % 3, :], hf[:, e % 3, :], ACT.Copy).then_inc(sem["h_hi"], 1)

            def y_out(b):
                sc.wait_ge(sem["y_acc"], at(b, "y_acc", NX))
                for k in range(NK):
                    A(yT[:, k, :], y_bank[k][:], ACT.Copy).then_inc(sem["y_sb"], 1)

            def y_tokens(b, half):
                sc.wait_ge(sem["y_turned"], at(b, "y_turned", half + 1))
                A(y_tok[:, 2 * half:2 * half + 2, :].rearrange("p a d -> p (a d)"), side[:], ACT.Copy).then_inc(sem["y_tok"], 1)

            for k in range(NK):
                x_parts(0, 0, k)
            route_logits(0)
            comb_high(0, 0)

            def body(b, par, first, last):
                for e in range(NX):
                    silu(b, e)
                    if e:
                        high(b, e - 1)
                    elif not first:
                        high(b - 1, NX - 1)
                    if not first:
                        if e == 1:
                            y_out(b - 1)
                        if e in S_YT:
                            y_tokens(b - 1, S_YT.index(e))
                    if not last:
                        if e in S_TURN:
                            x_parts(b + 1, 1 - par, S_TURN.index(e))
                        if e == S_ROUTE:
                            route_logits(b + 1)
                        if e == S_COMB:
                            comb_high(b + 1, 1 - par)

            batches(sc, body)
            high(B - 1, NX - 1)
            y_out(B - 1)
            for half in range(2):
                y_tokens(B - 1, half)

        @block.tensor
        def _(pe):
            T = nc.tensor

            def turn_x(b, k):
                pe.wait_ge(sem["normed"], at(b, "normed", NT))
                if k:
                    pe.wait_ge(sem["x_f"], at(b, "x_f", k))
                for i in range(NT):
                    ins = T.transpose(side[:, i * P:(i + 1) * P], xn[:, i, k * P:(k + 1) * P], ident[:])
                ins.then_inc(sem["turned"], 1)

            def route(b):
                pe.wait_ge(sem["x_f"], at(b, "x_f", NK))
                for i in range(NT):
                    for k in range(NK):
                        ins = T.matmul(side[:, i * NE:(i + 1) * NE], xf[:, k, i * P:(i + 1) * P], gate_w[:, k, :],
                                       start=k == 0, stop=k == NK - 1)
                ins.then_inc(sem["route_ps"], 1)

            def turn_comb(b):
                pe.wait_ge(sem["comb"], at(b, "comb", 1))
                for i in range(NT):
                    ins = T.transpose(side[0:NE, i * P:(i + 1) * P], comb[:, i, :], ident[:])
                ins.then_inc(sem["comb_ps"], 1)

            def turn_y(b, half):
                if half:
                    pe.wait_ge(sem["y_tok"], at(b, "y_tok", half))
                else:
                    pe.wait_ge(sem["y_sb"], at(b, "y_sb", NK))
                for i in range(2):
                    for k in range(NK):
                        ins = T.transpose(side[:, i * D + k * P:i * D + (k + 1) * P], yT[:, k, (2 * half + i) * P:(2 * half + i + 1) * P], ident[:])
                ins.then_inc(sem["y_turned"], 1)

            def product(o, cols, e, hi, lo, first, last):
                terms = ((w_hi, hi), (w_hi, lo), (w_lo, hi))
                for c, (w, m) in enumerate(terms):
                    ins = T.matmul(o, w[:, e, cols:cols + P], m, start=first and c == 0, stop=last and c == 2)
                return ins

            def gate_up(b, par, e, first):
                if e >= 2:
                    pe.wait_ge(sem["silu"], at(b, "silu", e - 1))
                elif not first:
                    pe.wait_ge(sem["silu"], at(b, "silu", 0))
                for k in range(NK):
                    ins = product(gate_bank[e % 2][:], k * 2 * INTER, e, xh[par][:, k, :], xl[par][:, k, :], k == 0, k == NK - 1)
                ins.then_inc(sem["gate_ps"], 1)
                if e >= 2:
                    pe.wait_ge(sem["h_f"], at(b, "h_f", e - 1))
                elif not first:
                    pe.wait_ge(sem["h_f"], at(b, "h_f", 0))
                for k in range(NK):
                    ins = product(up_bank[e % 2][:], k * 2 * INTER + INTER, e, xh[par][:, k, :], xl[par][:, k, :], k == 0, k == NK - 1)
                ins.then_inc(sem["up_ps"], 1)

            def spread_c(b, par, e, first):
                if e == 0:
                    pe.wait_ge(sem["comb_lo"], at(b, "comb_lo", 1))
                else:
                    pe.wait_ge(sem["h_f"], at(b, "h_f", e))
                T.matmul(c_bank[:], sel_e[:, e, :], combT[par][:], start=True, stop=True).then_inc(sem["c_ps"], 1)

            def down(b, e, first):
                pe.wait_ge(sem["h_lo"], at(b, "h_lo", e + 1))
                if e == 0 and not first:
                    pe.wait_ge(sem["y_sb"], at(b, "y_sb", 0))
                for k in range(NK):
                    ins = product(y_bank[k][:], W13 + k * P, e, hh[:, e % 3, :], hl[:, e % 3, :], e == 0, e == NX - 1)
                ins.then_inc(sem["y_acc"], 1)

            pe.wait_ge(const_ready, 1)
            for k in range(NK):
                turn_x(0, k)
            route(0)
            turn_comb(0)
            pe.wait_ge(w_split, NX)
            pe.wait_ge(sem["x_lo"], NK)

            def body(b, par, first, last):
                if not first:
                    pe.wait_ge(sem["x_lo"], at(b, "x_lo", NK))
                for e in range(NX):
                    gate_up(b, par, e, first)
                    if e >= 2:
                        down(b, e - 2, first)
                    elif not first:
                        down(b - 1, NX - 2 + e, False)
                    if e < NE:
                        spread_c(b, par, e, first)
                    if not first and e in S_YT:
                        turn_y(b - 1, S_YT.index(e))
                    if not last:
                        if e in S_TURN:
                            turn_x(b + 1, S_TURN.index(e))
                        if e == S_ROUTE:
                            route(b + 1)
                        if e == S_COMB:
                            turn_comb(b + 1)

            batches(pe, body)
            for e in (NX - 2, NX - 1):
                down(B - 1, e, False)
            for half in range(2):
                turn_y(B - 1, half)


def constants():
    import numpy as np

    f = np.float32
    p = np.arange(P)
    c = {"c_ident": np.eye(P, dtype=f), "c_ones": np.ones((P, P), f)}
    block = (p[:, None] // HD == p[None, :] // HD).astype(f)
    c["c_blockones"] = block
    c["c_selo"] = np.stack([block * (p[None, :] % HD == j) for j in range(HD)], 1).astype(f)
    c["c_selv"] = np.stack([block * (p[:, None] % HD == j) for j in range(HD)], 1).reshape(P, HD * P).astype(f)
    sel = np.zeros((P, PAIRS, 4, P), f)
    quarters = ((0, 1), (2, 3), (0, 2), (1, 3))
    for j in range(PAIRS):
        for c4, qs in enumerate(quarters):
            for q in qs:
                r = np.arange(32)
                sel[32 * j + r, j, c4, 32 * q + r] = 1
    c["c_selqk"] = sel.reshape(P, -1)
    c["c_parmask"] = np.stack([(p % 32 // HD == par) for par in range(2)], 1).astype(f)
    c["c_lhmask"] = (np.arange(LD)[:, None] // 16 == np.arange(LH)[None, :]).astype(f)
    i, k = p[:, None], p[None, :]
    prev = (k >= i) & ~((i == 0) & (k == 0))
    own = k < i
    m = np.where(np.concatenate([prev, own], 1), 0, NEG).astype(f)
    c["c_wmask"] = np.stack([m, m], 1).reshape(P, 512)
    tok = np.arange(NT)[None, :, None] * P + p[:, None, None]
    lm = np.where(np.arange(NLAT)[None, None, :] < tok // CHUNK, 0, NEG).astype(f)
    c["c_lmask"] = np.repeat(lm[:, :, None, :], LH, 2).reshape(P, -1)
    c["c_rowloc"] = np.repeat(tok > 0, H, 2).astype(f)
    c["c_rowlat"] = np.repeat(tok >= CHUNK, LH, 2).astype(f)
    c["c_mhalf"] = np.full((P, 64), -0.5, f)
    c["c_euler"] = np.full((P, NT * NE), np.e, f)
    se = np.zeros((64, NE, P), f)
    for e in range(NE):
        se[e, e] = se[32 + e, e] = 1
    c["c_sele"] = se.reshape(64, -1)
    return c


def kernel(**inputs):
    import numpy as np
    import concourse.bacc as _bacc
    from concourse.bass_utils import run_bass_kernel_spmd as _run

    a = {k: np.asarray(v) for k, v in inputs.items()}
    col = lambda v: v.reshape(-1, P).T
    t = constants()
    t["x"] = a["L0_attn_x"]
    t["wqkv"] = a["L0_attn_qkv_w"]
    t["qkb"] = col(a["L0_attn_qkv_b"][:2 * D])
    t["vb"] = a["L0_attn_qkv_b"][2 * D:]
    t["wrq"] = a["L0_attn_rq_w"]
    t["rqb"] = a["L0_attn_rq_b"].reshape(LD, 1)
    t["wrkv"] = a["L0_attn_rkv_w"]
    t["rkb"] = a["L0_attn_rkv_b"][:LD].reshape(LD, 1)
    t["rvb"] = a["L0_attn_rkv_b"][LD:]
    t["wrout"], t["routb"] = a["L0_attn_rout_w"], a["L0_attn_rout_b"]
    t["wout"], t["outb"] = a["L0_attn_out_w"], a["L0_attn_out_b"]
    t["gl"], t["gr"] = a["L0_attn_gl_w"][:, 0], a["L0_attn_gr_w"][:, 0]
    t["w1"], t["w2"] = a["L0_ffn_W1"].T, a["L0_ffn_W2"].T
    t["b1"], t["b2"] = col(a["L0_ffn_b1"]), col(a["L0_ffn_b2"])
    t["wrk"] = np.stack([a["L1_attn_W_" + n].T for n in "vkwro"])
    t["tm"] = np.stack([col(a["L1_attn_tm_" + n]) for n in "vkwr"], 1)
    t["u"] = col(a["L1_attn_u"].reshape(-1))
    t["lnwb"] = np.stack([np.tile(a["L1_attn_ln_w"], 8), np.tile(a["L1_attn_ln_b"], 8)], 1)
    t["gate_w"], t["gate_b"] = a["L1_ffn_gate_w"].T, a["L1_ffn_gate_b"]
    t["w13"] = np.concatenate([a["L1_ffn_w13"], a["L1_ffn_w13_s"][None]]).transpose(0, 2, 1)
    t["w2e"] = np.concatenate([a["L1_ffn_w2"], a["L1_ffn_w2_s"][None]]).transpose(0, 2, 1)

    nc = _bacc.Bacc("TRN2", target_bir_lowering=False, num_devices=1)
    arrays, aps = {}, {}
    for name, v in t.items():
        v = np.ascontiguousarray(v)
        arrays[f"in_{name}"] = v
        aps[name] = nc.dram_tensor(f"in_{name}", v.shape, mybir.dt.from_np(v.dtype), kind="ExternalInput").ap()
    out = nc.dram_tensor("out_0", (B, S, D), F32, kind="ExternalOutput").ap()
    program(nc, aps, out)
    r = _run(nc, [arrays], core_ids=[0])
    return r.results[0]["out_0"]
```

```python
from contextlib import ExitStack

import concourse.bass as bass
from concourse import mybir

F32 = mybir.dt.float32
F32R = mybir.dt.float32r
BF16 = mybir.dt.bfloat16
ALU = mybir.AluOpType
ACT = mybir.ActivationFunctionType
X = mybir.AxisListType.X

P = 128
B, S, D = 8, 512, 256
NT, NK = S // P, D // P
H, HD = 16, 16
LH, LD, NLAT = 4, 64, 64
CHUNK = S // NLAT
FF = 1024
NF = FF // P
NE, TOPK, INTER = 16, 4, 128
ROUTE_SCALE = 2.5
EPS = 1e-5
NEG = -1e30
BIG = 3e38
NPAIR = H // 2
PAIRS = 4

PER = dict(
    x_in=16, var=4, rstd=4, normed=2 * NT, turned=2 * NK, evened=2 * NK, x_free=1, a_final=1, own_a=24,
    pooled=1, q_ps=2, k_ps=2, v_ps=2, rq_ps=1, rkv_ps=1, q_hi=2, k_hi=2, q_lo=2, k_lo=2, v_sb=2, rq_sb=1, rk_sb=1,
    lat_ps=2, lat_sub=2, lat_exp=2, lat_turned=NT, lat_probs=NT, lat_out=1, lat_normed=1, lat_nt=1, lat_nt_sb=1,
    remote_ps=1, remote=1, remote_gr=1,
    stack_q=NPAIR, stack_k=NPAIR, stq_sb=NPAIR, stk_sb=NPAIR, scores=NPAIR * NT, negmax=NPAIR * NT,
    probs=NPAIR * NT, p_turned=NPAIR * NT, p_sb=NPAIR * NT, local_ps=NPAIR, local_raw=NPAIR,
    loc=1, diff=1, gate_z=1, gate_e=1, mixed=1, mixed_t=2, mixed_sb=2, out_ps=1,
    f_lo=1, h_ps=NF, g_hi=NF, g_lo=NF, f_y=NF, fy_sb=2, fy_tok=1,
    r_var=2, r_rstd=2, r_normed=NT, r_turned=NK, r_xt=NK, mix=8, proj=8, v_f=2, v_lo=1, k_f=2, dec=2, decay=1, r_f=2,
    rb=1, bonus_ps=1, bonus=1, v_bc=2 * HD, kv=2 * HD, state=2 * HD, rs=2 * HD, rs_hi=2 * HD, rs_lo=2 * HD, summed=2 * HD, o_sb=2, o_tok=1, o_diff=1, o_sq=1,
    o_var=1, o_rstd=1, o_norm=1, o_back=1, o_aff=2, y_in=1, w_ps=1, x_final=1, x_out=16, own_b=3, own_c=6, x_kept=1,
)

N_SCAN = 2 * HD
N_LOC = NPAIR * NT
STEPS_A = (["norm1", "turn1", "q", "k", "v", "lat_scores", "lat_turn0", "lat_turn1", "lat_out", "lat_nt", "remote", "scores0"]
           + [f"local{n}" for n in range(N_LOC + 1)] + ["gate", "mix", "out", "resid1", "norm2", "turn2"]
           + [f"ffn{f}" for f in range(NF + 2)] + ["ffn_y", "ffn_tok", "resid2"])
STEPS_HEAD = (["rnorm", "rturn", "rmix0", "rmix1", "rmix2", "rmix3", "rproj0", "rproj1", "rproj2", "rproj3", "rbonus", "rspread"]
              + [f"scan{n}" for n in range(N_SCAN + 2)])
STEPS_TAIL = ["o_tok", "o_var", "wait0", "wait1", "wait2", "wait3", "wait4", "wait5", "o_norm", "o_back", "o_out", "rresid"]

ORDER = dict(
    tensor="aararaarrrrrararaaraararrararararararararararararararaaraarraarararaaararararaararaarraararrraararaaaaaaaaaarraaarrrrrrrrr",
    vector="araararrraraaaarrrraararrrarararararararararararararaararaarraaraararaararararaaararaararrraaarraraarrrrraaaaarraaaarararr",
    scalar="aaarrararrrrarraaararaaarrrrararaararraarraararraaraarraaraararraaraaararraararaaaarrraaarrrraaaraaraaaaaaaaaaarrrrrrrrrrr",
    gpsimd="aarrarrrrrraaraaaaraaraaaaaaaaaaarrrarrrrrrarrrrraaaaaaaaaaaraaaaaaaaarrrrrrrrrrrrrraarrraarraaaaaaaaaaaaarrarrarrrrrrrrra",
)


def weave(order, attention, rwkv):
    steps = {"a": [(name, g) for names, g in attention for name in names],
             "r": [(name, g) for names, g in rwkv for name in names]}
    short = {c: order.count(c) - len(left) for c, left in steps.items()}
    for c in order:
        if short[c]:
            short[c] -= 1
            continue
        name, stream = steps[c].pop(0)
        assert next(stream) == name, name
    assert not steps["a"] and not steps["r"]


def batches_woven(eng, order, attention_ffn, rwkv_head, rwkv_tail):
    weave(order, [(STEPS_A, attention_ffn(0))], [])
    with eng.Fori(1, B) as b:
        weave(order, [(STEPS_A, attention_ffn(b))], [(STEPS_HEAD, rwkv_head(b - 1)), (STEPS_TAIL, rwkv_tail(b - 1))])
    weave(order, [], [(STEPS_HEAD, rwkv_head(B - 1)), (STEPS_TAIL, rwkv_tail(B - 1))])


def program(nc, t, out):
    x3 = nc.dram_tensor("x_after_rwkv", (B, S, D), F32, kind="Internal").ap()
    mid_token_layers(nc, t, x3)
    expert_layer(nc, t, x3, out)


class Own:

    def __init__(self, eng, sem, per):
        self.eng, self.sem, self.per, self.n, self.base = eng, sem, per, 0, 0

    def start(self, b):
        self.base, self.n = b * self.per, 0

    def link(self, ins, tick=None):
        self.n += 1
        ins.then_inc(self.sem, 1)
        self.eng.wait_ge(self.sem, self.base + self.n)
        if tick is not None:
            self.eng.memset(tick, 0.0)

    def end(self):
        assert self.n == self.per, f"{self.n} links in a batch, not {self.per}"


def mid_token_layers(nc, t, x3):
    with ExitStack() as ctx:
        def sb(name, shape, dt=F32):
            return ctx.enter_context(nc.sbuf_tensor(name, shape, dt))

        bank = [ctx.enter_context(nc.psum_tensor(f"bank{i}", [P, 512], F32)) for i in range(8)]
        sem = {n: ctx.enter_context(nc.semaphore(n)) for n in PER}
        loaded = ctx.enter_context(nc.semaphore("loaded"))
        const_ready = ctx.enter_context(nc.semaphore("const_ready"))
        tern_sum = ctx.enter_context(nc.semaphore("tern_sum"))
        tern_tot = ctx.enter_context(nc.semaphore("tern_tot"))
        setup_own = ctx.enter_context(nc.semaphore("setup_own"))
        s_zero = ctx.enter_context(nc.semaphore("s_zero"))
        act_own = ctx.enter_context(nc.semaphore("act_own"))

        ident = sb("ident", [P, P])
        ident_b = sb("ident_b", [P, P], BF16)
        blockones = sb("blockones", [P, P])
        sel_band = sb("sel_band", [P, HD + P], F32R)
        sel_v = sb("sel_v", [P, HD, P], F32R)
        sel_qk = sb("sel_qk", [P, PAIRS, 4, P], F32R)
        parmask = sb("parmask", [P, 2])
        lhmask = sb("lhmask", [LD, LH])
        lmask = sb("lmask", [P, NT, LH * NLAT], BF16)
        wmask = sb("wmask", [P, 2, 2 * P], BF16)
        row_loc = sb("row_loc", [P, NT, H])
        row_lat = sb("row_lat", [P, NT, LH])
        wqkv = sb("wqkv", [P, NK, 3 * D])
        qkb = sb("qkb", [P, 4])
        wrq = sb("wrq", [P, NK, LD])
        rqb = sb("rqb", [LD, 1])
        wrkv = sb("wrkv", [P, NK, 2 * LD])
        rkb = sb("rkb", [LD, 1])
        rvb = sb("rvb", [LD, LD])
        wrout = sb("wrout", [LD, D])
        wout = sb("wout", [P, NK, D])
        vb = sb("vb", [P, D])
        routb = sb("routb", [P, D])
        outb = sb("outb", [P, D])
        glr = sb("glr", [P, 2, HD])
        w1t = sb("w1t", [P, NK, FF], F32R)
        w2t = sb("w2t", [P, NF, D], F32R)
        b1 = sb("b1", [P, NF])
        b2 = sb("b2", [P, NK])
        wrk = sb("wrk", [P, 5, NK, D])
        tm = sb("tm", [P, 4, NK])
        u_c = sb("u_c", [P, NK])
        lnwb = sb("lnwb", [P, 2])
        mhalf = sb("mhalf", [P, 64])
        tick = sb("tick", [P, 1])[:]

        x_new = sb("x_new", [P, NT, D])
        x_tok = sb("x_tok", [P, NT, D])
        xT = sb("xT", [P, NK, S])
        st = sb("st", [P, 2, NT, 6])
        mv = sb("mv", [P, 2, NT, 2])
        vare = sb("vare", [P, 2, NT])
        rstd = sb("rstd", [P, 2, NT])
        hiT = sb("hiT", [P, 4, S], F32R)
        loT = sb("loT", [P, 4, S], F32R)
        work = sb("work", [P, 12, S])
        stq = sb("stq", [P, 2, S], F32R)
        stk = sb("stk", [P, 2, 2, S], F32R)
        rsum = sb("rsum", [P, NT, H])
        rinv = sb("rinv", [P, NT, H])
        nmx = sb("nmx", [P, N_LOC, 2])
        small = sb("small", [P, 6, 64])
        pt = sb("pt", [P, 2, 512])
        probs = sb("probs", [P, 4, 512])
        v_tok = sb("v_tok", [P, NT, D])
        poolx = sb("poolx", [P, 2, NK, NLAT])
        rk_bd = sb("rk_bd", [LD, LH, NLAT])
        rv_sb = sb("rv_sb", [LD, LD])

        x_b = sb("x_b", [P, NT, D])
        r_xT = sb("r_xT", [P, NK, S + 2])
        r_work = sb("r_work", [P, 12, S])
        r_small = sb("r_small", [P, 5, 64])
        v_hi = sb("v_hi", [P, NK, S], F32R)
        v_lo = sb("v_lo", [P, NK, S], F32R)
        kvb = sb("kvb", [P, 2, S])
        s_buf = sb("s_buf", [P, 2, S + 2])
        p_buf = sb("p_buf", [P, 2, S])
        p_hi = sb("p_hi", [P, 2, S], F32R)
        p_lo = sb("p_lo", [P, 2, S], F32R)
        ones = s_buf[:, 0, 0:P]

        xn, y_tok = work[:, 10:12, :], work[:, 0:2, :]
        r_xn = r_work[:, 0:2, :]
        as_tiles = lambda a: a.rearrange("p a (c d) -> p (a c) d", d=D)
        heads = lambda a: a.rearrange("p a (h d) -> p (a h) d", d=HD)
        A0, A1, A2, A3, A4, R0, R1, R2 = bank
        RB = (R0, R1, R2)

        def sel_o(j):
            return sel_band[:, HD - j:HD - j + P]

        def at(b, name, k):
            return b * PER[name] + k

        raw = work[:, :, :].rearrange("p a s -> p (a s)")
        n_load = [0]

        block = ctx.enter_context(nc.Block())

        def bc(ap, *shape):
            return ap.broadcast_to(shape)

        @block.sync
        def _(sp):
            def load(dst, src):
                n_load[0] += 1
                sp.dma_start(dst, src).then_inc(loaded, 16)
            load(ident[:], t["c_ident"])
            load(blockones[:], t["c_blockones"])
            load(ones, t["c_ones"])
            load(parmask[:], t["c_parmask"])
            load(lhmask[:], t["c_lhmask"])
            load(row_loc[:], t["c_rowloc"])
            load(row_lat[:], t["c_rowlat"])
            load(mhalf[:], t["c_mhalf"])
            load(wqkv[:], t["wqkv"].rearrange("(k p) n -> p k n", p=P))
            load(qkb[:], t["qkb"])
            load(wrq[:], t["wrq"].rearrange("(k p) n -> p k n", p=P))
            load(rqb[:], t["rqb"])
            load(wrkv[:], t["wrkv"].rearrange("(k p) n -> p k n", p=P))
            load(rkb[:], t["rkb"])
            load(rvb[:], t["rvb"].partition_broadcast(LD))
            load(wrout[:], t["wrout"])
            load(wout[:], t["wout"].rearrange("(k p) n -> p k n", p=P))
            load(vb[:], t["vb"].partition_broadcast(P))
            load(routb[:], t["routb"].partition_broadcast(P))
            load(outb[:], t["outb"].partition_broadcast(P))
            load(glr[:, 0, :], t["gl"].partition_broadcast(P))
            load(glr[:, 1, :], t["gr"].partition_broadcast(P))
            load(b1[:], t["b1"])
            load(b2[:], t["b2"])
            load(wrk[:], t["wrk"].rearrange("w (k p) n -> p w k n", p=P))
            load(tm[:], t["tm"])
            load(u_c[:], t["u"])
            load(lnwb[:], t["lnwb"])
            load(raw[:, 0:2048], t["w1"].rearrange("(k p) n -> p k n", p=P))
            load(raw[:, 2048:4096], t["w2"].rearrange("(k p) n -> p k n", p=P))
            load(raw[:, 4096:6144], t["c_selv"])
            load(xT[:, 0, :], t["c_wmask"])
            load(xT[:, 1, 0:HD + P], t["c_selo"])
            load(x_tok[:].rearrange("p a d -> p (a d)"), t["c_lmask"])
            load(probs[:].rearrange("p a d -> p (a d)"), t["c_selqk"])
            rows = lambda ap: ap.rearrange("o (t p) d -> p (o t) d", p=P)

            def next_x(b):
                sp.wait_ge(sem["x_free"], at(b, "x_free", 1))
                sp.dma_start(x_new[:], rows(t["x"][bass.ds(b + 1, 1)])).then_inc(sem["x_in"], 16)

            def store(b):
                sp.wait_ge(sem["x_final"], at(b, "x_final", 1))
                sp.dma_start(rows(x3[bass.ds(b, 1)]), x_b[:]).then_inc(sem["x_out"], 16)

            sp.dma_start(x_new[:], rows(t["x"][0:1])).then_inc(sem["x_in"], 16)
            next_x(0)
            with sp.Fori(1, B - 1) as b:
                next_x(b)
                store(b - 1)
            store(B - 2)
            store(B - 1)
            sp.wait_ge(sem["x_out"], B * 16)

        @block.vector
        def _(ve):
            V = nc.vector
            own = Own(ve, setup_own, 0)
            ve.wait_ge(loaded, 16 * n_load[0])
            V.tensor_copy(ident_b[:], ident[:])
            V.tensor_copy(sel_v[:].rearrange("p a m -> p (a m)"), raw[:, 4096:6144])
            V.tensor_copy(sel_band[:], xT[:, 1, 0:HD + P])
            V.tensor_copy(wmask[:].rearrange("p a m -> p (a m)"), xT[:, 0, 0:512])
            V.tensor_copy(lmask[:].rearrange("p a m -> p (a m)"), x_tok[:].rearrange("p a d -> p (a d)"))
            V.tensor_copy(sel_qk[:].rearrange("p a c m -> p (a c m)"), probs[:].rearrange("p a d -> p (a d)"))
            V.tensor_scalar(qkb[:, 0:2], qkb[:, 0:2], 0.25, None, ALU.mult)
            V.tensor_scalar(wqkv[:, :, 0:D], wqkv[:, :, 0:D], 0.25, None, ALU.mult)
            for i in range(2):
                V.tensor_reduce(small[:, i, 0:1], raw[:, 2048 * i:2048 * i + 2048], X, ALU.add,
                                apply_absolute_value=True).then_inc(tern_sum, 1)
            ve.wait_ge(tern_tot, 1)
            for i in range(2):
                own.link(V.tensor_scalar(small[:, i, 1:2], bank[0][:, i:i + 1], 1.0 / (FF * D), 1e-8, ALU.mult, ALU.max))
                own.link(V.tensor_scalar(small[:, i, 2:3], small[:, i, 1:2], 0.5, None, ALU.mult))
                own.link(V.tensor_scalar(small[:, i, 3:4], small[:, i, 1:2], -0.5, None, ALU.mult))
                w = raw[:, 2048 * i:2048 * i + 2048]
                neg = hiT[:].rearrange("p a s -> p (a s)")
                dst = (w1t, w2t)[i][:].rearrange("p a s -> p (a s)")
                own.link(V.tensor_scalar(neg, w, small[:, i, 3:4], None, ALU.is_lt))
                own.link(V.scalar_tensor_tensor(dst, w, small[:, i, 2:3], neg.bitcast(F32), ALU.is_gt, ALU.subtract))
            V.memset(r_xT[:, :, 0:1], 0.0).then_inc(const_ready, 1)

            def stats(b, own, side, n, src):
                for i in range(NT):
                    ins = V.bn_stats(st[:, side, i, :], src(i))
                own.link(ins, tick)
                for i in range(NT):
                    ins = V.bn_aggr(mv[:, side, i, :], st[:, side, i, :])
                own.link(ins)
                V.tensor_scalar(vare[:, side], mv[:, side, :, 1], EPS, None, ALU.add).then_inc(sem[("var", "r_var")[side]], 1)
                rs = ("rstd", "r_rstd")[side]
                ve.wait_ge(sem[rs], at(b, rs, n))

            def normalize(side, dst, src, name):
                for i in range(NT):
                    ins = V.tensor_scalar(as_tiles(dst)[:, i, :], src(i), mv[:, side, i, 0:1], rstd[:, side, i:i + 1],
                                          ALU.subtract, ALU.mult)
                    if name:
                        ins.then_inc(sem[name], 1)
                return ins

            def attention_ffn(b):
                own = Own(ve, sem["own_a"], PER["own_a"])
                own.start(b)
                ve.wait_ge(sem["x_in"], at(b, "x_in", 16))
                stats(b, own, 0, 1, lambda i: x_new[:, i, :])
                normalize(0, xn, lambda i: x_new[:, i, :], "normed")
                yield "norm1"
                ve.wait_ge(sem["evened"], at(b, "evened", 2))
                own.link(V.tensor_reduce(poolx[:, 0], xT[:].rearrange("p k (l c) -> p k l c", c=CHUNK), X, ALU.add))
                V.tensor_scalar(poolx[:, 1], poolx[:, 0], 1.0 / CHUNK, None, ALU.mult).then_inc(sem["pooled"], 1)
                yield "turn1"

                def low(hi, lo, i, src):
                    ve.wait_ge(sem[hi], at(b, hi, i % 2 + 1))
                    V.scalar_tensor_tensor(loT[:, i, :], src[:], qkb[:, i:i + 1], hiT[:, i, :].bitcast(F32),
                                           ALU.add, ALU.subtract).then_inc(sem[lo], 1)

                low("q_hi", "q_lo", 0, A2)
                low("q_hi", "q_lo", 1, A3)
                yield "q"

                def v_out(i, src):
                    ve.wait_ge(sem["v_ps"], at(b, "v_ps", i + 1))
                    V.tensor_tensor(v_tok[:, 2 * i:2 * i + 2, :], src[:].rearrange("p (a d) -> p a d", a=2),
                                    bc(vb[:].unsqueeze(1), P, 2, D), ALU.add).then_inc(sem["v_sb"], 1)

                low("k_hi", "k_lo", 2, A0)
                low("k_hi", "k_lo", 3, A1)
                v_out(0, A4)
                yield "k"
                v_out(1, A2)
                ve.wait_ge(sem["rkv_ps"], at(b, "rkv_ps", 1))
                for h in range(LH):
                    V.tensor_scalar(rk_bd[:, h, :], A4[0:LD, 0:NLAT], rkb[:, 0:1], lhmask[:, h:h + 1], ALU.add, ALU.mult)
                V.tensor_tensor(rv_sb[:], A4[0:NLAT, NLAT:NLAT + LD], rvb[:], ALU.add).then_inc(sem["rk_sb"], 1)
                yield "v"

                lsub, lexp = work[:, 0:2, :], work[:, 2:4, :]
                for i, src in enumerate((A0, A1)):
                    ve.wait_ge(sem["lat_ps"], at(b, "lat_ps", i + 1))
                    ps = src[:].rearrange("p (a l) -> p a l", l=NLAT)
                    own.link(V.tensor_reduce(small[:, 0, 8 * i:8 * i + 8], ps, X, ALU.max))
                    V.tensor_tensor(lsub[:, i, :].rearrange("p (a l) -> p a l", l=NLAT), ps,
                                    bc(small[:, 0, 8 * i:8 * i + 8].unsqueeze(2), P, 8, NLAT), ALU.subtract
                                    ).then_inc(sem["lat_sub"], 1)
                yield "lat_scores"
                ve.wait_ge(sem["lat_exp"], at(b, "lat_exp", 2))
                own.link(V.tensor_reduce(small[:, 1, 0:16], lexp.rearrange("p a (h l) -> p (a h) l", l=NLAT), X, ALU.add))
                own.link(V.reciprocal(small[:, 2, 0:16], small[:, 1, 0:16]))
                own.link(V.tensor_tensor(small[:, 3, 0:16], small[:, 2, 0:16], row_lat[:].rearrange("p a h -> p (a h)"), ALU.mult))
                yield "lat_turn0"
                yield "lat_turn1"
                ve.wait_ge(sem["lat_out"], at(b, "lat_out", 1))
                V.tensor_tensor(work[:, 4, 0:256].rearrange("p (a d) -> p a d", d=16), A4[:, 0:256].rearrange("p (a d) -> p a d", d=16),
                                bc(small[:, 3, 0:16].unsqueeze(2), P, 16, 16), ALU.mult).then_inc(sem["lat_normed"], 1)
                yield "lat_out"
                yield "lat_nt"

                def stack_k(p):
                    ve.wait_ge(sem["stack_k"], at(b, "stack_k", p + 1))
                    for par in range(2):
                        ins = V.tensor_scalar(stk[:, p % 2, par, :], A4[:], parmask[:, par:par + 1], None, ALU.mult)
                    ins.then_inc(sem["stk_sb"], 1)

                def negmax(n):
                    w = P if n % NT == 0 else 2 * P
                    ve.wait_ge(sem["scores"], at(b, "scores", n + 1))
                    V.tensor_reduce(nmx[:, n, :], bank[n % 2][:, 0:2 * w].rearrange("p (h k) -> p h k", h=2), X, ALU.max,
                                    negate=True).then_inc(sem["negmax"], 1)

                rem = work[:, 6:8, :]
                ve.wait_ge(sem["remote_ps"], at(b, "remote_ps", 1))
                for i, src in enumerate((A2, A3)):
                    ins = V.tensor_tensor(rem[:, i, :].rearrange("p (a d) -> p a d", a=2), src[:].rearrange("p (a d) -> p a d", a=2),
                                          bc(routb[:].unsqueeze(1), P, 2, D), ALU.add)
                ins.then_inc(sem["remote"], 1)
                stack_k(0)
                yield "remote"
                negmax(0)
                negmax(1)
                yield "scores0"
                loc_raw = work[:, 8:10, :]
                for n in range(N_LOC + 1):
                    if n + 2 < N_LOC:
                        negmax(n + 2)
                    if n % NT == 1 and n // NT + 1 < NPAIR:
                        stack_k(n // NT + 1)
                    if n and n % NT == 0:
                        p = n // NT - 1
                        ve.wait_ge(sem["local_ps"], at(b, "local_ps", p + 1))
                        V.tensor_copy(as_tiles(loc_raw)[:, :, 32 * p:32 * p + 32], A3[:, 0:128].rearrange("p (a d) -> p a d", d=32)
                                      ).then_inc(sem["local_raw"], 1)
                    yield f"local{n}"
                ve.wait_ge(sem["local_raw"], at(b, "local_raw", NPAIR))
                own.link(V.reciprocal(rinv[:], rsum[:]))
                own.link(V.tensor_tensor(rinv[:], rinv[:], row_loc[:], ALU.mult))
                loc, c1 = work[:, 0:2, :], work[:, 2:4, :]
                V.tensor_tensor(heads(loc), heads(loc_raw), bc(rinv[:].rearrange("p a h -> p (a h)").unsqueeze(2), P, 64, HD), ALU.mult
                                ).then_inc(sem["loc"], 1)
                ve.wait_ge(sem["loc"], at(b, "loc", 1))
                own.link(V.tensor_tensor(heads(c1), heads(loc), bc(glr[:, 0, :].unsqueeze(1), P, 64, HD), ALU.mult))
                ve.wait_ge(sem["remote_gr"], at(b, "remote_gr", 1))
                own.link(V.tensor_tensor(c1, c1, work[:, 10:12, :], ALU.add))
                V.tensor_reduce(small[:, 4, :], heads(c1), X, ALU.add).then_inc(sem["gate_z"], 1)
                yield "gate"
                ve.wait_ge(sem["gate_e"], at(b, "gate_e", 1))
                own.link(V.tensor_scalar(small[:, 5, :], small[:, 5, :], 1.0, None, ALU.add))
                own.link(V.reciprocal(small[:, 5, :], small[:, 5, :]))
                ve.wait_ge(sem["diff"], at(b, "diff", 1))
                own.link(V.tensor_tensor(heads(c1), heads(work[:, 4:6, :]), bc(small[:, 5, :].unsqueeze(2), P, 64, HD), ALU.mult))
                V.tensor_tensor(c1, c1, rem, ALU.add).then_inc(sem["mixed"], 1)
                yield "mix"
                ve.wait_ge(sem["out_ps"], at(b, "out_ps", 1))
                yt = as_tiles(y_tok)
                for i, src in enumerate((A2, A3)):
                    ins = V.tensor_tensor(yt[:, 2 * i:2 * i + 2, :], src[:].rearrange("p (a d) -> p a d", a=2),
                                          bc(outb[:].unsqueeze(1), P, 2, D), ALU.add)
                own.link(ins)
                stats(b, own, 0, 2, lambda i: yt[:, i, :])
                yield "out"
                own.link(normalize(0, xn, lambda i: yt[:, i, :], None))
                if not (isinstance(b, int) and b == 0):
                    ve.wait_ge(sem["x_kept"], at(b, "x_kept", 0))
                V.tensor_tensor(x_tok[:], x_new[:], as_tiles(xn), ALU.add).then_inc(sem["x_free"], 1)
                yield "resid1"
                ve.wait_ge(sem["x_free"], at(b, "x_free", 1))
                stats(b, own, 0, 3, lambda i: x_tok[:, i, :])
                normalize(0, xn, lambda i: x_tok[:, i, :], "normed")
                yield "norm2"

                ve.wait_ge(sem["evened"], at(b, "evened", 4))
                for k, src in enumerate((A0, A1)):
                    ins = V.tensor_tensor(loT[:, k, :], src[:], hiT[:, k, :].bitcast(F32), ALU.subtract)
                ins.then_inc(sem["f_lo"], 1)
                yield "turn2"
                for f in range(NF + 2):
                    if f < NF:
                        ve.wait_ge(sem["g_hi"], at(b, "g_hi", f + 1))
                        V.tensor_tensor(stk[:, 0, f % 2, :], work[:, f % 2, :], stq[:, f % 2, :].bitcast(F32), ALU.subtract
                                        ).then_inc(sem["g_lo"], 1)
                    yield f"ffn{f}"
                yield "ffn_y"
                tok = lambda i: (A0, A1)[i // 2][:, (i % 2) * D:(i % 2) * D + D]
                ve.wait_ge(sem["fy_tok"], at(b, "fy_tok", 1))
                stats(b, own, 0, 4, tok)
                yield "ffn_tok"
                own.link(normalize(0, xn, tok, None))
                V.tensor_tensor(x_tok[:], x_tok[:], as_tiles(xn), ALU.add).then_inc(sem["a_final"], 1)
                own.end()
                yield "resid2"

            def rwkv_head(b):
                own = Own(ve, sem["own_b"], PER["own_b"])
                own.start(b)
                ve.wait_ge(sem["a_final"], at(b, "a_final", 1))
                stats(b, own, 1, 1, lambda i: x_tok[:, i, :])
                normalize(1, r_xn, lambda i: x_tok[:, i, :], "r_normed")
                yield "rnorm"
                ve.wait_ge(sem["r_xt"], at(b, "r_xt", 2))
                dx = r_work[:, 0:2, :]
                own.link(V.tensor_tensor(dx, r_xT[:, :, 1:S + 1], r_xT[:, :, 0:S], ALU.subtract))
                yield "rturn"
                for w in range(4):
                    for k in range(NK):
                        V.scalar_tensor_tensor(r_work[:, 2 + 2 * w + k, :], dx[:, k, :], tm[:, w, k:k + 1], r_xT[:, k, 0:S],
                                               ALU.mult, ALU.add).then_inc(sem["mix"], 1)
                    yield f"rmix{w}"
                vf, kf, ek, dec, rf = (r_work[:, i:i + 2, :] for i in (0, 2, 4, 6, 8))
                for g in range(2):
                    ve.wait_ge(sem["v_f"], at(b, "v_f", g + 1))
                    ins = V.tensor_tensor(v_lo[:, g, :], vf[:, g, :], v_hi[:, g, :].bitcast(F32), ALU.subtract)
                ins.then_inc(sem["v_lo"], 1)
                yield "rproj0"
                yield "rproj1"
                yield "rproj2"
                ve.wait_ge(sem["dec"], at(b, "dec", 2))
                V.tensor_scalar(dec, dec, 0.9999000049998333, None, ALU.mult).then_inc(sem["decay"], 1)
                ve.wait_ge(sem["r_f"], at(b, "r_f", 2))
                V.tensor_tensor(r_work[:, 10:12, :], rf, ek, ALU.mult).then_inc(sem["rb"], 1)
                yield "rproj3"
                o_f = r_work[:, 10:12, :]
                ve.wait_ge(sem["bonus_ps"], at(b, "bonus_ps", 1))
                for g, src in enumerate((R1, R2)):
                    ins = V.tensor_tensor(o_f[:, g, :], vf[:, g, :], src[:], ALU.mult)
                ins.then_inc(sem["bonus"], 1)
                yield "rbonus"

                def kv(n):
                    ve.wait_ge(sem["v_bc"], at(b, "v_bc", n + 1))
                    if n >= 2:
                        ve.wait_ge(sem["state"], at(b, "state", n - 1))
                    V.tensor_tensor(kvb[:, n % 2, :], kf[:, n // HD, :], RB[n % 2][:], ALU.mult).then_inc(sem["kv"], 1)

                kv(0)
                yield "rspread"
                for n in range(N_SCAN + 2):
                    if n + 1 < N_SCAN:
                        kv(n + 1)
                    if n < N_SCAN:
                        ve.wait_ge(sem["kv"], at(b, "kv", n + 1))
                        if n >= 2:
                            ve.wait_ge(sem["rs"], at(b, "rs", n - 1))
                        V.tensor_tensor_scan(s_buf[:, n % 2, 1:S + 1], dec[:, n // HD, :], kvb[:, n % 2, :], 0.0, ALU.mult, ALU.add
                                             ).then_inc(sem["state"], 1)
                    if n > 1 and n % HD == 1:
                        g = n // HD - 1
                        ve.wait_ge(sem["summed"], at(b, "summed", n - 1))
                        ve.wait_ge(sem["bonus"], at(b, "bonus", 1))
                        V.tensor_tensor(o_f[:, g, :], o_f[:, g, :], R2[:], ALU.add).then_inc(sem["o_sb"], 1)
                    if n == N_SCAN + 1:
                        own.end()
                    yield f"scan{n}"

            def rwkv_tail(b):
                own = Own(ve, sem["own_c"], PER["own_c"])
                own.start(b)
                rf = r_work[:, 8:10, :]
                ve.wait_ge(sem["o_tok"], at(b, "o_tok", 1))
                od, osq, on = r_work[:, 4:6, :], r_work[:, 6:8, :], r_work[:, 2:4, :]
                for i, src in enumerate((R0, R1)):
                    ins = V.tensor_reduce(r_small[:, 0, 32 * i:32 * i + 32], src[:].rearrange("p (a d) -> p a d", d=HD), X, ALU.add)
                own.link(ins)
                own.link(V.tensor_scalar(r_small[:, 1, :], r_small[:, 0, :], 1.0 / HD, None, ALU.mult))
                for i, src in enumerate((R0, R1)):
                    ins = V.tensor_tensor(od[:, i, :].rearrange("p (a d) -> p a d", d=HD), src[:].rearrange("p (a d) -> p a d", d=HD),
                                          bc(r_small[:, 1, 32 * i:32 * i + 32].unsqueeze(2), P, 32, HD), ALU.subtract)
                ins.then_inc(sem["o_diff"], 1)
                yield "o_tok"
                ve.wait_ge(sem["o_sq"], at(b, "o_sq", 1))
                own.link(V.tensor_reduce(r_small[:, 2, :], heads(osq), X, ALU.add))
                V.tensor_scalar(r_small[:, 3, :], r_small[:, 2, :], 1.0 / HD, EPS, ALU.mult, ALU.add).then_inc(sem["o_var"], 1)
                yield "o_var"
                for i in range(6):
                    yield f"wait{i}"
                ve.wait_ge(sem["o_rstd"], at(b, "o_rstd", 1))
                V.tensor_tensor(heads(on), heads(od), bc(r_small[:, 4, :].unsqueeze(2), P, 64, HD), ALU.mult).then_inc(sem["o_norm"], 1)
                yield "o_norm"
                ve.wait_ge(sem["o_aff"], at(b, "o_aff", 2))
                V.tensor_tensor(r_work[:, 6:8, :], r_work[:, 4:6, :], rf, ALU.mult).then_inc(sem["y_in"], 1)
                yield "o_back"
                rtok = lambda i: (R1, R2)[i // 2][:, (i % 2) * D:(i % 2) * D + D]
                ve.wait_ge(sem["w_ps"], at(b, "w_ps", 1))
                stats(b, own, 1, 2, rtok)
                yield "o_out"
                own.link(normalize(1, r_xn, rtok, None))
                V.tensor_tensor(x_b[:], x_b[:], as_tiles(r_xn), ALU.add).then_inc(sem["x_final"], 1)
                own.end()
                yield "rresid"

            batches_woven(ve, ORDER["vector"], attention_ffn, rwkv_head, rwkv_tail)

        @block.gpsimd
        def _(gp):
            G = nc.gpsimd
            gp.wait_ge(tern_tot, 1)
            G.memset(s_buf[:, :, 0:1], 0.0).then_inc(s_zero, 1)
            gp.wait_ge(const_ready, 1)

            def root(b, side, n):
                v, r = (("var", "rstd"), ("r_var", "r_rstd"))[side]
                gp.wait_ge(sem[v], at(b, v, n))
                G.tensor_tensor(rstd[:, side], vare[:, side], mhalf[:, 0:NT], ALU.pow).then_inc(sem[r], 1)

            def attention_ffn(b):
                for name in STEPS_A:
                    if name == "norm1":
                        root(b, 0, 1)
                    if name == "scores0":
                        gp.wait_ge(sem["remote"], at(b, "remote", 1))
                        G.tensor_tensor(heads(work[:, 10:12, :]), heads(work[:, 6:8, :]), bc(glr[:, 1, :].unsqueeze(1), P, 64, HD), ALU.mult
                                        ).then_inc(sem["remote_gr"], 1)
                    if name == "gate":
                        gp.wait_ge(sem["loc"], at(b, "loc", 1))
                        G.tensor_tensor(work[:, 4:6, :], work[:, 0:2, :], work[:, 6:8, :], ALU.subtract).then_inc(sem["diff"], 1)
                    if name == "out":
                        root(b, 0, 2)
                    if name == "norm2":
                        root(b, 0, 3)
                    if name == "ffn_tok":
                        root(b, 0, 4)
                    yield name

            def rwkv_head(b):
                rf = r_work[:, 8:10, :]
                for name in STEPS_HEAD:
                    if name == "rnorm":
                        root(b, 1, 1)
                    if name == "scan0":
                        gp.wait_ge(s_zero, 1)
                        gp.wait_ge(sem["r_f"], at(b, "r_f", 2))
                    n = int(name[4:]) if name.startswith("scan") else -1
                    if 0 <= n < N_SCAN:
                        gp.wait_ge(sem["state"], at(b, "state", n + 1))
                        if n >= 2:
                            gp.wait_ge(sem["rs_lo"], at(b, "rs_lo", n - 1))
                        G.tensor_tensor(p_buf[:, n % 2, :], s_buf[:, n % 2, 0:S], rf[:, n // HD, :], ALU.mult).then_inc(sem["rs"], 1)
                    if 1 <= n <= N_SCAN:
                        gp.wait_ge(sem["rs_hi"], at(b, "rs_hi", n))
                        m = (n - 1) % 2
                        G.tensor_tensor(p_lo[:, m, :], p_buf[:, m, :], p_hi[:, m, :].bitcast(F32), ALU.subtract).then_inc(sem["rs_lo"], 1)
                    yield name

            def rwkv_tail(b):
                for name in STEPS_TAIL:
                    if name == "o_var":
                        gp.wait_ge(sem["o_var"], at(b, "o_var", 1))
                        G.tensor_tensor(r_small[:, 4, :], r_small[:, 3, :], mhalf[:], ALU.pow).then_inc(sem["o_rstd"], 1)
                    if name == "o_out":
                        root(b, 1, 2)
                    yield name

            batches_woven(gp, ORDER["gpsimd"], attention_ffn, rwkv_head, rwkv_tail)

        @block.scalar
        def _(sc):
            A = nc.scalar.activation
            sc.wait_ge(const_ready, 1)

            def attention_ffn(b):
                yield "norm1"
                for k, src in enumerate((A0, A1)):
                    sc.wait_ge(sem["turned"], at(b, "turned", k + 1))
                    A(xT[:, k, :], src[:], ACT.Copy).then_inc(sem["evened"], 1)
                yield "turn1"
                for i, src in enumerate((A2, A3)):
                    sc.wait_ge(sem["q_ps"], at(b, "q_ps", i + 1))
                    A(hiT[:, i, :], src[:], ACT.Identity, bias=qkb[:, i:i + 1]).then_inc(sem["q_hi"], 1)
                yield "q"
                for i, src in enumerate((A0, A1)):
                    sc.wait_ge(sem["k_ps"], at(b, "k_ps", i + 1))
                    A(hiT[:, 2 + i, :], src[:], ACT.Identity, bias=qkb[:, 2 + i:3 + i]).then_inc(sem["k_hi"], 1)
                yield "k"
                sc.wait_ge(sem["rq_ps"], at(b, "rq_ps", 1))
                A(work[0:LD, 5, :], A3[0:LD, :], ACT.Identity, bias=rqb[:, 0:1]).then_inc(sem["rq_sb"], 1)
                yield "v"
                for i in range(2):
                    sc.wait_ge(sem["lat_sub"], at(b, "lat_sub", i + 1))
                    A(work[:, 2 + i, :], work[:, i, :], ACT.Exp, scale=0.25).then_inc(sem["lat_exp"], 1)
                yield "lat_scores"
                for half in range(2):
                    for c, src in enumerate((A2, A3)):
                        i = 2 * half + c
                        sc.wait_ge(sem["lat_turned"], at(b, "lat_turned", i + 1))
                        A(work[0:NLAT, 8 + i, :], src[0:NLAT, :], ACT.Copy).then_inc(sem["lat_probs"], 1)
                    yield f"lat_turn{half}"
                yield "lat_out"

                def stack_q(p):
                    sc.wait_ge(sem["stack_q"], at(b, "stack_q", p + 1))
                    A(stq[:, p % 2, :], A4[:], ACT.Copy).then_inc(sem["stq_sb"], 1)

                def exps(n):
                    p, i = divmod(n, NT)
                    w = P if i == 0 else 2 * P
                    sc.wait_ge(sem["negmax"], at(b, "negmax", n + 1))
                    for h in range(2):
                        ins = A(probs[:, i, h * w:h * w + w], bank[n % 2][:, h * w:h * w + w], ACT.Exp, bias=nmx[:, n, h:h + 1],
                                accum_out=rsum[:, i, 2 * p + h:2 * p + h + 1])
                    ins.then_inc(sem["probs"], 1)

                sc.wait_ge(sem["lat_nt"], at(b, "lat_nt", 1))
                A(work[0:LD, 5, :], A0[0:LD, :], ACT.Copy).then_inc(sem["lat_nt_sb"], 1)
                stack_q(0)
                yield "lat_nt"
                yield "remote"
                exps(0)
                yield "scores0"
                for n in range(N_LOC + 1):
                    if n + 1 < N_LOC:
                        exps(n + 1)
                    if n % NT == 0 and n // NT + 1 < NPAIR:
                        stack_q(n // NT + 1)
                    if n < N_LOC:
                        w = 256 if n % NT == 0 else 512
                        sc.wait_ge(sem["p_turned"], at(b, "p_turned", n + 1))
                        A(pt[:, n % 2, 0:w], A2[:, 0:w], ACT.Copy).then_inc(sem["p_sb"], 1)
                    yield f"local{n}"
                sc.wait_ge(sem["gate_z"], at(b, "gate_z", 1))
                A(small[:, 5, :], small[:, 4, :], ACT.Exp, scale=-1.0).then_inc(sem["gate_e"], 1)
                yield "gate"
                for k, src in enumerate((A0, A1)):
                    sc.wait_ge(sem["mixed_t"], at(b, "mixed_t", k + 1))
                    A(work[:, 8 + k, :], src[:], ACT.Copy).then_inc(sem["mixed_sb"], 1)
                yield "mix"
                yield "out"
                yield "resid1"
                yield "norm2"
                for k, src in enumerate((A0, A1)):
                    sc.wait_ge(sem["turned"], at(b, "turned", 2 + k + 1))
                    A(hiT[:, k, :], src[:], ACT.Copy).then_inc(sem["evened"], 1)
                yield "turn2"
                for f in range(NF + 2):
                    if f < NF:
                        sc.wait_ge(sem["h_ps"], at(b, "h_ps", f + 1))
                        if f >= 2:
                            sc.wait_ge(sem["g_lo"], at(b, "g_lo", f - 1))
                        g_ins = A(work[:, f % 2, :], bank[f % 3][:], ACT.Gelu, bias=b1[:, f:f + 1])
                        g_ins.then_inc(act_own, 1)
                        if f >= 2:
                            sc.wait_ge(sem["f_y"], at(b, "f_y", f - 1))
                        sc.wait_ge(act_own, b * NF + f + 1)
                        A(stq[:, f % 2, :], work[:, f % 2, :], ACT.Copy).then_inc(sem["g_hi"], 1)
                    yield f"ffn{f}"
                sc.wait_ge(sem["f_y"], at(b, "f_y", NF))
                for k, src in enumerate((A3, A4)):
                    A(work[:, 2 + k, :], src[:], ACT.Identity, bias=b2[:, k:k + 1]).then_inc(sem["fy_sb"], 1)
                yield "ffn_y"
                yield "ffn_tok"
                yield "resid2"

            def rwkv_head(b):
                vf, kf, ek, dec, rf = (r_work[:, i:i + 2, :] for i in (0, 2, 4, 6, 8))
                sc.wait_ge(sem["a_final"], at(b, "a_final", 1))
                if not (isinstance(b, int) and b == 0):
                    sc.wait_ge(sem["x_out"], at(b, "x_out", 0))
                A(x_b[:], x_tok[:], ACT.Copy).then_inc(sem["x_kept"], 1)
                yield "rnorm"
                for k in range(NK):
                    sc.wait_ge(sem["r_turned"], at(b, "r_turned", k + 1))
                    A(r_xT[:, k, 1:S + 1], RB[k][:], ACT.Copy).then_inc(sem["r_xt"], 1)
                yield "rturn"
                for w in range(4):
                    yield f"rmix{w}"
                sc.wait_ge(sem["mix"], at(b, "mix", 8))
                for g in range(2):
                    sc.wait_ge(sem["proj"], at(b, "proj", g + 1))
                    A(v_hi[:, g, :], RB[(2 + g) % 3][:], ACT.Copy)
                    A(vf[:, g, :], RB[(2 + g) % 3][:], ACT.Copy).then_inc(sem["v_f"], 1)
                yield "rproj0"
                sc.wait_ge(sem["proj"], at(b, "proj", 4))
                for g in range(2):
                    A(kf[:, g, :], RB[(4 + g) % 3][:], ACT.Copy)
                    A(ek[:, g, :], RB[(4 + g) % 3][:], ACT.Exp, bias=u_c[:, g:g + 1]).then_inc(sem["k_f"], 1)
                yield "rproj1"
                yield "rproj2"
                sc.wait_ge(sem["proj"], at(b, "proj", 6))
                for g in range(2):
                    A(dec[:, g, :], RB[(6 + g) % 3][:], ACT.Sigmoid).then_inc(sem["dec"], 1)
                sc.wait_ge(sem["proj"], at(b, "proj", 8))
                for g in range(2):
                    A(rf[:, g, :], RB[(8 + g) % 3][:], ACT.Sigmoid).then_inc(sem["r_f"], 1)
                yield "rproj3"
                yield "rbonus"
                yield "rspread"
                for n in range(N_SCAN + 2):
                    if 1 <= n <= N_SCAN:
                        sc.wait_ge(sem["rs"], at(b, "rs", n))
                        if n >= 3:
                            sc.wait_ge(sem["summed"], at(b, "summed", n - 2))
                        A(p_hi[:, (n - 1) % 2, :], p_buf[:, (n - 1) % 2, :], ACT.Copy).then_inc(sem["rs_hi"], 1)
                    yield f"scan{n}"

            def rwkv_tail(b):
                for name in STEPS_TAIL:
                    if name == "o_tok":
                        sc.wait_ge(sem["o_diff"], at(b, "o_diff", 1))
                        A(r_work[:, 6:8, :], r_work[:, 4:6, :], ACT.Square).then_inc(sem["o_sq"], 1)
                    if name == "o_back":
                        sc.wait_ge(sem["o_back"], at(b, "o_back", 1))
                        for g, src in enumerate((R2, R0)):
                            A(r_work[:, 4 + g, :], src[:], ACT.Identity, bias=lnwb[:, 1:2], scale=lnwb[:, 0:1]).then_inc(sem["o_aff"], 1)
                    yield name

            batches_woven(sc, ORDER["scalar"], attention_ffn, rwkv_head, rwkv_tail)

        @block.tensor
        def _(pe):
            T = nc.tensor
            pe.wait_ge(loaded, 16 * n_load[0])
            pe.wait_ge(tern_sum, 2)
            for i in range(2):
                ins = T.matmul(bank[0][:, i:i + 1], ones, small[:, i, 0:1], start=True, stop=True)
            ins.then_inc(tern_tot, 1)
            pe.wait_ge(const_ready, 1)

            def turn(b, name, n, out_name, dst, src):
                for k in range(NK):
                    for i in range(NT):
                        if k == 0:
                            pe.wait_ge(sem[name], at(b, name, NT * n + i + 1))
                        ins = T.transpose(dst[k][:, i * P:(i + 1) * P], as_tiles(src)[:, i, k * P:(k + 1) * P], ident[:])
                    ins.then_inc(sem[out_name], 1)

            def project(dst, w, src, cols=P):
                for k in range(NK):
                    ins = T.matmul(dst, w[:, k, :], src[:, k, :], start=k == 0, stop=k == NK - 1)
                return ins

            def to_tokens(dst, src, w):
                for i in range(NT):
                    for k in range(NK):
                        ins = T.matmul(dst[i // 2][:, (i % 2) * D:(i % 2) * D + D], src[:, k, i * P:(i + 1) * P],
                                       w[:, k, :], start=k == 0, stop=k == NK - 1)
                return ins

            def attention_ffn(b):
                yield "norm1"
                turn(b, "normed", 0, "turned", (A0, A1), xn)
                yield "turn1"
                pe.wait_ge(sem["evened"], at(b, "evened", 2))
                for i, dst in enumerate((A2, A3)):
                    project(dst[:], wqkv[:, :, i * P:(i + 1) * P], xT[:]).then_inc(sem["q_ps"], 1)
                yield "q"
                for i, dst in enumerate((A0, A1)):
                    project(dst[:], wqkv[:, :, D + i * P:D + (i + 1) * P], xT[:]).then_inc(sem["k_ps"], 1)

                def v_tiles(i, dst):
                    for c in range(2):
                        for k in range(NK):
                            ins = T.matmul(dst[:, c * D:c * D + D], xT[:, k, (2 * i + c) * P:(2 * i + c + 1) * P],
                                           wqkv[:, k, 2 * D:3 * D], start=k == 0, stop=k == NK - 1)
                    ins.then_inc(sem["v_ps"], 1)

                v_tiles(0, A4)
                yield "k"
                pe.wait_ge(sem["q_lo"], at(b, "q_lo", 2))
                v_tiles(1, A2)
                project(A3[0:LD, :], wrq[:], xT[:]).then_inc(sem["rq_ps"], 1)
                pe.wait_ge(sem["pooled"], at(b, "pooled", 1))
                pe.wait_ge(sem["v_sb"], at(b, "v_sb", 1))
                project(A4[0:LD, 0:NLAT], wrkv[:, :, 0:LD], poolx[:, 1])
                project(A4[0:NLAT, NLAT:NLAT + LD], poolx[:, 1], wrkv[:, :, LD:2 * LD]).then_inc(sem["rkv_ps"], 1)
                yield "v"
                pe.wait_ge(sem["k_lo"], at(b, "k_lo", 2))
                pe.wait_ge(sem["rk_sb"], at(b, "rk_sb", 1))
                pe.wait_ge(sem["rq_sb"], at(b, "rq_sb", 1))
                for i in range(NT):
                    o = bank[i // 2][:, (i % 2) * 256:(i % 2) * 256 + 256]
                    T.matmul(o, ident_b[:], lmask[:, i, :], start=True, stop=False)
                    ins = T.matmul(o, work[0:LD, 5, i * P:(i + 1) * P], rk_bd[:].rearrange("p h l -> p (h l)"), start=False, stop=True)
                    if i % 2:
                        ins.then_inc(sem["lat_ps"], 1)
                yield "lat_scores"
                pe.wait_ge(sem["lat_exp"], at(b, "lat_exp", 2))
                pe.wait_ge(sem["v_sb"], at(b, "v_sb", 2))
                for half in range(2):
                    if half:
                        pe.wait_ge(sem["lat_probs"], at(b, "lat_probs", 2))
                    T.transpose(A2[:, 0:P], work[:, 2, 0:P], ident[:])
                    for c, dst in enumerate((A2, A3)):
                        i = 2 * half + c
                        for h in range(LH):
                            ins = T.transpose(dst[0:NLAT, h * P:(h + 1) * P],
                                              work[:, 2 + i // 2, (i % 2) * 256 + h * NLAT:(i % 2) * 256 + (h + 1) * NLAT], ident[:])
                        ins.then_inc(sem["lat_turned"], 1)
                    yield f"lat_turn{half}"
                for i in range(NT):
                    pe.wait_ge(sem["lat_probs"], at(b, "lat_probs", i + 1))
                    for h in range(LH):
                        ins = T.matmul(A4[:, i * LD + h * 16:i * LD + h * 16 + 16], work[0:NLAT, 8 + i, h * P:(h + 1) * P],
                                       rv_sb[:, h * 16:h * 16 + 16], start=True, stop=True)
                ins.then_inc(sem["lat_out"], 1)
                yield "lat_out"

                def stack_q(p):
                    g, j = p // PAIRS, p % PAIRS
                    if p:
                        pe.wait_ge(sem["stk_sb"], at(b, "stk_sb", p))
                    T.matmul(A4[:], sel_qk[:, j, 0, :], hiT[:, g, :], start=True, stop=False)
                    T.matmul(A4[:], sel_qk[:, j, 1, :], loT[:, g, :], start=False, stop=True).then_inc(sem["stack_q"], 1)

                def stack_k(p):
                    g, j = p // PAIRS, p % PAIRS
                    pe.wait_ge(sem["stq_sb"], at(b, "stq_sb", p + 1))
                    T.matmul(A4[:], sel_qk[:, j, 2, :], hiT[:, 2 + g, :], start=True, stop=False)
                    T.matmul(A4[:], sel_qk[:, j, 3, :], loT[:, 2 + g, :], start=False, stop=True).then_inc(sem["stack_k"], 1)

                def scores(n):
                    p, i = divmod(n, NT)
                    if i == 0:
                        pe.wait_ge(sem["stk_sb"], at(b, "stk_sb", p + 1))
                    o = bank[n % 2]
                    q = stq[:, p % 2, i * P:(i + 1) * P]
                    w, k0 = (P, 0) if i == 0 else (2 * P, (i - 1) * P)
                    mask = wmask[:, :, P:2 * P] if i == 0 else wmask[:]
                    T.matmul(o[:, 0:2 * w], ident_b[:], mask, start=True, stop=True)
                    for par in range(2):
                        ins = T.matmul(o[:, par * w:par * w + w], q, stk[:, p % 2, par, k0:k0 + w], start=False, stop=True,
                                       skip_group_check=True)
                    ins.then_inc(sem["scores"], 1)

                pe.wait_ge(sem["lat_normed"], at(b, "lat_normed", 1))
                T.transpose(A0[:, 0:P], work[:, 4, 0:P], ident[:])
                for i in range(NT):
                    ins = T.transpose(A0[0:LD, i * P:(i + 1) * P], work[:, 4, i * LD:(i + 1) * LD], ident[:])
                ins.then_inc(sem["lat_nt"], 1)
                stack_q(0)
                yield "lat_nt"
                pe.wait_ge(sem["lat_nt_sb"], at(b, "lat_nt_sb", 1))
                for i in range(NT):
                    ins = T.matmul((A2, A3)[i // 2][:, (i % 2) * D:(i % 2) * D + D], work[0:LD, 5, i * P:(i + 1) * P], wrout[:],
                                   start=True, stop=True)
                ins.then_inc(sem["remote_ps"], 1)
                stack_k(0)
                yield "remote"
                scores(0)
                scores(1)
                pe.wait_ge(sem["remote"], at(b, "remote", 1))
                yield "scores0"
                for n in range(N_LOC + 1):
                    p, i = divmod(n, NT)
                    if n < N_LOC:
                        pe.wait_ge(sem["probs"], at(b, "probs", n + 1))
                        if n:
                            pe.wait_ge(sem["p_sb"], at(b, "p_sb", n))
                        for c in range(2 if i == 0 else 4):
                            ins = T.transpose(A2[:, c * P:(c + 1) * P], probs[:, i, c * P:(c + 1) * P], ident[:])
                        ins.then_inc(sem["p_turned"], 1)
                    if n + 2 < N_LOC:
                        scores(n + 2)
                    if i == 0 and p + 1 < NPAIR:
                        stack_q(p + 1)
                    if i == 1 and p + 1 < NPAIR:
                        stack_k(p + 1)
                    if n:
                        m = n - 1
                        p, i = divmod(m, NT)
                        pe.wait_ge(sem["p_sb"], at(b, "p_sb", m + 1))
                        if i == 0 and p:
                            pe.wait_ge(sem["local_raw"], at(b, "local_raw", p))
                        blocks = [0] if i == 0 else [i - 1, i]
                        for h in range(2):
                            hh = 2 * p + h
                            for c, kb in enumerate(blocks):
                                ins = T.matmul(A3[:, 32 * i + 16 * h:32 * i + 16 * h + 16],
                                               pt[:, m % 2, (h * len(blocks) + c) * P:(h * len(blocks) + c + 1) * P],
                                               v_tok[:, kb, hh * HD:(hh + 1) * HD], start=c == 0, stop=c == len(blocks) - 1)
                        if i == NT - 1:
                            ins.then_inc(sem["local_ps"], 1)
                    yield f"local{n}"
                yield "gate"
                pe.wait_ge(sem["mixed"], at(b, "mixed", 1))
                for k, dst in enumerate((A0, A1)):
                    for i in range(NT):
                        c = (i % 2) * D + k * P
                        ins = T.transpose(dst[:, i * P:(i + 1) * P], work[:, 2 + i // 2, c:c + P], ident[:])
                    ins.then_inc(sem["mixed_t"], 1)
                yield "mix"
                pe.wait_ge(sem["mixed_sb"], at(b, "mixed_sb", 2))
                to_tokens((A2, A3), work[:, 8:10, :], wout[:]).then_inc(sem["out_ps"], 1)
                yield "out"
                yield "resid1"
                yield "norm2"
                turn(b, "normed", 1, "turned", (A0, A1), xn)
                yield "turn2"

                def up(f):
                    if f >= 3:
                        pe.wait_ge(sem["g_hi"], at(b, "g_hi", f - 2))
                    for k in range(NK):
                        for c, part in enumerate((hiT, loT)):
                            ins = T.matmul(bank[f % 3][:], w1t[:, k, f * P:(f + 1) * P], part[:, k, :],
                                           start=k == 0 and c == 0, stop=k == NK - 1 and c == 1)
                    ins.then_inc(sem["h_ps"], 1)

                def down(f):
                    pe.wait_ge(sem["g_lo"], at(b, "g_lo", f + 1))
                    for k, dst in enumerate((A3, A4)):
                        for c, part in enumerate((stq[:, f % 2, :], stk[:, 0, f % 2, :])):
                            ins = T.matmul(dst[:], w2t[:, f, k * P:(k + 1) * P], part, start=f == 0 and c == 0,
                                           stop=f == NF - 1 and c == 1)
                    ins.then_inc(sem["f_y"], 1)

                pe.wait_ge(sem["f_lo"], at(b, "f_lo", 1))
                for f in range(NF + 2):
                    if f < NF:
                        up(f)
                    if f >= 2:
                        down(f - 2)
                    yield f"ffn{f}"
                yield "ffn_y"
                pe.wait_ge(sem["fy_sb"], at(b, "fy_sb", 2))
                for i in range(NT):
                    for k in range(NK):
                        ins = T.transpose((A0, A1)[i // 2][:, (i % 2) * D + k * P:(i % 2) * D + (k + 1) * P],
                                          work[:, 2 + k, i * P:(i + 1) * P], ident[:])
                ins.then_inc(sem["fy_tok"], 1)
                yield "ffn_tok"
                yield "resid2"

            def rwkv_head(b):
                yield "rnorm"
                turn(b, "r_normed", 0, "r_turned", (R0, R1), r_xn)
                yield "rturn"

                def proj(w):
                    pe.wait_ge(sem["mix"], at(b, "mix", 2 * w + 2))
                    if w == 0:
                        pe.wait_ge(sem["r_xt"], at(b, "r_xt", 2))
                    if w == 1:
                        pe.wait_ge(sem["v_f"], at(b, "v_f", 1))
                    if w == 2:
                        pe.wait_ge(sem["v_f"], at(b, "v_f", 2))
                        pe.wait_ge(sem["k_f"], at(b, "k_f", 1))
                    if w == 3:
                        pe.wait_ge(sem["k_f"], at(b, "k_f", 2))
                        pe.wait_ge(sem["dec"], at(b, "dec", 1))
                    for g in range(2):
                        project(RB[(2 + 2 * w + g) % 3][:], wrk[:, w, :, g * P:(g + 1) * P], r_work[:, 2 + 2 * w:4 + 2 * w, :]
                                ).then_inc(sem["proj"], 1)

                for w in range(4):
                    yield f"rmix{w}"
                proj(0)
                yield "rproj0"
                proj(1)
                yield "rproj1"
                proj(2)
                yield "rproj2"
                proj(3)
                yield "rproj3"
                pe.wait_ge(sem["rb"], at(b, "rb", 1))
                for g, dst in enumerate((R1, R2)):
                    ins = T.matmul(dst[:], blockones[:], r_work[:, 10 + g, :], start=True, stop=True)
                ins.then_inc(sem["bonus_ps"], 1)
                yield "rbonus"

                def spread_v(n):
                    g, j = divmod(n, HD)
                    if n >= 2:
                        pe.wait_ge(sem["kv"], at(b, "kv", n - 1))
                    T.matmul(RB[n % 2][:], sel_v[:, j, :], v_hi[:, g, :], start=True, stop=False)
                    T.matmul(RB[n % 2][:], sel_v[:, j, :], v_lo[:, g, :], start=False, stop=True).then_inc(sem["v_bc"], 1)

                pe.wait_ge(sem["v_lo"], at(b, "v_lo", 1))
                spread_v(0)
                pe.wait_ge(sem["bonus"], at(b, "bonus", 1))
                spread_v(1)
                yield "rspread"
                for n in range(N_SCAN + 2):
                    if n >= 2:
                        g, j = divmod(n - 2, HD)
                        pe.wait_ge(sem["rs_lo"], at(b, "rs_lo", n - 1))
                        if j == 0 and g:
                            pe.wait_ge(sem["o_sb"], at(b, "o_sb", g))
                        T.matmul(R2[:], sel_o(j), p_hi[:, n % 2, :], start=j == 0, stop=False)
                        T.matmul(R2[:], sel_o(j), p_lo[:, n % 2, :], start=False, stop=j == HD - 1).then_inc(sem["summed"], 1)
                    if n + 2 < N_SCAN:
                        spread_v(n + 2)
                    yield f"scan{n}"

            def rwkv_tail(b):
                pe.wait_ge(sem["o_sb"], at(b, "o_sb", 2))
                for i in range(NT):
                    for g in range(2):
                        ins = T.transpose((R0, R1)[i // 2][:, (i % 2) * D + g * P:(i % 2) * D + (g + 1) * P],
                                          r_work[:, 10 + g, i * P:(i + 1) * P], ident[:])
                ins.then_inc(sem["o_tok"], 1)
                yield "o_tok"
                yield "o_var"
                for i in range(6):
                    yield f"wait{i}"
                yield "o_norm"
                pe.wait_ge(sem["o_norm"], at(b, "o_norm", 1))
                for g, dst in enumerate((R2, R0)):
                    for i in range(NT):
                        c = (i % 2) * D + g * P
                        ins = T.transpose(dst[:, i * P:(i + 1) * P], r_work[:, 2 + i // 2, c:c + P], ident[:])
                ins.then_inc(sem["o_back"], 1)
                yield "o_back"
                pe.wait_ge(sem["y_in"], at(b, "y_in", 1))
                to_tokens((R1, R2), r_work[:, 6:8, :], wrk[:, 4]).then_inc(sem["w_ps"], 1)
                yield "o_out"
                yield "rresid"

            batches_woven(pe, ORDER["tensor"], attention_ffn, rwkv_head, rwkv_tail)


PER2 = dict(
    x_in=16, x_out=16, var0=1, var1=1, rstd0=1, rstd1=1, normed=NT, turned=NK, x_f=NK, x_lo=NK, route_ps=1, route_z=1, route_e=1, comb=1, comb_ps=1,
    comb_hi=1, comb_lo=1, gate_ps=NE + 1, up_ps=NE + 1, c_ps=NE, silu=NE + 1, h_f=NE + 1, h_hi=NE + 1, h_lo=NE + 1,
    y_acc=NE + 1, y_sb=NK, y_turned=2, y_tok=2, x_final=1, own_hidden=NE, own_norm=2, own_route=11, own_end=3,
)
S_YT = (2, 3)
S_END = (4, 5)
S_STAT, S_NORM, S_TURN, S_ROUTE, S_TOP, S_COMB = 7, 8, (9, 10), 11, 15, 16
LEAD = 3


def expert_layer(nc, t, x3, out):
    with ExitStack() as ctx:
        def sb(name, shape, dt=F32):
            return ctx.enter_context(nc.sbuf_tensor(name, shape, dt))

        bank = [ctx.enter_context(nc.psum_tensor(f"mbank{i}", [P, 512], F32)) for i in range(8)]
        gate_bank, up_bank, c_bank, y_bank, side = bank[0:2], bank[2:4], bank[4], bank[5:7], bank[7]
        sem = {n: ctx.enter_context(nc.semaphore("m_" + n)) for n in PER2}
        loaded = ctx.enter_context(nc.semaphore("m_loaded"))
        w_loaded = [ctx.enter_context(nc.semaphore(f"m_w_loaded{i}")) for i in range(2)]
        w_split = ctx.enter_context(nc.semaphore("m_w_split"))
        w_hi_made = ctx.enter_context(nc.semaphore("m_w_hi_made"))
        const_ready = ctx.enter_context(nc.semaphore("m_const_ready"))

        NX = NE + 1
        W13, W2 = NK * 2 * INTER, D
        ident = sb("m_ident", [P, P])
        sel_e = sb("sel_e", [64, NE, P], F32R)
        gate_w = sb("gate_w", [P, NK, NE])
        gate_b = sb("gate_b", [P, NE])
        mhalf = sb("m_mhalf", [P, NT])
        euler = sb("euler", [P, NT * NE])
        w_hi = sb("w_hi", [P, NX, W13 + W2], F32R)
        w_lo = sb("w_lo", [P, NX, W13 + W2], F32R)
        w_raw = sb("w_raw", [P, 2, W13 + W2])
        sel_raw = sb("sel_raw", [64, NE * P])
        tick = sb("m_tick", [P, 1])[:]

        x_tok = [sb(f"m_x_tok{i}", [P, NT, D]) for i in range(2)]
        xh = [sb(f"m_xh{i}", [P, NK, S], F32R) for i in range(2)]
        xl = [sb(f"m_xl{i}", [P, NK, S], F32R) for i in range(2)]
        combT = [sb(f"combT{i}", [64, S], F32R) for i in range(2)]
        xn = sb("m_xn", [P, NT, D])
        xf = sb("m_xf", [P, NK, S])
        y_tok = sb("m_y_tok_sb", [P, NT, D])
        yn = sb("m_yn", [P, NT, D])
        st = sb("m_st", [P, 2, NT, 6])
        mv = sb("m_mv", [P, 2, NT, 2])
        vare = sb("m_vare", [P, 2, NT])
        rstd = sb("m_rstd", [P, 2, NT])
        rz = sb("rz", [P, NT * NE])
        re_ = sb("re_", [P, NT * NE])
        score = sb("score", [P, NT, NE])
        biased = sb("biased", [P, NT, NE + TOPK])
        rest = sb("rest", [P, NT, NE + TOPK])
        top = sb("top", [P, NT, 8])
        comb = sb("comb", [P, NT, NE])
        csum = sb("csum", [P, 2, NT])
        sg = sb("sg", [P, 3, S])
        hf = sb("hf", [P, 3, S])
        hh = sb("hh", [P, 3, S], F32R)
        hl = sb("hl", [P, 3, S], F32R)
        yT = sb("yT", [P, NK, S])

        def at(b, name, k):
            return b * PER2[name] + k

        def bc(ap, *shape):
            return ap.broadcast_to(shape)

        def batches(eng, body):
            body(0, 0, True, False)
            with eng.Fori(0, B // 2 - 1) as i:
                body(i * 2 + 1, 1, False, False)
                body(i * 2 + 2, 0, False, False)
            body(B - 1, 1, False, True)

        N_LOAD = 6
        rows = lambda ap: ap.rearrange("o (t p) d -> p (o t) d", p=P)
        block = ctx.enter_context(nc.Block())

        @block.sync
        def _(sp):
            sp.dma_start(ident[:], t["c_ident"]).then_inc(loaded, 16)
            sp.dma_start(gate_w[:], t["gate_w"].rearrange("(k p) n -> p k n", p=P)).then_inc(loaded, 16)
            sp.dma_start(gate_b[:], t["gate_b"].partition_broadcast(P)).then_inc(loaded, 16)
            sp.dma_start(mhalf[:], t["c_mhalf"][:, 0:NT]).then_inc(loaded, 16)
            sp.dma_start(euler[:], t["c_euler"]).then_inc(loaded, 16)
            sp.dma_start(sel_raw[:], t["c_sele"]).then_inc(loaded, 16)
            for i in range(2):
                sp.dma_start(x_tok[i][:], rows(x3[i:i + 1])).then_inc(sem["x_in"], 16)
            for e in range(NX):
                if e >= 2:
                    sp.wait_ge(w_split, e - 1)
                sp.dma_start(w_raw[:, e % 2, 0:W13], t["w13"][e].rearrange("(k p) n -> p k n", p=P)).then_inc(w_loaded[e % 2], 16)
                sp.dma_start(w_raw[:, e % 2, W13:], t["w2e"][e]).then_inc(w_loaded[e % 2], 16)

            def store(b, par):
                sp.wait_ge(sem["x_final"], at(b, "x_final", 1))
                sp.dma_start(rows(out[bass.ds(b, 1)]), x_tok[par][:]).then_inc(sem["x_out"], 16)

            def exchange(b, par):
                store(b, par)
                sp.wait_ge(sem["x_out"], at(b, "x_out", 16))
                sp.dma_start(x_tok[par][:], rows(x3[bass.ds(b + 2, 1)])).then_inc(sem["x_in"], 16)

            with sp.Fori(0, B // 2 - 1) as i:
                exchange(i * 2, 0)
                exchange(i * 2 + 1, 1)
            store(B - 2, 0)
            store(B - 1, 1)
            sp.wait_ge(sem["x_out"], B * 16)

        @block.vector
        def _(ve):
            V = nc.vector
            for i in range(2):
                V.memset(combT[i][:].bitcast(F32), 0.0)
            V.memset(biased[:, :, NE:], BIG)
            ve.wait_ge(loaded, 16 * N_LOAD)
            V.tensor_copy(sel_e[:].rearrange("p e m -> p (e m)"), sel_raw[:]).then_inc(const_ready, 1)

            own_hidden, own_norm, own_route, own_end = (Own(ve, sem[n], PER2[n]) for n in ("own_hidden", "own_norm", "own_route", "own_end"))

            def stats(own, b, side_, src):
                for i in range(NT):
                    ins = V.bn_stats(st[:, side_, i, :], src[:, i, :])
                own.link(ins, tick)
                for i in range(NT):
                    ins = V.bn_aggr(mv[:, side_, i, :], st[:, side_, i, :])
                own.link(ins)
                V.tensor_scalar(vare[:, side_], mv[:, side_, :, 1], EPS, None, ALU.add).then_inc(sem["var0" if side_ == 0 else "var1"], 1)

            def norm(b, par):
                ve.wait_ge(sem["rstd0"], at(b, "rstd0", 1))
                for i in range(NT):
                    V.tensor_scalar(xn[:, i, :], x_tok[par][:, i, :], mv[:, 0, i, 0:1], rstd[:, 0, i:i + 1], ALU.subtract, ALU.mult
                                    ).then_inc(sem["normed"], 1)

            def x_low(b, par, k):
                ve.wait_ge(sem["x_f"], at(b, "x_f", k + 1))
                V.tensor_tensor(xl[par][:, k, :], xf[:, k, :], xh[par][:, k, :].bitcast(F32), ALU.subtract).then_inc(sem["x_lo"], 1)

            def route(b):
                own = own_route
                own.start(b)
                ve.wait_ge(sem["route_e"], at(b, "route_e", 1))
                own.link(V.tensor_scalar(re_[:], re_[:], 1.0, None, ALU.add))
                own.link(V.reciprocal(score[:].rearrange("p a e -> p (a e)"), re_[:]))
                own.link(V.tensor_tensor(biased[:, :, 0:NE], score[:], bc(gate_b[:].unsqueeze(1), P, NT, NE), ALU.add), tick)
                for i in range(NT):
                    ins = V.max(top[:, i, :], biased[:, i, :])
                own.link(ins, tick)
                for i in range(NT):
                    ins = V.match_replace(rest[:, i, :], top[:, i, :], biased[:, i, :], -BIG)
                own.link(ins)
                own.link(V.tensor_tensor(comb[:], rest[:, :, 0:NE], biased[:, :, 0:NE], ALU.is_lt))
                own.link(V.tensor_tensor(comb[:], comb[:], score[:], ALU.mult))
                own.link(V.tensor_reduce(csum[:, 0, :], comb[:], X, ALU.add))
                own.link(V.reciprocal(csum[:, 1, :], csum[:, 0, :]))
                own.link(V.tensor_tensor(comb[:], comb[:], bc(csum[:, 1, :].unsqueeze(2), P, NT, NE), ALU.mult))
                own.link(V.tensor_scalar(comb[:], comb[:], ROUTE_SCALE, None, ALU.mult))
                V.memset(tick, 0.0).then_inc(sem["comb"], 1)
                own.end()

            def comb_low(b, par):
                ve.wait_ge(sem["comb_hi"], at(b, "comb_hi", 1))
                V.tensor_tensor(combT[par][32:32 + NE, :], side[0:NE, :], combT[par][0:NE, :].bitcast(F32), ALU.subtract
                                ).then_inc(sem["comb_lo"], 1)

            def start_stats(b, par):
                ve.wait_ge(sem["x_in"], 32 if isinstance(b, int) and b == 0 else at(b, "x_in", 16))
                own_norm.start(b)
                stats(own_norm, b, 0, x_tok[par])
                own_norm.end()

            def end_stats(b):
                ve.wait_ge(sem["y_tok"], at(b, "y_tok", 2))
                own_end.start(b)
                stats(own_end, b, 1, y_tok)

            def end_norm(b, par):
                ve.wait_ge(sem["rstd1"], at(b, "rstd1", 1))
                for i in range(NT):
                    ins = V.tensor_scalar(yn[:, i, :], y_tok[:, i, :], mv[:, 1, i, 0:1], rstd[:, 1, i:i + 1], ALU.subtract, ALU.mult)
                own_end.link(ins)
                V.tensor_tensor(x_tok[par][:], x_tok[par][:], yn[:], ALU.add).then_inc(sem["x_final"], 1)
                own_end.end()

            def hidden(b, e):
                ve.wait_ge(sem["silu"], at(b, "silu", e + 1))
                ve.wait_ge(sem["up_ps"], at(b, "up_ps", e + 1))
                sl = e % 3
                if e < NE:
                    own_hidden.link(V.tensor_tensor(sg[:, sl, :], sg[:, sl, :], up_bank[e % 2][:], ALU.mult))
                    ve.wait_ge(sem["c_ps"], at(b, "c_ps", e + 1))
                    V.tensor_tensor(hf[:, sl, :], sg[:, sl, :], c_bank[:], ALU.mult).then_inc(sem["h_f"], 1)
                else:
                    V.tensor_tensor(hf[:, sl, :], sg[:, sl, :], up_bank[e % 2][:], ALU.mult).then_inc(sem["h_f"], 1)

            def low(b, e):
                ve.wait_ge(sem["h_hi"], at(b, "h_hi", e + 1))
                V.tensor_tensor(hl[:, e % 3, :], hf[:, e % 3, :], hh[:, e % 3, :].bitcast(F32), ALU.subtract).then_inc(sem["h_lo"], 1)

            def weights_low(e):
                ve.wait_ge(w_hi_made, e + 1)
                V.tensor_tensor(w_lo[:, e, :], w_raw[:, e % 2, :], w_hi[:, e, :].bitcast(F32), ALU.subtract).then_inc(w_split, 1)

            start_stats(0, 0)
            norm(0, 0)
            for e in range(LEAD):
                weights_low(e)
            for k in range(NK):
                x_low(0, 0, k)
            route(0)

            def body(b, par, first, last):
                own_hidden.start(b)
                for e in range(NX):
                    if e == 0:
                        comb_low(b, par)
                    if e:
                        low(b, e - 1)
                    elif not first:
                        low(b - 1, NX - 1)
                    hidden(b, e)
                    if first and e + LEAD < NX:
                        weights_low(e + LEAD)
                    if not first:
                        if e == S_END[0]:
                            end_stats(b - 1)
                        if e == S_END[1]:
                            end_norm(b - 1, 1 - par)
                    if not last:
                        if e == S_STAT:
                            start_stats(b + 1, 1 - par)
                        if e == S_NORM:
                            norm(b + 1, 1 - par)
                        if e == S_TURN[0] + 1:
                            x_low(b + 1, 1 - par, 0)
                        if e == S_TURN[1] + 1:
                            x_low(b + 1, 1 - par, 1)
                        if e == S_TOP:
                            route(b + 1)
                own_hidden.end()

            batches(ve, body)
            low(B - 1, NX - 1)
            end_stats(B - 1)
            end_norm(B - 1, 1)

        @block.gpsimd
        def _(gp):
            G = nc.gpsimd
            gp.wait_ge(loaded, 16 * N_LOAD)

            def root(b, side_):
                n = f"{side_}"
                gp.wait_ge(sem["var" + n], at(b, "var" + n, 1))
                G.tensor_tensor(rstd[:, side_], vare[:, side_], mhalf[:], ALU.pow).then_inc(sem["rstd" + n], 1)

            def route_exp(b):
                gp.wait_ge(sem["route_z"], at(b, "route_z", 1))
                G.tensor_tensor(re_[:], euler[:], rz[:], ALU.pow).then_inc(sem["route_e"], 1)

            def body(b, par, first, last):
                if not first:
                    root(b - 1, 1)
                if not last:
                    root(b + 1, 0)
                    route_exp(b + 1)

            root(0, 0)
            route_exp(0)
            batches(gp, body)
            root(B - 1, 1)

        @block.scalar
        def _(sc):
            A = nc.scalar.activation
            def weights_high(e):
                sc.wait_ge(w_loaded[e % 2], 32 * (e // 2 + 1))
                A(w_hi[:, e, :], w_raw[:, e % 2, :], ACT.Copy).then_inc(w_hi_made, 1)

            for e in range(LEAD):
                weights_high(e)

            def x_parts(b, par, k):
                sc.wait_ge(sem["turned"], at(b, "turned", k + 1))
                A(xh[par][:, k, :], side[:], ACT.Copy)
                A(xf[:, k, :], side[:], ACT.Copy).then_inc(sem["x_f"], 1)

            def route_logits(b):
                sc.wait_ge(sem["route_ps"], at(b, "route_ps", 1))
                A(rz[:], side[:, 0:NT * NE], ACT.Copy, scale=-1.0).then_inc(sem["route_z"], 1)

            def comb_high(b, par):
                sc.wait_ge(sem["comb_ps"], at(b, "comb_ps", 1))
                A(combT[par][0:NE, :], side[0:NE, :], ACT.Copy).then_inc(sem["comb_hi"], 1)

            def silu(b, e):
                sc.wait_ge(sem["gate_ps"], at(b, "gate_ps", e + 1))
                A(sg[:, e % 3, :], gate_bank[e % 2][:], ACT.Silu).then_inc(sem["silu"], 1)

            def high(b, e):
                sc.wait_ge(sem["h_f"], at(b, "h_f", e + 1))
                A(hh[:, e % 3, :], hf[:, e % 3, :], ACT.Copy).then_inc(sem["h_hi"], 1)

            def y_out(b):
                sc.wait_ge(sem["y_acc"], at(b, "y_acc", NX))
                for k in range(NK):
                    A(yT[:, k, :], y_bank[k][:], ACT.Copy).then_inc(sem["y_sb"], 1)

            def y_tokens(b, half):
                sc.wait_ge(sem["y_turned"], at(b, "y_turned", half + 1))
                A(y_tok[:, 2 * half:2 * half + 2, :].rearrange("p a d -> p (a d)"), side[:], ACT.Copy).then_inc(sem["y_tok"], 1)

            for k in range(NK):
                x_parts(0, 0, k)
            route_logits(0)
            comb_high(0, 0)

            def body(b, par, first, last):
                for e in range(NX):
                    if first and e + LEAD < NX:
                        weights_high(e + LEAD)
                    silu(b, e)
                    if e:
                        high(b, e - 1)
                    elif not first:
                        high(b - 1, NX - 1)
                    if not first:
                        if e == 1:
                            y_out(b - 1)
                        if e in S_YT:
                            y_tokens(b - 1, S_YT.index(e))
                    if not last:
                        if e in S_TURN:
                            x_parts(b + 1, 1 - par, S_TURN.index(e))
                        if e == S_ROUTE:
                            route_logits(b + 1)
                        if e == S_COMB:
                            comb_high(b + 1, 1 - par)

            batches(sc, body)
            high(B - 1, NX - 1)
            y_out(B - 1)
            for half in range(2):
                y_tokens(B - 1, half)

        @block.tensor
        def _(pe):
            T = nc.tensor

            def turn_x(b, k):
                pe.wait_ge(sem["normed"], at(b, "normed", NT))
                if k:
                    pe.wait_ge(sem["x_f"], at(b, "x_f", k))
                for i in range(NT):
                    ins = T.transpose(side[:, i * P:(i + 1) * P], xn[:, i, k * P:(k + 1) * P], ident[:])
                ins.then_inc(sem["turned"], 1)

            def route(b):
                pe.wait_ge(sem["x_f"], at(b, "x_f", NK))
                for i in range(NT):
                    for k in range(NK):
                        ins = T.matmul(side[:, i * NE:(i + 1) * NE], xf[:, k, i * P:(i + 1) * P], gate_w[:, k, :],
                                       start=k == 0, stop=k == NK - 1)
                ins.then_inc(sem["route_ps"], 1)

            def turn_comb(b):
                pe.wait_ge(sem["comb"], at(b, "comb", 1))
                for i in range(NT):
                    ins = T.transpose(side[0:NE, i * P:(i + 1) * P], comb[:, i, :], ident[:])
                ins.then_inc(sem["comb_ps"], 1)

            def turn_y(b, half):
                if half:
                    pe.wait_ge(sem["y_tok"], at(b, "y_tok", half))
                else:
                    pe.wait_ge(sem["y_sb"], at(b, "y_sb", NK))
                for i in range(2):
                    for k in range(NK):
                        ins = T.transpose(side[:, i * D + k * P:i * D + (k + 1) * P], yT[:, k, (2 * half + i) * P:(2 * half + i + 1) * P], ident[:])
                ins.then_inc(sem["y_turned"], 1)

            def product(o, cols, e, hi, lo, first, last):
                terms = ((w_hi, hi), (w_hi, lo), (w_lo, hi))
                for c, (w, m) in enumerate(terms):
                    ins = T.matmul(o, w[:, e, cols:cols + P], m, start=first and c == 0, stop=last and c == 2)
                return ins

            def gate_up(b, par, e, first):
                if e >= 2:
                    pe.wait_ge(sem["silu"], at(b, "silu", e - 1))
                elif not first:
                    pe.wait_ge(sem["silu"], at(b, "silu", 0))
                for k in range(NK):
                    ins = product(gate_bank[e % 2][:], k * 2 * INTER, e, xh[par][:, k, :], xl[par][:, k, :], k == 0, k == NK - 1)
                ins.then_inc(sem["gate_ps"], 1)
                if e >= 2:
                    pe.wait_ge(sem["h_f"], at(b, "h_f", e - 1))
                elif not first:
                    pe.wait_ge(sem["h_f"], at(b, "h_f", 0))
                for k in range(NK):
                    ins = product(up_bank[e % 2][:], k * 2 * INTER + INTER, e, xh[par][:, k, :], xl[par][:, k, :], k == 0, k == NK - 1)
                ins.then_inc(sem["up_ps"], 1)

            def spread_c(b, par, e, first):
                if e == 0:
                    pe.wait_ge(sem["comb_lo"], at(b, "comb_lo", 1))
                else:
                    pe.wait_ge(sem["h_f"], at(b, "h_f", e))
                T.matmul(c_bank[:], sel_e[:, e, :], combT[par][:], start=True, stop=True).then_inc(sem["c_ps"], 1)

            def down(b, e, first):
                pe.wait_ge(sem["h_lo"], at(b, "h_lo", e + 1))
                if e == 0 and not first:
                    pe.wait_ge(sem["y_sb"], at(b, "y_sb", 0))
                for k in range(NK):
                    ins = product(y_bank[k][:], W13 + k * P, e, hh[:, e % 3, :], hl[:, e % 3, :], e == 0, e == NX - 1)
                ins.then_inc(sem["y_acc"], 1)

            pe.wait_ge(const_ready, 1)
            for k in range(NK):
                turn_x(0, k)
            route(0)
            turn_comb(0)
            pe.wait_ge(sem["x_lo"], NK)

            def body(b, par, first, last):
                if not first:
                    pe.wait_ge(sem["x_lo"], at(b, "x_lo", NK))
                for e in range(NX):
                    if first:
                        pe.wait_ge(w_split, e + 1)
                    gate_up(b, par, e, first)
                    if e >= 2:
                        down(b, e - 2, first)
                    elif not first:
                        down(b - 1, NX - 2 + e, False)
                    if e < NE:
                        spread_c(b, par, e, first)
                    if not first and e in S_YT:
                        turn_y(b - 1, S_YT.index(e))
                    if not last:
                        if e in S_TURN:
                            turn_x(b + 1, S_TURN.index(e))
                        if e == S_ROUTE:
                            route(b + 1)
                        if e == S_COMB:
                            turn_comb(b + 1)

            batches(pe, body)
            for e in (NX - 2, NX - 1):
                down(B - 1, e, False)
            for half in range(2):
                turn_y(B - 1, half)


def constants():
    import numpy as np

    f = np.float32
    p = np.arange(P)
    c = {"c_ident": np.eye(P, dtype=f), "c_ones": np.ones((P, P), f)}
    block = (p[:, None] // HD == p[None, :] // HD).astype(f)
    c["c_blockones"] = block
    c["c_selo"] = (np.arange(HD + P)[None, :] == HD + p[:, None] // HD * HD).astype(f)
    c["c_selv"] = np.stack([block * (p[:, None] % HD == j) for j in range(HD)], 1).reshape(P, HD * P).astype(f)
    sel = np.zeros((P, PAIRS, 4, P), f)
    quarters = ((0, 1), (2, 3), (0, 2), (1, 3))
    for j in range(PAIRS):
        for c4, qs in enumerate(quarters):
            for q in qs:
                r = np.arange(32)
                sel[32 * j + r, j, c4, 32 * q + r] = 1
    c["c_selqk"] = sel.reshape(P, -1)
    c["c_parmask"] = np.stack([(p % 32 // HD == par) for par in range(2)], 1).astype(f)
    c["c_lhmask"] = (np.arange(LD)[:, None] // 16 == np.arange(LH)[None, :]).astype(f)
    i, k = p[:, None], p[None, :]
    prev = (k >= i) & ~((i == 0) & (k == 0))
    own = k < i
    m = np.where(np.concatenate([prev, own], 1), 0, NEG).astype(f)
    c["c_wmask"] = np.stack([m, m], 1).reshape(P, 512)
    tok = np.arange(NT)[None, :, None] * P + p[:, None, None]
    lm = np.where(np.arange(NLAT)[None, None, :] < tok // CHUNK, 0, NEG).astype(f)
    c["c_lmask"] = np.repeat(lm[:, :, None, :], LH, 2).reshape(P, -1)
    c["c_rowloc"] = np.repeat(tok > 0, H, 2).astype(f)
    c["c_rowlat"] = np.repeat(tok >= CHUNK, LH, 2).astype(f)
    c["c_mhalf"] = np.full((P, 64), -0.5, f)
    c["c_euler"] = np.full((P, NT * NE), np.e, f)
    se = np.zeros((64, NE, P), f)
    for e in range(NE):
        se[e, e] = se[32 + e, e] = 1
    c["c_sele"] = se.reshape(64, -1)
    return c


def kernel(**inputs):
    import numpy as np
    import concourse.bacc as _bacc
    from concourse.bass_utils import run_bass_kernel_spmd as _run

    a = {k: np.asarray(v) for k, v in inputs.items()}
    col = lambda v: v.reshape(-1, P).T
    t = constants()
    t["x"] = a["L0_attn_x"]
    t["wqkv"] = a["L0_attn_qkv_w"]
    t["qkb"] = col(a["L0_attn_qkv_b"][:2 * D])
    t["vb"] = a["L0_attn_qkv_b"][2 * D:]
    t["wrq"] = a["L0_attn_rq_w"]
    t["rqb"] = a["L0_attn_rq_b"].reshape(LD, 1)
    t["wrkv"] = a["L0_attn_rkv_w"]
    t["rkb"] = a["L0_attn_rkv_b"][:LD].reshape(LD, 1)
    t["rvb"] = a["L0_attn_rkv_b"][LD:]
    t["wrout"], t["routb"] = a["L0_attn_rout_w"], a["L0_attn_rout_b"]
    t["wout"], t["outb"] = a["L0_attn_out_w"], a["L0_attn_out_b"]
    t["gl"], t["gr"] = a["L0_attn_gl_w"][:, 0], a["L0_attn_gr_w"][:, 0]
    t["w1"], t["w2"] = a["L0_ffn_W1"].T, a["L0_ffn_W2"].T
    t["b1"], t["b2"] = col(a["L0_ffn_b1"]), col(a["L0_ffn_b2"])
    t["wrk"] = np.stack([a["L1_attn_W_" + n].T for n in "vkwro"])
    t["tm"] = np.stack([col(a["L1_attn_tm_" + n]) for n in "vkwr"], 1)
    t["u"] = col(a["L1_attn_u"].reshape(-1))
    t["lnwb"] = np.stack([np.tile(a["L1_attn_ln_w"], 8), np.tile(a["L1_attn_ln_b"], 8)], 1)
    t["gate_w"], t["gate_b"] = a["L1_ffn_gate_w"].T, a["L1_ffn_gate_b"]
    t["w13"] = np.concatenate([a["L1_ffn_w13"], a["L1_ffn_w13_s"][None]]).transpose(0, 2, 1)
    t["w2e"] = np.concatenate([a["L1_ffn_w2"], a["L1_ffn_w2_s"][None]]).transpose(0, 2, 1)

    nc = _bacc.Bacc("TRN2", target_bir_lowering=False, num_devices=1)
    arrays, aps = {}, {}
    for name, v in t.items():
        v = np.ascontiguousarray(v)
        arrays[f"in_{name}"] = v
        aps[name] = nc.dram_tensor(f"in_{name}", v.shape, mybir.dt.from_np(v.dtype), kind="ExternalInput").ap()
    out = nc.dram_tensor("out_0", (B, S, D), F32, kind="ExternalOutput").ap()
    program(nc, aps, out)
    r = _run(nc, [arrays], core_ids=[0])
    return r.results[0]["out_0"]
```
